# Optimizing a Trainium2 kernel written in Bass

```python
import numpy as np
import jax
import jax.numpy as jnp

def _softmax(x, axis=-1):
    return jax.nn.softmax(x, axis=axis)

def _gelu(x):
    return jax.nn.gelu(x, approximate=True)

def _silu(x):
    return jax.nn.silu(x)

def _sigmoid(x):
    return jax.nn.sigmoid(x)

def _layernorm(x, axis=-1, eps=1e-05):
    m = jnp.mean(x, axis=axis, keepdims=True)
    v = jnp.var(x, axis=axis, keepdims=True)
    return (x - m) / jnp.sqrt(v + eps)

def _scatter_add(tgt, idx, src, axis=0):
    return tgt.at[idx].add(src)

def _segment_sum(src, seg, n):
    return jax.ops.segment_sum(src, seg, n)
kernel_name = 'mk_gps_d2_gnn_r16_a616ce'

def setup_inputs(seed: int=0):
    np.random.seed(seed)
    _w = jnp.asarray

    def _rec_inputs():
        import jax
        import jax.numpy as jnp
        _gk = jax.random.key(seed)
        x = -0.0002117 + 1 * jax.random.normal(jax.random.fold_in(_gk, 1), (6250, 256), jnp.float32)
        src = jax.random.randint(jax.random.fold_in(_gk, 2), (100000,), 0, 6250, jnp.int32)
        dst = jnp.minimum((6250 * jax.random.uniform(jax.random.fold_in(_gk, 3), (100000,)) ** 2.0).astype(jnp.int32), 99999)
        _o = jnp.argsort(dst, stable=True)
        src = src[_o]
        dst = dst[_o]
        edge_weight = jax.random.uniform(jax.random.fold_in(_gk, 12), (100000,), jnp.float32, 0.0, 1)
        return (x, src, dst, edge_weight)
    x, src, dst, edge_weight = _rec_inputs()

    def _L0_gnn_setup():
        import jax, jax.numpy as jnp
        import numpy as np
        N_NODES = 6250
        N_EDGES = 200000
        D_IN = 256
        D_OUT = 256
        key = jax.random.key(seed)
        k1, k2, k3, k4, k5, k6 = jax.random.split(key, 6)
        node_features = jax.random.normal(k1, (N_NODES, D_IN), dtype=jnp.float32)
        edge_src = jax.random.randint(k2, (N_EDGES,), 0, N_NODES, dtype=jnp.int64)
        edge_dst = jax.random.randint(k3, (N_EDGES,), 0, N_NODES, dtype=jnp.int64)
        edge_val = jax.random.uniform(k4, (N_EDGES,), dtype=jnp.float32)
        W = jax.random.normal(k5, (D_IN, D_OUT), dtype=jnp.float32) * (1.0 / np.sqrt(D_IN))
        b = jax.random.normal(k6, (D_OUT,), dtype=jnp.float32) * 0.01
        return {'node_features': node_features, 'edge_src': edge_src, 'edge_dst': edge_dst, 'edge_val': edge_val, 'W': W, 'b': b}
    _L0_gnn_all = _L0_gnn_setup()
    _L0_gnn_in = {k: v for k, v in _L0_gnn_all.items() if k in ('W', 'b')}
    del _L0_gnn_all

    def _L0_mix_setup():
        import jax, jax.numpy as jnp
        import numpy as np
        NUM_HEADS = 8
        key = jax.random.key(seed)
        ks = jax.random.split(key, 5)
        B, N, C = (8, 1024, 256)
        x = jax.random.normal(ks[0], (B, N, C), dtype=jnp.float32)
        Wq = jax.random.normal(ks[1], (C, C), dtype=jnp.float32) * 0.02
        Wkv = jax.random.normal(ks[2], (2 * C, C), dtype=jnp.float32) * 0.02
        Wproj = jax.random.normal(ks[3], (C, C), dtype=jnp.float32) * 0.02
        bproj = jnp.zeros((C,), dtype=jnp.float32)
        return {'x': x, 'Wq': Wq, 'Wkv': Wkv, 'Wproj': Wproj, 'bproj': bproj}
    _L0_mix_all = _L0_mix_setup()
    _L0_mix_in = {k: v for k, v in _L0_mix_all.items() if k in ('Wq', 'Wkv', 'Wproj', 'bproj')}
    del _L0_mix_all

    def _L0_ffn_setup():
        import jax, jax.numpy as jnp
        import numpy as np
        B, K, D = (512, 16, 256)
        E = 32
        H = int(D * 0.25)
        key = jax.random.key(seed)
        ks = jax.random.split(key, 7)
        d_rs = D ** (-0.5)
        h_rs = H ** (-0.5)
        x = jax.random.normal(ks[0], (B, K, D), dtype=jnp.float32)
        router_w = jax.random.uniform(ks[1], (E, D), jnp.float32, -d_rs, d_rs)
        router_b = jax.random.uniform(ks[2], (E,), jnp.float32, -d_rs, d_rs)
        W1 = jax.random.uniform(ks[3], (E, D, H), jnp.float32, -h_rs, h_rs)
        b1 = jax.random.uniform(ks[4], (E, H), jnp.float32, -h_rs, h_rs)
        W2 = jax.random.uniform(ks[5], (E, H, D), jnp.float32, -d_rs, d_rs)
        b2 = jax.random.uniform(ks[6], (E, D), jnp.float32, -d_rs, d_rs)
        return {'x': x, 'router_w': router_w, 'router_b': router_b, 'W1': W1, 'b1': b1, 'W2': W2, 'b2': b2}
    _L0_ffn_all = _L0_ffn_setup()
    _L0_ffn_in = {k: v for k, v in _L0_ffn_all.items() if k in ('router_w', 'router_b', 'W1', 'b1', 'W2', 'b2')}
    del _L0_ffn_all

    def _L1_gnn_setup():
        import jax, jax.numpy as jnp
        import numpy as np
        N_NODES = 6250
        N_EDGES = 100000
        IN_FEATS = 256
        OUT_FEATS = 64
        NHEAD = 4
        ALPHA = 0.2
        key = jax.random.key(seed)
        k1, k2, k3, k4, k5, k6 = jax.random.split(key, 6)
        stdv_w = np.sqrt(6.0 / (IN_FEATS + OUT_FEATS * NHEAD))
        stdv_a = np.sqrt(6.0 / (NHEAD + OUT_FEATS))
        return {'x': jax.random.normal(k1, (N_NODES, IN_FEATS), dtype=jnp.float32), 'W': jax.random.uniform(k2, (IN_FEATS, OUT_FEATS * NHEAD), minval=-stdv_w, maxval=stdv_w, dtype=jnp.float32), 'a_l': jax.random.uniform(k3, (1, NHEAD, OUT_FEATS), minval=-stdv_a, maxval=stdv_a, dtype=jnp.float32), 'a_r': jax.random.uniform(k4, (1, NHEAD, OUT_FEATS), minval=-stdv_a, maxval=stdv_a, dtype=jnp.float32), 'row': jax.random.randint(k5, (N_EDGES,), 0, N_NODES, dtype=jnp.int32), 'col': jax.random.randint(k6, (N_EDGES,), 0, N_NODES, dtype=jnp.int32)}
    _L1_gnn_all = _L1_gnn_setup()
    _L1_gnn_in = {k: v for k, v in _L1_gnn_all.items() if k in ('W', 'a_l', 'a_r')}
    del _L1_gnn_all

    def _L1_mix_setup():
        import jax, jax.numpy as jnp
        import numpy as np
        EPS = 1e-05

        def _layernorm(x, weight, bias):
            mean = jnp.mean(x, axis=-1, keepdims=True)
            std = jnp.std(x, axis=-1, keepdims=True, ddof=1)
            out = (x - mean) / (std + EPS)
            return weight * out + bias
        key = jax.random.key(seed)
        B, N, C = (4, 2048, 256)
        H, hc = (8, C // 8)
        kx, = jax.random.split(key, 1)
        x = jax.random.normal(kx, (B, N, C), dtype=jnp.float32)
        return {'x': x, 'kln_weight': jnp.ones((H, 1, hc), dtype=jnp.float32), 'kln_bias': jnp.zeros((H, 1, hc), dtype=jnp.float32), 'vln_weight': jnp.ones((H, 1, hc), dtype=jnp.float32), 'vln_bias': jnp.zeros((H, 1, hc), dtype=jnp.float32)}
    _L1_mix_all = _L1_mix_setup()
    _L1_mix_in = {k: v for k, v in _L1_mix_all.items() if k in ('kln_weight', 'kln_bias', 'vln_weight', 'vln_bias')}
    del _L1_mix_all

    def _L1_ffn_setup():
        import jax, jax.numpy as jnp
        import numpy as np
        B, S, H, F, E, K = (8, 256, 256, 512, 16, 2)
        EPS = 1e-05
        key = jax.random.key(seed)
        ks = jax.random.split(key, 9)
        sc = 0.02
        return {'x': jax.random.normal(ks[0], (B, S, H), dtype=jnp.float32), 'gate_w': jax.random.normal(ks[1], (H, E), dtype=jnp.float32) * sc, 'gate_b': jnp.zeros((E,), dtype=jnp.float32), 'w1': jax.random.normal(ks[2], (E, H, F), dtype=jnp.float32) * sc, 'b1': jnp.zeros((E, F), dtype=jnp.float32), 'w2': jax.random.normal(ks[3], (E, F, H), dtype=jnp.float32) * sc, 'b2': jnp.zeros((E, H), dtype=jnp.float32), 'gamma': jnp.ones((H,), dtype=jnp.float32), 'beta': jnp.zeros((H,), dtype=jnp.float32)}
    _L1_ffn_all = _L1_ffn_setup()
    _L1_ffn_in = {k: v for k, v in _L1_ffn_all.items() if k in ('gate_w', 'gate_b', 'w1', 'b1', 'w2', 'b2', 'gamma', 'beta')}
    del _L1_ffn_all
    return {'x': x, 'src': src, 'dst': dst, 'edge_weight': edge_weight, 'L0_gnn_W': _L0_gnn_in['W'], 'L0_gnn_b': _L0_gnn_in['b'], 'L0_mix_Wq': _L0_mix_in['Wq'], 'L0_mix_Wkv': _L0_mix_in['Wkv'], 'L0_mix_Wproj': _L0_mix_in['Wproj'], 'L0_mix_bproj': _L0_mix_in['bproj'], 'L0_ffn_router_w': _L0_ffn_in['router_w'], 'L0_ffn_router_b': _L0_ffn_in['router_b'], 'L0_ffn_W1': _L0_ffn_in['W1'], 'L0_ffn_b1': _L0_ffn_in['b1'], 'L0_ffn_W2': _L0_ffn_in['W2'], 'L0_ffn_b2': _L0_ffn_in['b2'], 'L1_gnn_W': _L1_gnn_in['W'], 'L1_gnn_a_l': _L1_gnn_in['a_l'], 'L1_gnn_a_r': _L1_gnn_in['a_r'], 'L1_mix_kln_weight': _L1_mix_in['kln_weight'], 'L1_mix_kln_bias': _L1_mix_in['kln_bias'], 'L1_mix_vln_weight': _L1_mix_in['vln_weight'], 'L1_mix_vln_bias': _L1_mix_in['vln_bias'], 'L1_ffn_gate_w': _L1_ffn_in['gate_w'], 'L1_ffn_gate_b': _L1_ffn_in['gate_b'], 'L1_ffn_w1': _L1_ffn_in['w1'], 'L1_ffn_b1': _L1_ffn_in['b1'], 'L1_ffn_w2': _L1_ffn_in['w2'], 'L1_ffn_b2': _L1_ffn_in['b2'], 'L1_ffn_gamma': _L1_ffn_in['gamma'], 'L1_ffn_beta': _L1_ffn_in['beta']}

def reference(x, src, dst, edge_weight, L0_gnn_W, L0_gnn_b, L0_mix_Wq, L0_mix_Wkv, L0_mix_Wproj, L0_mix_bproj, L0_ffn_router_w, L0_ffn_router_b, L0_ffn_W1, L0_ffn_b1, L0_ffn_W2, L0_ffn_b2, L1_gnn_W, L1_gnn_a_l, L1_gnn_a_r, L1_mix_kln_weight, L1_mix_kln_bias, L1_mix_vln_weight, L1_mix_vln_bias, L1_ffn_gate_w, L1_ffn_gate_b, L1_ffn_w1, L1_ffn_b1, L1_ffn_w2, L1_ffn_b2, L1_ffn_gamma, L1_ffn_beta):
    import jax
    import jax.numpy as jnp

    def _L0_gnn_ref(node_features, edge_src, edge_dst, edge_val, W, b):
        import jax, jax.numpy as jnp
        import numpy as np
        N_NODES = 6250
        N_EDGES = 200000
        D_IN = 256
        D_OUT = 256
        msgs = edge_val[:, None] * node_features[edge_src]
        agg = jax.ops.segment_sum(msgs, edge_dst, num_segments=N_NODES)
        return jax.nn.relu(agg @ W + b)

    def _L0_mix_ref(x, Wq, Wkv, Wproj, bproj):
        import jax, jax.numpy as jnp
        import numpy as np
        NUM_HEADS = 8
        B, N, C = x.shape
        h = NUM_HEADS
        d = C // h
        q = jnp.einsum('bnc,oc->bno', x, Wq).reshape(B, N, h, d).transpose(0, 2, 1, 3)
        kv = jnp.einsum('bnc,oc->bno', x, Wkv).reshape(B, N, 2, h, d)
        k = kv[:, :, 0].transpose(0, 2, 1, 3)
        v = kv[:, :, 1].transpose(0, 2, 1, 3)
        q = jax.nn.elu(q) + 1.0
        k = jax.nn.elu(k) + 1.0
        k_sum = k.sum(axis=2)
        D_inv = 1.0 / jnp.maximum(jnp.einsum('bhnd,bhd->bhn', q, k_sum), 1e-06)
        context = jnp.einsum('bhnd,bhne->bhde', k, v)
        attn = jnp.einsum('bhnd,bhde->bhne', q, context) * D_inv[..., None]
        out = attn.transpose(0, 2, 1, 3).reshape(B, N, C)
        out = jnp.einsum('bnc,oc->bno', out, Wproj) + bproj
        return out

    def _L0_ffn_ref(x, router_w, router_b, W1, b1, W2, b2):
        import jax, jax.numpy as jnp
        import numpy as np
        B, K, D = (512, 16, 256)
        E = 32
        H = int(D * 0.25)
        xf = x.reshape(-1, D)
        logits = xf @ router_w.T + router_b
        idx = jnp.argmax(logits, axis=-1)
        w1t = jnp.take(W1, idx, axis=0)
        h = jnp.einsum('nd,ndh->nh', xf, w1t) + jnp.take(b1, idx, axis=0)
        h = jax.nn.relu(h)
        w2t = jnp.take(W2, idx, axis=0)
        out = jnp.einsum('nh,nhd->nd', h, w2t) + jnp.take(b2, idx, axis=0)
        out = jax.nn.relu(out)
        return out.reshape(x.shape)

    def _L1_gnn_ref(x, W, a_l, a_r, row, col):
        import jax, jax.numpy as jnp
        import numpy as np
        N_NODES = 6250
        N_EDGES = 100000
        IN_FEATS = 256
        OUT_FEATS = 64
        NHEAD = 4
        ALPHA = 0.2
        n = x.shape[0]
        h = (x @ W).reshape(n, NHEAD, OUT_FEATS)
        h = jnp.where(jnp.isnan(h), 0.0, h)
        h_l = (a_l * h).sum(-1)
        h_r = (a_r * h).sum(-1)
        e = h_l[row] + h_r[col]
        e = jnp.where(e > 0, e, ALPHA * e)
        m = jax.ops.segment_max(e, row, num_segments=n)
        m = jnp.where(jnp.isfinite(m), m, 0.0)
        ex = jnp.exp(e - m[row])
        denom = jax.ops.segment_sum(ex, row, num_segments=n)
        att = ex / (denom[row] + 1e-16)
        msg = att[:, :, None] * h[col]
        out = jax.ops.segment_sum(msg, row, num_segments=n)
        return out.reshape(n, NHEAD * OUT_FEATS)

    def _L1_mix_ref(x, kln_weight, kln_bias, vln_weight, vln_bias):
        import jax, jax.numpy as jnp
        import numpy as np
        EPS = 1e-05

        def _layernorm(x, weight, bias):
            mean = jnp.mean(x, axis=-1, keepdims=True)
            std = jnp.std(x, axis=-1, keepdims=True, ddof=1)
            out = (x - mean) / (std + EPS)
            return weight * out + bias
        B, N, C = x.shape
        H = kln_weight.shape[0]
        hc = C // H
        qkv = x.reshape(B, N, H, hc).transpose(0, 2, 1, 3)
        q = qkv
        k = _layernorm(qkv, kln_weight, kln_bias)
        v = _layernorm(qkv, vln_weight, vln_bias)
        kv = jnp.einsum('bhnd,bhne->bhde', k, v) / N
        out = jnp.einsum('bhnd,bhde->bhne', q, kv)
        out = out.transpose(0, 2, 1, 3).reshape(B, N, C)
        return out + x

    def _L1_ffn_ref(x, gate_w, gate_b, w1, b1, w2, b2, gamma, beta):
        import jax, jax.numpy as jnp
        import numpy as np
        B, S, H, F, E, K = (8, 256, 256, 512, 16, 2)
        EPS = 1e-05
        gate_logits = x @ gate_w + gate_b
        topk_vals, topk_idx = jax.lax.top_k(gate_logits, K)
        topk_w = jax.nn.softmax(topk_vals, axis=-1)
        h = jax.nn.relu(jnp.einsum('bsh,ehf->bsef', x, w1) + b1)
        expert_out = jnp.einsum('bsef,efh->bseh', h, w2) + b2
        sel = jnp.take_along_axis(expert_out, topk_idx[:, :, :, None], axis=2)
        moe = jnp.sum(topk_w[..., None] * sel, axis=2)
        y = x + moe
        mu = jnp.mean(y, axis=-1, keepdims=True)
        var = jnp.var(y, axis=-1, keepdims=True)
        return (y - mu) / jnp.sqrt(var + EPS) * gamma + beta
    xn = _layernorm(x, axis=-1)
    x = x + _L0_gnn_ref(xn, src, dst, edge_weight, L0_gnn_W, L0_gnn_b) + _L0_mix_ref(xn[None], L0_mix_Wq, L0_mix_Wkv, L0_mix_Wproj, L0_mix_bproj)[0]
    x = x + _L0_ffn_ref(_layernorm(x, axis=-1)[None], L0_ffn_router_w, L0_ffn_router_b, L0_ffn_W1, L0_ffn_b1, L0_ffn_W2, L0_ffn_b2)[0]
    xn = _layernorm(x, axis=-1)
    x = x + _L1_gnn_ref(xn, L1_gnn_W, L1_gnn_a_l, L1_gnn_a_r, src, dst) + _L1_mix_ref(xn[None], L1_mix_kln_weight, L1_mix_kln_bias, L1_mix_vln_weight, L1_mix_vln_bias)[0]
    x = x + _L1_ffn_ref(_layernorm(x, axis=-1)[None], L1_ffn_gate_w, L1_ffn_gate_b, L1_ffn_w1, L1_ffn_b1, L1_ffn_w2, L1_ffn_b2, L1_ffn_gamma, L1_ffn_beta)[0]
    return x

_drawn_inputs = setup_inputs


def setup_inputs(seed=0):
    import zlib

    import numpy as np

    out = dict(_drawn_inputs(seed))
    spreads = {'L0_mix_bproj': (0.0, 0.1),
     'L1_mix_kln_weight': (1.0, 0.2),
     'L1_mix_kln_bias': (0.0, 0.454),
     'L1_mix_vln_weight': (1.0, 0.2),
     'L1_mix_vln_bias': (0.0, 0.454),
     'L1_ffn_gate_b': (0.0, 0.633),
     'L1_ffn_b1': (0.0, 0.8),
     'L1_ffn_b2': (0.0, 0.532),
     'L1_ffn_gamma': (1.0, 0.2),
     'L1_ffn_beta': (0.0, 0.406)}
    factors = {'L0_gnn_b': 5.811,
     'L0_mix_Wq': 8.0,
     'L0_mix_Wkv': 8.0,
     'L0_mix_Wproj': 8.0,
     'L0_ffn_b1': 8.0,
     'L0_ffn_b2': 3.602,
     'L1_ffn_gate_w': 2.853,
     'L1_ffn_w1': 4.413,
     'L1_ffn_w2': 3.516}
    for name, (base, spread) in spreads.items():
        noise = np.random.default_rng([zlib.crc32(name.encode()), seed]).standard_normal(out[name].shape)
        drawn = base * np.exp(spread * noise) if base else spread * noise
        out[name] = jnp.asarray(drawn.astype(out[name].dtype))
    for name, factor in factors.items():
        out[name] = (out[name] * factor).astype(out[name].dtype)
    return out
```

```python
from contextlib import ExitStack, contextmanager

import concourse.bass as bass
from concourse import mybir

F32 = mybir.dt.float32
I32 = mybir.dt.int32
U32 = mybir.dt.uint32
BF16 = mybir.dt.bfloat16
ALU = mybir.AluOpType
ACT = mybir.ActivationFunctionType
AX_X = mybir.AxisListType.X
RMAX = bass.bass_isa.ReduceOp.max
ds = bass.ds

P = 128
NODES, D, EDGES = 6250, 256, 100000
T = -(-NODES // P)
NP = T * P
TAIL = NODES - (T - 1) * P
B = 7
LOOPS = T // B
assert LOOPS * B == T
KD = D // P
C = -(-EDGES // P)
EP = C * P
BUCKETS = T + 1
SCAT = 17
SCAT_LOOPS = C // (2 * SCAT)
assert SCAT_LOOPS * 2 * SCAT == C
U = 8
HALF_U = U // 2
GROUP_LOOPS = -(-(C + T - 1) // (2 * U))
VT = -(-(GROUP_LOOPS * 2 * U) // P)
NV = VT * P
HC = 32
GH, GF = 4, 64
ROW1 = D + 2 * GH
ACC_W = D + GH
E0, H0 = 32, 64
HB = E0 * H0 // P
HALF = B * P // 2
E1, F1, K1 = 16, 512, 2
FB = F1 // P
SLOT_TILES = K1 * T + E1
SLOTS = SLOT_TILES * P
LN_EPS, KV_EPS, D_MIN = 1e-5, 1e-5, 1e-6
ALPHA = 0.2
LIFT = 60.0
DEN_MIN = 1e-30
PARTS = 3


class Steps:

    def __init__(self, engine, sem):
        self.engine, self.sem, self.n, self.i, self.per = engine, sem, 0, None, 0

    def add(self, ins):
        ins.then_inc(self.sem, 1)
        self.n += 1

    def settle(self):
        self.engine.wait_ge(self.sem, self.n if self.i is None else self.n + self.i * self.per)

    def then(self, ins):
        self.add(ins)
        self.settle()

    @contextmanager
    def loop(self, count, per):
        first = self.n
        with self.engine.Fori(0, count) as i:
            self.i, self.per = i, per
            yield i
            assert self.n - first == per, (self.n - first, per)
        self.i, self.n = None, first + per * count


def gps_two_layers(nc, x, src, dst, edge_weight, L0_gnn_W, L0_gnn_b, L0_mix_Wq, L0_mix_Wkv, L0_mix_Wproj,
                   L0_mix_bproj, L0_ffn_router_w, L0_ffn_router_b, L0_ffn_W1, L0_ffn_b1, L0_ffn_W2, L0_ffn_b2,
                   L1_gnn_W, L1_gnn_a_l, L1_gnn_a_r, L1_mix_kln_weight, L1_mix_kln_bias, L1_mix_vln_weight,
                   L1_mix_vln_bias, L1_ffn_gate_w, L1_ffn_gate_b, L1_ffn_w1, L1_ffn_b1, L1_ffn_w2, L1_ffn_b2,
                   L1_ffn_gamma, L1_ffn_beta, out):
    with ExitStack() as ctx:
        def sem(name):
            return ctx.enter_context(nc.semaphore(name))

        def dram(name, shape, dt=F32):
            return nc.dram_tensor(name, shape, dt, kind="Internal").ap()

        h0_table = dram("h0_table", (NP, D))
        h1_table = dram("h1_table", (NP, ROW1))
        edges_by = [dram("edges_by_dst", (EP, 4)), dram("edges_by_src", (EP, 4))]
        visit_tiles = dram("visit_tiles", (2, NV), I32)
        slot_rows = dram("slot_rows", (SLOTS + K1 * P, D))
        slot_out = dram("slot_out", (SLOTS, D))

        arena_words = 53200
        arena = ctx.enter_context(nc.sbuf_tensor("arena", [P, arena_words], F32))
        place = {"at": 0}

        def take(words):
            at = place["at"]
            place["at"] = at + words
            assert place["at"] <= place.get("end", arena_words), place
            return arena[:, at:at + words]

        def scratch(at, end=arena_words):
            place["at"], place["end"] = at, end

        xres = take(T * D)
        ident, tri, ones, iota = take(P), take(P), take(P), take(P)
        zeros = take(P)
        blk = take(P)
        lane, rowmask = take(1), take(1)
        stats, mean, rstd, lnt = take(6 * T), take(T), take(T), take(4 * T)
        tot, base_all = take(BUCKETS), take(GROUP_LOOPS)
        base = base_all[:, 0:BUCKETS]
        unsorted_f, unsorted = take(2), take(1).bitcast(I32)
        cnt = [take(2 * BUCKETS), take(2 * BUCKETS)]
        GRAPH = place["at"]
        rl_all = take(BUCKETS * 2 * GH)
        v_loc, v_w = take(NV), take(NV)
        v_idx = take(NV).bitcast(I32)
        tile_row = take(NV).bitcast(I32)
        XNT = place["at"]
        xnT = take(KD * NP)
        ACC = place["at"]
        acc = take(BUCKETS * ACC_W)
        src_f, dst_f, pos_src = take(C), take(C), take(C)
        w_f, pos_dst = take(C), take(C)
        FREE = place["at"]
        xnT3 = xnT.rearrange("p (k n) -> p k n", k=KD)
        acc3 = acc.rearrange("p (t w) -> p t w", w=ACC_W)

        ps = ctx.enter_context(nc.psum_tensor("ps", [P, 8 * 512], F32))

        def bank(b, width=512, at=0):
            return ps[:, b * 512 + at:b * 512 + at + width]

        def half(b, i, width=D):
            return ps[:, b * 512 + i * 256:b * 512 + i * 256 + width]

        V, G = Steps(nc.vector, sem("dve_step")), Steps(nc.gpsimd, sem("pool_step"))
        V_SORT, G_SORT = Steps(nc.vector, sem("dve_sort_step")), Steps(nc.gpsimd, sem("pool_sort_step"))

        var_ready, std_ready = sem("var_ready"), sem("std_ready")
        calls = {"ln_dve": 0, "ln_act": 0}

        def ln_stats(dve, rows=xres):
            with V.loop(T, 1) as t:
                V.add(dve.bn_stats(stats[:, ds(t * 6, 6)], rows[:, ds(t * D, D)]))
            V.settle()
            s = stats.rearrange("p (t s) -> p t s", s=6)
            a, b, c, d = (lnt[:, i * T:(i + 1) * T] for i in range(4))
            V.add(dve.tensor_tensor(a, s[:, :, 1], s[:, :, 4], ALU.add))
            V.add(dve.tensor_tensor(b, s[:, :, 1], s[:, :, 4], ALU.subtract))
            V.then(dve.tensor_tensor(c, s[:, :, 2], s[:, :, 5], ALU.add))
            V.add(dve.tensor_scalar(mean, a, 0.5, None, ALU.mult))
            V.then(dve.tensor_tensor(d, b, b, ALU.mult))
            V.then(dve.scalar_tensor_tensor(b, d, D / 4, c, ALU.mult, ALU.add))
            dve.tensor_scalar(a, b, 1.0 / D, LN_EPS, ALU.mult, ALU.add).then_inc(var_ready, 1)
            calls["ln_dve"] += 1
            dve.wait_ge(std_ready, calls["ln_dve"])
            V.then(dve.reciprocal(c, b))
            V.then(dve.tensor_tensor(d, c, c, ALU.mult))
            V.then(dve.tensor_tensor(b, d, a, ALU.mult))
            V.then(dve.tensor_scalar(d, b, -0.5, 1.5, ALU.mult, ALU.add))
            V.then(dve.tensor_tensor(rstd, d, c, ALU.mult))

        def ln_root(act):
            calls["ln_act"] += 1
            act.wait_ge(var_ready, calls["ln_act"])
            act.activation(lnt[:, T:2 * T], lnt[:, 0:T], ACT.Sqrt).then_inc(std_ready, 1)

        def normalise(dve, to, t, rows=xres):
            return dve.tensor_scalar(to, rows[:, ds(t * D, D)], mean[:, ds(t, 1)], rstd[:, ds(t, 1)],
                                     ALU.subtract, ALU.mult)

        tot_ready, base_ps = sem("tot_ready"), sem("base_ps")

        def rank_keys(dve, keys, temps):
            key_t, eq, _, part = temps
            V.then(dve.tensor_copy(part.bitcast(I32), keys))
            V.then(dve.tensor_scalar(eq.bitcast(I32), part.bitcast(I32), 7, None, ALU.arith_shift_right))
            V.then(dve.tensor_copy(key_t, eq.bitcast(I32)))

        def rank_counts(dve, call, pos, temps):
            key_t, eq, _, _ = temps
            with V.loop(BUCKETS, 2) as b:
                V.then(dve.tensor_scalar(eq, key_t, iota[:, ds(b, 1)], None, ALU.is_equal))
                V.then(dve.tensor_reduce(tot[:, ds(b, 1)], eq, AX_X, ALU.add))
            dve.memset(pos, 0.0).then_inc(tot_ready, 1)
            dve.wait_ge(base_ps, call + 1)
            count, cum = cnt[call][:, 0:BUCKETS], cnt[call][:, BUCKETS:]
            V.then(dve.tensor_copy(count, bank(7, BUCKETS, 64)))
            V.then(dve.tensor_tensor_scan(cum, count, count, 0.0, ALU.add, ALU.bypass))
            V.then(dve.tensor_tensor(base, cum, count, ALU.subtract))
            V.then(dve.scalar_tensor_tensor(base, base, -1.0, bank(7, BUCKETS), ALU.add, ALU.add))

        def rank_tile(dve, steps, b, pos, temps):
            key_t, eq, scan, part = temps
            steps.then(dve.tensor_scalar(eq, key_t, iota[:, ds(b, 1)], None, ALU.is_equal))
            steps.then(dve.tensor_tensor_scan(scan, eq, eq, 0.0, ALU.add, ALU.bypass))
            steps.then(dve.scalar_tensor_tensor(part, scan, base_all[:, ds(b, 1)], eq, ALU.add, ALU.mult))
            steps.then(dve.tensor_tensor(pos, pos, part, ALU.add))

        def rank_sums(pe, call):
            pe.wait_ge(tot_ready, call + 1)
            pe.matmul(bank(7, BUCKETS), tri, tot, start=True, stop=True)
            pe.matmul(bank(7, BUCKETS, 64), ones, tot, start=True, stop=True).then_inc(base_ps, 1)

        scat_done = [[sem(f"scat{c}_done{b}") for b in range(2)] for c in range(2)]
        dma_turn = sem("dma_turn")

        def scatter(pool, G, call, pos, fields, ring):
            offs = ring[:, 0:2 * SCAT].bitcast(I32).rearrange("p (b s) -> p b s", b=2)
            load = ring[:, 2 * SCAT:10 * SCAT].rearrange("p (b s f) -> p b s f", b=2, s=SCAT)
            G.then(pool.memset(ring[:, 2 * SCAT:10 * SCAT], 0.0))

            def fill(b, first):
                G.add(pool.tensor_copy(offs[:, b, :], pos[:, ds(first, SCAT)]))
                for f, field in enumerate(fields):
                    G.add(pool.tensor_copy(load[:, b, :, f], field[:, ds(first, SCAT)]))
                G.settle()

            def send(b):
                pool.sem_inc(dma_turn, 1)
                for s in range(SCAT):
                    pool.indirect_dma_start(edges_by[call], bass.IndirectOffsetOnAxis(ap=offs[:, b, s:s + 1], axis=0),
                                            load[:, b, s, :], None).then_inc(scat_done[call][b], 16)

            per = 1 + len(fields)
            for b in range(2):
                fill(b, b * SCAT)
                send(b)
            with G.loop(SCAT_LOOPS - 1, 2 * per) as j:
                for b in range(2):
                    pool.wait_ge(scat_done[call][b], (j + 1) * (16 * SCAT))
                    fill(b, (j + 1) * (2 * SCAT) + b * SCAT)
                    send(b)
            for b in range(2):
                pool.wait_ge(scat_done[call][b], SCAT_LOOPS * 16 * SCAT)

        vis_done, vis_rows, vis_cols, vis_ps, vis_tile, vis_out, vis_back = (sem(n) for n in (
            "vis_done", "vis_rows", "vis_cols", "vis_ps", "vis_tile", "vis_out", "vis_back"))

        def visit_views():
            v = {n: take(w) for n, w in (("grid", VT * T), ("tmp", 8 * T), ("vid", VT), ("tile", VT),
                                         ("chunk", VT), ("rows", VT * 4 * P), ("cols", VT * 3 * P))}
            v.update({n: take(VT).bitcast(I32) for n in ("chunk_i", "tile_i", "vid_i")})
            return v

        def visits_dve(dve, call, v):
            count, cum = cnt[call][:, 0:T], cnt[call][:, BUCKETS:BUCKETS + T]
            t = [v["tmp"][:, i * T:(i + 1) * T] for i in range(8)]
            ti = [a.bitcast(I32) for a in t]
            V.add(dve.tensor_tensor(t[0], cum, count, ALU.subtract))
            V.then(dve.tensor_scalar(t[1], cum, float(P - 1), None, ALU.add))
            V.add(dve.tensor_copy(ti[2], t[0]))
            V.then(dve.tensor_copy(ti[3], t[1]))
            V.add(dve.tensor_scalar(ti[4], ti[2], 7, None, ALU.arith_shift_right))
            V.then(dve.tensor_scalar(ti[5], ti[3], 7, None, ALU.arith_shift_right))
            V.add(dve.tensor_copy(t[0], ti[4]))
            V.then(dve.tensor_copy(t[1], ti[5]))
            V.add(dve.tensor_scalar(t[2], count, 0.0, None, ALU.is_gt))
            V.then(dve.tensor_tensor(t[3], t[1], t[0], ALU.subtract))
            V.then(dve.tensor_tensor(t[3], t[3], t[2], ALU.mult))
            V.then(dve.tensor_tensor_scan(t[4], t[3], t[3], 0.0, ALU.add, ALU.bypass))
            V.then(dve.tensor_tensor(t[5], t[4], t[3], ALU.subtract))
            V.add(dve.memset(t[7], 0.0))
            V.then(dve.tensor_tensor(t[6], t[0], t[5], ALU.subtract))
            V.add(dve.tensor_tensor(t[7][:, 0:T - 1], t[6][:, 1:T], t[6][:, 0:T - 1], ALU.subtract))
            dve.wait_ge(vis_back, call + 1)
            V.then(dve.tensor_copy(v["vid"], v["vid_i"]))
            grid = v["grid"].rearrange("p (v t) -> p v t", t=T)
            V.then(dve.tensor_tensor(grid, v["vid"].unsqueeze(2).to_broadcast([P, VT, T]),
                                     t[4].unsqueeze(1).to_broadcast([P, VT, T]), ALU.is_ge))
            V.then(dve.tensor_reduce(v["tile"], grid, AX_X, ALU.add))
            V.then(dve.tensor_tensor(grid, grid, t[7].unsqueeze(1).to_broadcast([P, VT, T]), ALU.mult))
            V.then(dve.tensor_reduce(v["chunk"], grid, AX_X, ALU.add))
            V.then(dve.tensor_tensor(v["chunk"], v["chunk"], v["vid"], ALU.add))
            V.then(dve.tensor_scalar(v["chunk"], v["chunk"], t[6][:, 0:1], float(C - 1), ALU.add, ALU.min))
            dve.tensor_copy(v["tile_i"], v["tile"]).then_inc(vis_tile, 1)
            dve.tensor_copy(v["chunk_i"], v["chunk"]).then_inc(vis_done, 1)
            V.then(dve.tensor_scalar(v["tile"], v["tile"], float(P), None, ALU.mult))
            dve.wait_ge(vis_rows, (call + 1) * VT * 16)
            cols = v["cols"].rearrange("p (v f e) -> p v f e", v=VT, f=3)
            got = v["rows"].rearrange("p (v e f) -> p v f e", v=VT, f=4)
            for j in range(VT):
                dve.tensor_copy(cols[:, j, 0:3:2, :], got[:, j, 0:3:2, :]).then_inc(vis_cols, 1)
                dve.tensor_scalar(cols[:, j, 1, :], got[:, j, 1, :], v["tile"][:, j:j + 1], None,
                                  ALU.subtract).then_inc(vis_cols, 1)
            for j in range(VT):
                dve.wait_ge(vis_ps, call * VT + j + 1)
                got = bank(j, 3 * P)
                V.add(dve.tensor_scalar(v_idx[:, j * P:(j + 1) * P], got[:, 0:P], float(NP - 1), None, ALU.min))
                V.add(dve.tensor_copy(v_loc[:, j * P:(j + 1) * P], got[:, P:2 * P]))
                V.add(dve.tensor_copy(v_w[:, j * P:(j + 1) * P], got[:, 2 * P:]))

        def visits_pool(pool, call, v):
            pool.iota(v["vid_i"], [[P, VT]], base=0, channel_multiplier=1).then_inc(vis_back, 1)
            pool.wait_ge(vis_done, call + 1)
            table = edges_by[call].rearrange("(c e) f -> c (e f)", e=P)
            for j in range(VT):
                pool.indirect_dma_start(v["rows"][:, j * 4 * P:(j + 1) * 4 * P], None, table,
                                        bass.IndirectOffsetOnAxis(ap=v["chunk_i"][:, j:j + 1], axis=0)
                                        ).then_inc(vis_rows, 16)

        def visits_pe(pe, call, v):
            cols = v["cols"].rearrange("p (v f e) -> p v f e", v=VT, f=3)
            for j in range(VT):
                pe.wait_ge(vis_cols, (call * VT + j + 1) * 2)
                for f in range(3):
                    last = pe.transpose(bank(j, P, f * P), cols[:, j, f, :], ident)
                last.then_inc(vis_ps, 1)

        def visits_sync(sp, call, v):
            sp.wait_ge(vis_tile, call + 1)
            sp.dma_start(visit_tiles[call].rearrange("(v p) -> p v", p=P), v["tile_i"],
                         allow_slow_non_contiguous=True).then_inc(vis_out, 16)
            sp.wait_ge(vis_out, 16 * (2 * call + 1))
            sp.dma_start(tile_row[0:1, :], visit_tiles[call].rearrange("(o v) -> o v", o=1)).then_inc(vis_out, 16)
            sp.wait_ge(vis_out, 16 * (2 * call + 2))

        z_x, z_e, ld_x, ld_e, kc, zero_done, z_slots = (sem(n) for n in "z_x z_e ld_x ld_e kc zero_done z_slots".split())
        scratch(FREE)
        temps = [take(C) for _ in range(4)]
        iota_i, lane_i, shift_i, shift_f = (take(n) for n in (P, 1, P + 1, P + 1))
        scratch(ACC, FREE)
        inter = take(4 * C)
        inter_done, edges_out, sort_in, sort_ps, unsorted_done, ranked = (
            sem(n) for n in "inter_done edges_out sort_in sort_ps unsorted_done ranked".split())
        iota_i, lane_i, shift_i = (a.bitcast(I32) for a in (iota_i, lane_i, shift_i))

        def load_edges(sp, to, a):
            full, at = EDGES // C, 0
            for n in (full // 16 * 16, full % 16):
                sp.dma_start(to[at:at + n, :], a[at * C:(at + n) * C].rearrange("(p c) -> p c", c=C)).then_inc(ld_e, 16)
                at += n
            sp.dma_start(to[full:full + 1, 0:EDGES - full * C],
                         a[full * C:EDGES].rearrange("(o c) -> o c", o=1)).then_inc(ld_e, 16)

        with nc.Block() as block:
            @block.sync
            def _(sp):
                sp.wait_ge(z_e, 3)
                load_edges(sp, dst_f.bitcast(I32), dst)
                load_edges(sp, src_f.bitcast(I32), src)
                load_edges(sp, w_f, edge_weight)
                sp.wait_ge(z_x, 1)
                sp.dma_start(xres[:, 0:(T - 1) * D].rearrange("p (t d) -> p t d", d=D),
                             x[0:(T - 1) * P, :].rearrange("(t p) d -> p t d", p=P)).then_inc(ld_x, 16)
                sp.dma_start(xres[0:TAIL, (T - 1) * D:], x[(T - 1) * P:, :]).then_inc(ld_x, 16)
                sp.wait_ge(inter_done, 1)
                sp.dma_start(edges_by[0].rearrange("(p c) f -> p (c f)", p=P), inter).then_inc(edges_out, 16)
                sp.wait_ge(zero_done, 1)
                tiles = SLOT_TILES + K1
                sp.dma_start(slot_rows.rearrange("(p t) (k d) -> p (t k) d", p=P, k=KD),
                             zeros.unsqueeze(1).to_broadcast([P, tiles * KD, P])).then_inc(z_slots, 16)
                sp.wait_ge(ld_x, 32)
                sp.wait_ge(z_slots, 16)
                sp.wait_ge(edges_out, 16)

            @block.gpsimd
            def _(pool):
                G.add(pool.memset(ident, 0.0))
                G.add(pool.memset(tri, 1.0))
                pool.iota(iota_i, [[1, P]], base=0, channel_multiplier=0).then_inc(kc, 1)
                pool.iota(lane_i, [[0, 1]], base=0, channel_multiplier=1).then_inc(kc, 1)
                G.settle()
                pool.affine_select(out=ident, in_=ident, compare_op=ALU.not_equal, fill=1.0, base=0,
                                   pattern=[[-1, P]], channel_multiplier=1).then_inc(kc, 1)
                pool.affine_select(out=tri, in_=tri, compare_op=ALU.is_gt, fill=0.0, base=0,
                                   pattern=[[1, P]], channel_multiplier=-1).then_inc(kc, 1)

            @block.vector
            def _(dve):
                dve.memset(dst_f.bitcast(I32), NP).then_inc(z_e, 1)
                dve.memset(src_f.bitcast(I32), NP).then_inc(z_e, 1)
                dve.memset(w_f, 0.0).then_inc(z_e, 1)
                dve.memset(xres[:, (T - 1) * D:], 0.0).then_inc(z_x, 1)
                V.add(dve.memset(ones, 1.0))
                V.add(dve.memset(base_all, 0.0))
                dve.memset(zeros, 0.0).then_inc(zero_done, 1)
                dve.wait_ge(kc, 4)
                V.add(dve.tensor_copy(iota, iota_i))
                V.add(dve.tensor_copy(lane, lane_i))
                V.add(dve.tensor_scalar(shift_i[:, 0:P], iota_i, 5, None, ALU.arith_shift_right))
                V.then(dve.tensor_scalar(shift_i[:, P:], lane_i, 5, None, ALU.arith_shift_right))
                V.add(dve.tensor_scalar(rowmask, lane, float(TAIL), None, ALU.is_lt))
                V.then(dve.tensor_copy(shift_f, shift_i))
                V.then(dve.tensor_scalar(blk, shift_f[:, 0:P], shift_f[:, P:], None, ALU.is_equal))
                dve.wait_ge(ld_e, 9 * 16)
                for a in (dst_f, src_f):
                    V.then(dve.tensor_copy(temps[0], a.bitcast(I32)))
                    V.then(dve.tensor_copy(a, temps[0]))
                rows4 = inter.rearrange("p (c f) -> p c f", f=4)
                for f, a in enumerate((src_f, dst_f, w_f)):
                    V.add(dve.tensor_copy(rows4[:, :, f], a))
                V.then(dve.memset(rows4[:, :, 3], 0.0))
                dve.sem_inc(inter_done, 1)
                rank_keys(dve, dst_f, temps)
                key_t, eq = temps[0], temps[1]
                dve.memset(unsorted_f, 0.0).then_inc(sort_in, 1)
                V.then(dve.tensor_tensor(eq[:, 1:], key_t[:, 1:], key_t[:, 0:C - 1], ALU.is_lt))
                dve.wait_ge(sort_ps, 1)
                V.add(dve.tensor_reduce(unsorted_f[:, 0:1], eq[:, 1:], AX_X, ALU.max))
                V.add(dve.tensor_tensor(unsorted_f[0:P - 1, 1:2], ps[0:P - 1, 0:1], key_t[0:P - 1, C - 1:], ALU.is_lt))
                V.settle()
                dve.sem_inc(sort_in, 1)
                dve.wait_ge(sort_ps, 2)
                V.then(dve.tensor_reduce(unsorted_f[:, 0:1], bank(1, 2), AX_X, ALU.add))
                V.then(dve.tensor_copy(unsorted, unsorted_f[:, 0:1]))
                dve.sem_inc(unsorted_done, 1)
                rank_counts(dve, 0, pos_dst, temps)
                with dve.If(dve.value_load(unsorted[0:1, 0:1], min_val=0, max_val=2 * P) > 0):
                    with V_SORT.loop(BUCKETS, 4) as b:
                        rank_tile(dve, V_SORT, b, pos_dst, temps)

            @block.tensor
            def _(pe):
                pe.wait_ge(kc, 4)
                pe.wait_ge(sort_in, 1)
                pe.matmul(ps[0:P - 1, 0:1], ident[:, 1:], temps[0][:, 0:1], start=True, stop=True).then_inc(sort_ps, 1)
                pe.wait_ge(sort_in, 2)
                pe.matmul(bank(1, 2), ones, unsorted_f, start=True, stop=True).then_inc(sort_ps, 1)
                rank_sums(pe, 0)

        scratch(ACC, ACC + BUCKETS * ACC_W)
        w0, wq_r, wkv_r, wp_r = (take(n * D) for n in (KD, KD, 2 * KD, KD))
        wqT, wkvT, wpT = (take(n * D) for n in (KD, 2 * KD, KD))
        xn7 = take(B * D)
        xt7 = take(B * D)
        ring_a, ring_b = take(B * D), take(B * D)
        rank_temps = [a[:, 0:C] for a in (xn7, xt7, ring_a, ring_b)]
        scratch(FREE)
        h7 = take(B * D)
        v7 = take(B * KD * (P + 1))
        scat_ring = take(10 * SCAT)
        ctx_m, ctx_t, ksum, ksum_b, kv_out = take(KD * P), take(KD * P), take(KD), take(KD * P), take(KD * D)
        xn7v = xn7.rearrange("p (i k n) -> p i k n", i=B, k=KD)
        xt7v = xt7.rearrange("p (i k n) -> p i k n", i=B, k=KD)
        v7v = v7.rearrange("p (i k n) -> p i k n", i=B, k=KD)
        psA, psB = bank(0, B * D), bank(4, B * D)
        psK = bank(0, B * 512).rearrange("p (i w) -> p i w", w=2 * D)
        psC = bank(7, KD * (P + 1))
        (ld_w, w_ps, w_sb, xn_done, tp_done, xt_done, h_ps, h_sb, h_st, h_free, kv_ps, k_min, k_exp, k_done, v_done,
         c_done, c_sb, c_ps, c_back, q_ps, q_min, q_exp, q_done, den_ps, qn_done, mix_ps, mix_add) = (
            sem(n) for n in ("ld_w w_ps w_sb xn_done tp_done xt_done h_ps h_sb h_st h_free kv_ps k_min k_exp k_done "
                             "v_done c_done c_sb c_ps c_back q_ps q_min q_exp q_done den_ps qn_done mix_ps mix_add"
                             ).split())

        def norm7(dve, c, base):
            dve.wait_ge(tp_done, c + (base + 1))
            for i in range(B):
                last = normalise(dve, xn7[:, i * D:(i + 1) * D], c * B + i)
            last.then_inc(xn_done, 1)

        def transpose7(pe, c, base):
            pe.wait_ge(xn_done, c + (base + 1))
            for i in range(B):
                for k in range(KD):
                    last = pe.transpose(half(0, i)[:, k * P:(k + 1) * P], xn7v[:, i, k, :], ident)
            last.then_inc(tp_done, 1)

        def keep7(act, c, base):
            act.wait_ge(tp_done, c + (base + 2))
            act.copy(xt7, psA).then_inc(xt_done, 1)
            act.copy(xnT3[:, :, ds(c * (B * P), B * P)].rearrange("p k (i n) -> p i k n", i=B),
                     psA.rearrange("p (i k n) -> p i k n", i=B, k=KD)).then_inc(xt_done, 1)

        def store7(sp, c, base, ring, table, width):
            sp.wait_ge(h_sb, c + (base + 1))
            sp.dma_start(table[ds(c * (B * P), B * P), :].rearrange("(i p) d -> p i d", p=P),
                         ring.rearrange("p (i d) -> p i d", i=B)[:, :, 0:width]).then_inc(h_st, 16)
            sp.wait_ge(h_st, c * 16 + (base + 1) * 16)
            sp.sem_inc(h_free, 1)

        with nc.Block() as block:
            @block.sync
            def _(sp):
                for to, w in ((w0, L0_gnn_W), (wq_r, L0_mix_Wq), (wkv_r, L0_mix_Wkv), (wp_r, L0_mix_Wproj)):
                    sp.dma_start(to.rearrange("p (k c) -> p k c", c=D),
                                 w.rearrange("(k p) c -> p k c", p=P)).then_inc(ld_w, 16)
                sp.sem_inc(h_free, 1)
                with sp.Fori(0, LOOPS) as c:
                    store7(sp, c, 0, h7, h0_table, D)

            @block.gpsimd
            def _(pool):
                with pool.If(pool.value_load(unsorted[0:1, 0:1], min_val=0, max_val=2 * P) > 0):
                    scatter(pool, G_SORT, 0, pos_dst, (src_f, dst_f, w_f), scat_ring)

            @block.scalar
            def _(act):
                ln_root(act)
                for n, (to, b, width) in enumerate(((wqT, 0, 512), (wkvT, 1, 1024), (wpT, 3, 512))):
                    act.wait_ge(w_ps, n + 1)
                    act.copy(to, bank(b, width)).then_inc(w_sb, 1)
                act.wait_ge(v_done, 1)
                with act.Fori(0, LOOPS) as c:
                    keep7(act, c, 0)
                    act.wait_ge(h_ps, c + 1)
                    act.wait_ge(h_free, c + 1)
                    act.copy(h7, psA).then_inc(h_sb, 1)
                    act.wait_ge(k_min, c + 1)
                    act.activation(ring_a, ring_a, ACT.Exp).then_inc(k_exp, 1)
                    act.wait_ge(c_done, c + 1)
                    act.wait_ge(k_done, c + 1)
                    act.copy(v7v[:, :, :, 0:P], psK[:, :, D:].rearrange("p i (k n) -> p i k n", k=KD)
                             ).then_inc(v_done, 1)
                act.wait_ge(c_ps, 1)
                act.copy(ctx_t, bank(0, KD * P)).then_inc(c_back, 1)
                act.wait_ge(c_ps, 2)
                act.copy(kv_out, bank(1, KD * D)).then_inc(c_back, 1)
                with act.Fori(0, LOOPS) as c:
                    act.wait_ge(q_min, c + 1)
                    act.activation(ring_a, ring_a, ACT.Exp).then_inc(q_exp, 1)

            @block.vector
            def _(dve):
                ln_stats(dve)
                dve.memset(v7, 1.0).then_inc(v_done, 1)
                with dve.Fori(0, LOOPS) as c:
                    norm7(dve, c, 0)
                    dve.wait_ge(kv_ps, c + 1)
                    dve.tensor_scalar(ring_a, psK[:, :, 0:D], 0.0, None, ALU.min).then_inc(k_min, 1)
                    dve.wait_ge(k_exp, c + 1)
                    dve.wait_ge(c_done, c + 1)
                    dve.scalar_tensor_tensor(ring_b.rearrange("p (i d) -> p i d", i=B), psK[:, :, 0:D], 0.0,
                                             ring_a.rearrange("p (i d) -> p i d", i=B), ALU.max, ALU.add
                                             ).then_inc(k_done, 1)
                dve.wait_ge(c_done, LOOPS + 1)
                for j in range(KD):
                    V.add(dve.tensor_tensor(ctx_m[:, j * P:(j + 1) * P], psC[:, j * (P + 1):j * (P + 1) + P], blk,
                                            ALU.mult))
                last = dve.tensor_scalar(ksum, psC[:, P::P + 1], float(NODES - NP), None, ALU.add)
                V.then(last)
                for j in range(KD):
                    last = dve.tensor_scalar(ksum_b[:, j * P:(j + 1) * P], blk, ksum[:, j:j + 1], None, ALU.mult)
                last.then_inc(c_sb, 1)
                with V.loop(LOOPS, 2) as c:
                    dve.wait_ge(q_ps, c + 1)
                    dve.tensor_scalar(ring_a, psA, 0.0, None, ALU.min).then_inc(q_min, 1)
                    dve.wait_ge(q_exp, c + 1)
                    dve.scalar_tensor_tensor(ring_b, psA, 0.0, ring_a, ALU.max, ALU.add).then_inc(q_done, 1)
                    dve.wait_ge(den_ps, c + 1)
                    V.then(dve.tensor_scalar(xn7, psB, D_MIN, None, ALU.max))
                    V.then(dve.reciprocal(xn7, xn7))
                    dve.tensor_tensor(ring_b, ring_b, xn7, ALU.mult).then_inc(qn_done, 1)
                    dve.wait_ge(mix_ps, c + 1)
                    dve.tensor_tensor(xres[:, ds(c * (B * D), B * D)], xres[:, ds(c * (B * D), B * D)], psA, ALU.add
                                      ).then_inc(mix_add, 1)
                rank_keys(dve, src_f, rank_temps)
                rank_counts(dve, 1, pos_src, rank_temps)

            @block.tensor
            def _(pe):
                pe.sem_inc(tp_done, 1)
                pe.wait_ge(ld_w, 64)
                for n, (raw, b, blocks) in enumerate(((wq_r, 0, KD), (wkv_r, 1, 2 * KD), (wp_r, 3, KD))):
                    for k in range(KD):
                        for o in range(blocks):
                            last = pe.transpose(bank(b, P, (k * blocks + o) * P),
                                                raw[:, o * D + k * P:o * D + (k + 1) * P], ident)
                    last.then_inc(w_ps, 1)
                pe.wait_ge(w_sb, 3)
                pe.wait_ge(v_done, 1)
                pe.matmul(psC, zeros, v7[:, 0:KD * (P + 1)], start=True, stop=False, skip_group_check=True)
                pe.sem_inc(c_done, 1)
                with pe.Fori(0, LOOPS) as c:
                    transpose7(pe, c, 0)
                    pe.wait_ge(xt_done, c * 2 + 2)
                    for i in range(B):
                        for k in range(KD):
                            last = pe.matmul(half(0, i), xt7v[:, i, k, :], w0[:, k * D:(k + 1) * D],
                                             start=(k == 0), stop=(k == KD - 1))
                    last.then_inc(h_ps, 1)
                    pe.wait_ge(h_sb, c + 1)
                    for i in range(B):
                        for k in range(KD):
                            last = pe.matmul(psK[:, i, :], xt7v[:, i, k, :],
                                             wkvT[:, k * 2 * D:(k + 1) * 2 * D], start=(k == 0), stop=(k == KD - 1))
                    last.then_inc(kv_ps, 1)
                    pe.wait_ge(k_done, c + 1)
                    pe.wait_ge(v_done, c + 2)
                    for i in range(B):
                        for k in range(KD):
                            last = pe.matmul(psC[:, k * (P + 1):(k + 1) * (P + 1)],
                                             ring_b[:, i * D + k * P:i * D + (k + 1) * P], v7v[:, i, k, :],
                                             start=False, stop=False, skip_group_check=True)
                    last.then_inc(c_done, 1)
                pe.wait_ge(c_sb, 1)
                for j in range(KD):
                    last = pe.transpose(bank(0, P, j * P), ctx_m[:, j * P:(j + 1) * P], ident)
                last.then_inc(c_ps, 1)
                pe.wait_ge(c_back, 1)
                for j in range(KD):
                    last = pe.matmul(bank(1, D, j * D), ctx_t[:, j * P:(j + 1) * P], wpT[:, j * D:(j + 1) * D],
                                     start=True, stop=True)
                last.then_inc(c_ps, 1)
                pe.wait_ge(c_back, 2)
                pe.sem_inc(mix_add, 1)
                with pe.Fori(0, LOOPS) as c:
                    pe.wait_ge(mix_add, c + 1)
                    for i in range(B):
                        for o in range(KD):
                            for k in range(KD):
                                last = pe.matmul(half(0, i)[:, o * P:(o + 1) * P],
                                                 wqT[:, k * D + o * P:k * D + (o + 1) * P],
                                                 xnT3[:, k, ds((c * B + i) * P, P)], start=(k == 0), stop=(k == KD - 1))
                    last.then_inc(q_ps, 1)
                    pe.wait_ge(q_done, c + 1)
                    for i in range(B):
                        for k in range(KD):
                            q = ring_b[:, i * D + k * P:i * D + (k + 1) * P]
                            last = pe.matmul(half(4, i)[:, k * P:(k + 1) * P], ksum_b[:, k * P:(k + 1) * P], q,
                                             start=True, stop=True)
                    last.then_inc(den_ps, 1)
                    pe.wait_ge(qn_done, c + 1)
                    for i in range(B):
                        for k in range(KD):
                            q = ring_b[:, i * D + k * P:i * D + (k + 1) * P]
                            last = pe.matmul(half(0, i), q, kv_out[:, k * D:(k + 1) * D],
                                             start=(k == 0), stop=(k == KD - 1))
                    last.then_inc(mix_ps, 1)
                rank_sums(pe, 1)

        gather_done = [[sem(f"gather{b}{u}_done") for u in range(U)] for b in range(2)]
        edges_ready, tiles_ready, hot_done, gnn_ps, gnn_add = (sem(n) for n in (
            "edges_ready", "tiles_ready", "hot_done", "gnn_ps", "gnn_add"))
        scratch(XNT, ACC)
        vv = visit_views()
        rows = take(2 * U * ROW1).rearrange("p (b u w) -> p b u w", b=2, u=U)
        scratch(FREE)
        hot = take(2 * U * P).rearrange("p (b u n) -> p b u n", b=2, u=U)
        idx_ring = take(2 * U).bitcast(I32)
        rank_temps = [w_f, pos_dst, take(C), take(C)]
        NVIS = GROUP_LOOPS * 2 * U
        assert GROUP_LOOPS >= BUCKETS
        GNN0_BANKS, GNN1_BANKS = 8, 4

        def gather_rows(pool, call, table, width):
            pool.wait_ge(edges_ready, call + 1)
            with G.loop(GROUP_LOOPS, 2) as j:
                for b in range(2):
                    pool.wait_ge(gnn_ps, j * (2 * U) + (call * (NVIS + 2 * U) + (b + 1) * U))
                    G.then(pool.tensor_copy(idx_ring[:, b * U:(b + 1) * U], v_idx[:, ds(j * (2 * U) + b * U, U)]))
                    pool.sem_inc(dma_turn, 1)
                    for u in range(U):
                        pool.indirect_dma_start(rows[:, b, u, 0:width], None, table, bass.IndirectOffsetOnAxis(
                            ap=idx_ring[:, b * U + u:b * U + u + 1], axis=0)).then_inc(gather_done[b][u], 16)

        def gathered(engine, call, j, b, u):
            engine.wait_ge(gather_done[b][u], j * 16 + (call * GROUP_LOOPS + 1) * 16)

        def load_tiles(engine, first):
            return nc.values_load_multi_w_load_instructions(
                tile_row[0:1, ds(first, U)], engines=[engine.engine], min_val=0, max_val=T,
                skip_runtime_bounds_check_because="a visit's tile is a count of at most T tiles")[1]

        def add_sums(dve, call, j, b, u, tile, width, banks):
            n = j * (2 * U) + b * U + u
            dve.wait_ge(gnn_ps, n + (call * (NVIS + 2 * U) + 2 * U + 1))
            dve.wait_ge(gnn_add, n + (call * (NVIS + GNN0_BANKS) + banks[1]))
            to = acc[:, ds(tile * ACC_W, width)]
            dve.tensor_tensor(to, to, bank(banks[0] + u % banks[1], width), ALU.add).then_inc(gnn_add, 1)

        with nc.Block() as block:
            @block.sync
            def _(sp):
                visits_sync(sp, 0, vv)
                sp.sem_inc(tiles_ready, 1)

            @block.gpsimd
            def _(pool):
                visits_pool(pool, 0, vv)
                gather_rows(pool, 0, h0_table, D)

            @block.vector
            def _(dve):
                visits_dve(dve, 0, vv)
                V.then(dve.memset(acc, 0.0))
                dve.sem_inc(edges_ready, 1)
                dve.sem_inc(gnn_add, GNN0_BANKS)
                rank_keys(dve, src_f, rank_temps)
                dve.wait_ge(tiles_ready, 1)
                with V.loop(GROUP_LOOPS, 4) as j:
                    for b in range(2):
                        for u in range(U):
                            n = j * (2 * U) + b * U + u
                            dve.tensor_scalar(hot[:, b, u, :], iota, v_loc[:, ds(n, 1)], v_w[:, ds(n, 1)],
                                              ALU.is_equal, ALU.mult).then_inc(hot_done, 1)
                        tiles = load_tiles(dve, j * (2 * U) + b * U)
                        for u in range(U):
                            add_sums(dve, 0, j, b, u, tiles[u], D, (0, GNN0_BANKS))
                        if b == 0:
                            rank_tile(dve, V, j, pos_src, rank_temps)

            @block.tensor
            def _(pe):
                visits_pe(pe, 0, vv)
                pe.sem_inc(gnn_ps, 2 * U)
                pe.wait_ge(edges_ready, 1)
                with pe.Fori(0, GROUP_LOOPS) as j:
                    for b in range(2):
                        for u in range(U):
                            n = j * (2 * U) + b * U + u
                            pe.wait_ge(hot_done, n + 1)
                            gathered(pe, 0, j, b, u)
                            pe.wait_ge(gnn_add, n + 1)
                            pe.matmul(bank(u, D), hot[:, b, u, :], rows[:, b, u, 0:D], start=True, stop=True
                                      ).then_inc(gnn_ps, 1)

        scratch(FREE)
        scat_ring = take(10 * SCAT)
        xn7, xt7 = take(B * D), take(B * D)
        bias_b, bproj_b = take(D), take(D)
        idx_f = take(T)
        rev = take(E0)
        rw_t, router_b, expert_of, b1_t, b2_s = take(KD * E0), take(E0), take(HB), take(HB), take(D)
        scratch(place["at"])
        mean56, std56 = take(B * D // HC), take(B * D // HC)
        scratch(ACC, ACC + BUCKETS * ACC_W)
        w1_s, w2_s = take(KD * E0 * H0), take(HB * D)
        RINGS0 = place["at"]
        h_ring = [take(B * P) for _ in range(2)]
        hm_ring = [take(B * P) for _ in range(2)]
        logits, is_top = (arena[:, RINGS0 + i * T * E0:RINGS0 + (i + 1) * T * E0] for i in range(2))
        assert RINGS0 + 2 * T * E0 <= place["at"]
        idx_b = take(B * P)
        rw_raw = idx_b[0:E0, 0:D]
        w_f_at = ACC + BUCKETS * ACC_W + 3 * C
        scratch(w_f_at, FREE)
        hot32 = take(B * P)
        g1_w = take(KD * ROW1)
        scratch(ACC, ACC + BUCKETS * ACC_W)
        z7 = take(B * KD * (P + 1))
        xc7, sq7, h7 = take(B * D), take(B * D), take(B * ROW1)
        al_b, ar_b, wa_tmp = take(D), take(D), take(D)
        wk_c, bk_c, wv_b, bv_b, kcol = take(KD), take(KD), take(D), take(D), take(2 * KD)
        s_bc, kvm, kv_t = take(KD * P), take(KD * P), take(KD * P)
        xn7v = xn7.rearrange("p (i k n) -> p i k n", i=B, k=KD)
        xt7v = xt7.rearrange("p (i k n) -> p i k n", i=B, k=KD)
        z7v = z7.rearrange("p (i k n) -> p i k n", i=B, k=KD)
        w1v = w1_s.rearrange("p (k m) -> p k m", k=KD)
        (ld_b, ld_e1, ld_e2, ld_g, x1_done, rw_ps, rw_sb, lg_ps, lg_sb, ib_done, ib_ps, hot_e, m1_ps, he_done, hm_done,
         m2_ps, x2_add, x2_done, sq_in, sq_done, ss_done, sd_done, z_done, gram, s_done, s_ps, kvm_done, xs_done,
         mx_ps, mx_add) = (sem(n) for n in (
             "ld_b ld_e1 ld_e2 ld_g x1_done rw_ps rw_sb lg_ps lg_sb ib_done ib_ps hot_e m1_ps he_done hm_done m2_ps "
             "x2_add x2_done sq_in sq_done ss_done sd_done z_done gram s_done s_ps kvm_done xs_done mx_ps mx_add"
         ).split())
        CALL1, CALL2 = LOOPS, 2 * LOOPS

        def mask_padding(dve):
            last = xres[:, (T - 1) * D:]
            V.then(dve.tensor_scalar(last, last, rowmask, None, ALU.mult))

        with nc.Block() as block:
            @block.sync
            def _(sp):
                for to, a in ((bias_b, L0_gnn_b), (bproj_b, L0_mix_bproj), (router_b, L0_ffn_router_b)):
                    sp.dma_start(to, a.partition_broadcast(P)).then_inc(ld_b, 16)
                sp.dma_start(b1_t, L0_ffn_b1.rearrange("e h -> (e h)").rearrange("(j p) -> p j", p=P),
                             allow_slow_non_contiguous=True).then_inc(ld_b, 16)
                sp.dma_start(b2_s[0:E0, :], L0_ffn_b2).then_inc(ld_b, 16)
                sp.dma_start(g1_w.rearrange("p (k w) -> p k w", k=KD)[:, :, 0:D],
                             L1_gnn_W.rearrange("(k p) w -> p k w", p=P)).then_inc(ld_b, 16)
                sp.wait_ge(x1_done, 1)
                sp.dma_start(rw_raw, L0_ffn_router_w).then_inc(ld_e1, 16)
                for k in range(KD):
                    sp.dma_start(w1v[:, k, :].rearrange("p (e h) -> p e h", h=H0),
                                 L0_ffn_W1[:, k * P:(k + 1) * P, :].rearrange("e p h -> p e h")).then_inc(ld_e2, 16)
                sp.dma_start(w2_s.rearrange("p (j d) -> p j d", d=D),
                             L0_ffn_W2.rearrange("e h d -> (e h) d").rearrange("(j p) d -> p j d", p=P)
                             ).then_inc(ld_e2, 16)
                sp.wait_ge(ld_e2, 48)
                sp.wait_ge(x2_done, 1)
                sp.dma_start(al_b, L1_gnn_a_l.rearrange("o h f -> (o h f)").partition_broadcast(P)).then_inc(ld_g, 16)
                sp.dma_start(ar_b, L1_gnn_a_r.rearrange("o h f -> (o h f)").partition_broadcast(P)).then_inc(ld_g, 16)
                for to, a in ((wk_c, L1_mix_kln_weight), (bk_c, L1_mix_kln_bias)):
                    sp.dma_start(to, a.rearrange("h o c -> (h o c)").rearrange("(k p) -> p k", p=P),
                                 allow_slow_non_contiguous=True).then_inc(ld_g, 16)
                for to, a in ((wv_b, L1_mix_vln_weight), (bv_b, L1_mix_vln_bias)):
                    sp.dma_start(to, a.rearrange("h o c -> (h o c)").partition_broadcast(P)).then_inc(ld_g, 16)
                with sp.Fori(0, LOOPS) as c:
                    store7(sp, c, CALL1, h7, h1_table, ROW1)

            @block.gpsimd
            def _(pool):
                scatter(pool, G, 1, pos_src, (dst_f, src_f), scat_ring)

            @block.scalar
            def _(act):
                ln_root(act)
                act.wait_ge(rw_ps, 1)
                act.copy(rw_t, bank(7, KD * E0)).then_inc(rw_sb, 1)
                with act.Fori(0, LOOPS) as c:
                    keep7(act, c, CALL1)
                act.wait_ge(ld_b, 6 * 16)
                with act.Fori(0, LOOPS) as c:
                    for j in range(HB):
                        act.wait_ge(m1_ps, c * HB + (j + 1))
                        if j >= 2:
                            act.wait_ge(hm_done, c * HB + (j - 1))
                        act.activation(h_ring[j % 2].rearrange("p (f n) -> p f n", f=2),
                                       bank(2 * (j % 2), 1024).rearrange("p (f n) -> p f n", f=2)[:, :, 0:HALF],
                                       ACT.Relu, bias=b1_t[:, j:j + 1]).then_inc(he_done, 1)
                ln_root(act)
                with act.Fori(0, LOOPS) as c:
                    keep7(act, c, CALL2)
                    act.wait_ge(sq_in, c + 1)
                    act.activation(sq7, xc7, ACT.Square).then_inc(sq_done, 1)
                    act.wait_ge(ss_done, c + 1)
                    act.activation(std56, std56, ACT.Sqrt, scale=1.0 / (HC - 1)).then_inc(sd_done, 1)
                    act.wait_ge(h_ps, c + (LOOPS + 1))
                    act.wait_ge(h_free, c + (LOOPS + 1))
                    got = bank(0, B * 512).rearrange("p (i w) -> p i w", w=512)
                    act.copy(rl_all[:, ds(c * (B * 2 * GH), B * 2 * GH)].rearrange("p (i w) -> p i w", i=B),
                             got[:, :, D:ROW1])
                    act.copy(h7.rearrange("p (i w) -> p i w", i=B), got[:, :, 0:ROW1]).then_inc(h_sb, 1)
                act.sem_inc(xs_done, 1)
                with act.Fori(0, LOOPS) as c:
                    act.wait_ge(mx_ps, c + 1)
                    act.copy(xt7v.rearrange("p i k n -> p k i n"),
                             xnT3[:, :, ds(c * (B * P), B * P)].rearrange("p k (i n) -> p k i n", i=B)
                             ).then_inc(xs_done, 1)

            @block.vector
            def _(dve):
                dve.wait_ge(ld_b, 6 * 16)
                with V.loop(LOOPS, 3) as c:
                    a = xres[:, ds(c * (B * D), B * D)].rearrange("p (i d) -> p i d", i=B)
                    t = xn7.rearrange("p (i d) -> p i d", i=B)
                    got = acc[:, ds(c * (B * ACC_W), B * ACC_W)].rearrange("p (i w) -> p i w", i=B)[:, :, 0:D]
                    wide = [w.unsqueeze(1).to_broadcast([P, B, D]) for w in (bias_b, bproj_b)]
                    V.then(dve.tensor_tensor(t, got, wide[0], ALU.add))
                    V.then(dve.scalar_tensor_tensor(t, t, 0.0, wide[1], ALU.max, ALU.add))
                    V.then(dve.tensor_tensor(a, a, t, ALU.add))
                dve.sem_inc(x1_done, 1)
                mask_padding(dve)
                ln_stats(dve)
                with V.loop(LOOPS, 1) as c:
                    norm7(dve, c, CALL1)
                    dve.wait_ge(lg_ps, c + 1)
                    V.then(dve.tensor_copy(logits[:, ds(c * (B * E0), B * E0)], bank(4, B * E0)))
                wide = [P, T, E0]
                lg3, eq3 = (a.rearrange("p (t e) -> p t e", e=E0) for a in (logits, is_top))
                V.add(dve.tensor_scalar(rev, iota[:, 0:E0], -1.0, float(E0), ALU.mult, ALU.add))
                V.then(dve.tensor_reduce(idx_f, lg3, AX_X, ALU.max))
                V.then(dve.tensor_tensor(eq3, lg3, idx_f.unsqueeze(2).to_broadcast(wide), ALU.is_ge))
                V.then(dve.tensor_tensor(eq3, eq3, rev.unsqueeze(1).to_broadcast(wide), ALU.mult))
                V.then(dve.tensor_reduce(idx_f, eq3, AX_X, ALU.max))
                V.then(dve.tensor_scalar(idx_f, idx_f, -1.0, float(E0), ALU.mult, ALU.add))
                V.then(dve.tensor_scalar(mean56[:, 0:1], lane, float(H0), None, ALU.is_ge))
                V.then(dve.tensor_scalar(expert_of, iota[:, 0:HB], 2.0, mean56[:, 0:1], ALU.mult, ALU.add))
                with dve.Fori(0, LOOPS) as c:
                    dve.tensor_copy(xn7[:, 0:B * P].rearrange("p (i n) -> p i n", i=B),
                                    idx_f[:, ds(c * B, B)].unsqueeze(2).to_broadcast([P, B, P])).then_inc(ib_done, 1)
                    dve.wait_ge(ib_ps, c + 1)
                    dve.tensor_copy(idx_b, bank(0, B * P)).then_inc(hot_e, 1)
                    dve.tensor_scalar(hot32[0:E0, :], ps[0:E0, 0:B * P], lane[0:E0, :], None, ALU.is_equal
                                      ).then_inc(hot_e, 1)
                    dve.wait_ge(hot_e, c * 2 + 2)
                    for j in range(HB):
                        dve.wait_ge(he_done, c * HB + (j + 1))
                        if j >= 2:
                            dve.wait_ge(m2_ps, c * HB + (j - 1))
                        dve.scalar_tensor_tensor(hm_ring[j % 2], idx_b, expert_of[:, j:j + 1], h_ring[j % 2],
                                                 ALU.is_equal, ALU.mult).then_inc(hm_done, 1)
                    dve.wait_ge(m2_ps, c * HB + HB)
                    a = xres[:, ds(c * (B * D), B * D)]
                    dve.scalar_tensor_tensor(a, psB, 0.0, a, ALU.max, ALU.add).then_inc(x2_add, 1)
                dve.wait_ge(x2_add, LOOPS + 1)
                dve.sem_inc(x2_done, 1)
                mask_padding(dve)
                ln_stats(dve)
                dve.wait_ge(ld_g, 6 * 16)
                for k in range(KD):
                    for f, a in ((0, ar_b), (1, al_b)):
                        V.then(dve.tensor_tensor(wa_tmp, g1_w[:, k * ROW1:k * ROW1 + D], a, ALU.mult))
                        at = k * ROW1 + D + f * GH
                        V.then(dve.tensor_reduce(g1_w[:, at:at + GH], wa_tmp.rearrange("p (h f) -> p h f", h=GH),
                                                 AX_X, ALU.add))
                dve.memset(z7, 1.0).then_inc(z_done, 1)
                with V.loop(LOOPS, 5) as c:
                    norm7(dve, c, CALL2)
                    dve.wait_ge(xn_done, c + (CALL2 + 1))
                    heads = xn7.rearrange("p (m e) -> p m e", e=HC)
                    cents = xc7.rearrange("p (m e) -> p m e", e=HC)
                    V.then(dve.tensor_reduce(mean56, heads, AX_X, ALU.add))
                    V.then(dve.tensor_scalar(mean56, mean56, 1.0 / HC, None, ALU.mult))
                    dve.tensor_tensor(cents, heads, mean56.unsqueeze(2).to_broadcast([P, B * D // HC, HC]),
                                      ALU.subtract).then_inc(sq_in, 1)
                    dve.wait_ge(sq_done, c + 1)
                    dve.tensor_reduce(std56, sq7.rearrange("p (m e) -> p m e", e=HC), AX_X, ALU.add
                                      ).then_inc(ss_done, 1)
                    dve.wait_ge(sd_done, c + 1)
                    V.then(dve.tensor_scalar(std56, std56, KV_EPS, None, ALU.add))
                    V.then(dve.reciprocal(std56, std56))
                    dve.wait_ge(gram, c + 1)
                    V.add(dve.tensor_tensor(
                        z7.rearrange("p (m w) -> p m w", w=P + 1)[:, :, 0:P].rearrange("p m (h e) -> p m h e", e=HC),
                        xc7.rearrange("p (m h e) -> p m h e", m=B * KD, e=HC),
                        std56.rearrange("p (m h) -> p m h", m=B * KD).unsqueeze(3).to_broadcast(
                            [P, B * KD, P // HC, HC]), ALU.mult))
                    V.settle()
                    dve.sem_inc(z_done, 1)
                dve.wait_ge(gram, LOOPS + 1)
                V.add(dve.tensor_tensor(kcol[:, 0:KD], wk_c, psC[:, P::P + 1], ALU.mult))
                V.add(dve.tensor_scalar(kcol[:, KD:], bk_c, float(NODES), None, ALU.mult))
                for k in range(KD):
                    last = dve.tensor_copy(s_bc[:, k * P:(k + 1) * P],
                                           psC[:, k * (P + 1) + P:(k + 1) * (P + 1)].to_broadcast([P, P]))
                last.then_inc(s_done, 1)
                V.settle()
                dve.wait_ge(s_ps, 1)
                for k in range(KD):
                    m, at = kvm[:, k * P:(k + 1) * P], slice(k * P, (k + 1) * P)
                    t = kv_t[:, at]
                    V.add(dve.scalar_tensor_tensor(m, psC[:, k * (P + 1):k * (P + 1) + P], wk_c[:, k:k + 1],
                                                   wv_b[:, at], ALU.mult, ALU.mult))
                    V.then(dve.tensor_tensor(t, bank(0, P, k * P), wv_b[:, at], ALU.mult))
                    V.then(dve.scalar_tensor_tensor(m, bv_b[:, at], kcol[:, k:k + 1], m, ALU.mult, ALU.add))
                    V.then(dve.scalar_tensor_tensor(m, t, bk_c[:, k:k + 1], m, ALU.mult, ALU.add))
                    V.then(dve.scalar_tensor_tensor(m, bv_b[:, at], kcol[:, KD + k:KD + k + 1], m, ALU.mult, ALU.add))
                    V.then(dve.scalar_tensor_tensor(m, m, 1.0 / NODES, blk, ALU.mult, ALU.mult))
                    last = dve.tensor_tensor(m, m, ident, ALU.add)
                last.then_inc(kvm_done, 1)
                with dve.Fori(0, LOOPS) as c:
                    dve.wait_ge(mx_ps, c + 2)
                    a = xres[:, ds(c * (B * D), B * D)]
                    dve.tensor_tensor(a, a, psB, ALU.add).then_inc(mx_add, 1)

            @block.tensor
            def _(pe):
                pe.wait_ge(ld_e1, 16)
                for k in range(KD):
                    last = pe.transpose(bank(7, E0, k * E0), rw_raw[:, k * P:(k + 1) * P], ident[0:E0, 0:E0])
                last.then_inc(rw_ps, 1)
                pe.wait_ge(rw_sb, 1)
                pe.wait_ge(ld_b, 6 * 16)
                with pe.Fori(0, LOOPS) as c:
                    transpose7(pe, c, CALL1)
                    pe.wait_ge(xt_done, c * 2 + (2 * CALL1 + 2))
                    for i in range(B):
                        to = bank(4, E0, i * E0)
                        for k in range(KD):
                            pe.matmul(to, xt7v[:, i, k, :], rw_t[:, k * E0:(k + 1) * E0], start=(k == 0), stop=False)
                        last = pe.matmul(to, ones[0:1, :], router_b[0:1, :], start=False, stop=True)
                    last.then_inc(lg_ps, 1)
                pe.wait_ge(ld_e2, 48)
                pe.sem_inc(x2_add, 1)
                with pe.Fori(0, LOOPS) as c:
                    def hidden(j):
                        for f in range(2):
                            for k in range(KD):
                                last = pe.matmul(bank(2 * (j % 2) + f, HALF), w1v[:, k, j * P:(j + 1) * P],
                                                 xnT3[:, k, ds(c * (B * P) + f * HALF, HALF)],
                                                 start=(k == 0), stop=(k == KD - 1))
                        last.then_inc(m1_ps, 1)

                    pe.wait_ge(ib_done, c + 1)
                    for i in range(B):
                        last = pe.transpose(bank(0, P, i * P), xn7[:, i * P:(i + 1) * P], ident)
                    last.then_inc(ib_ps, 1)
                    pe.wait_ge(hot_e, c * 2 + 2)
                    pe.wait_ge(x2_add, c + 1)
                    for i in range(B):
                        pe.matmul(half(4, i), hot32[0:E0, i * P:(i + 1) * P], b2_s[0:E0, :], start=(i % 2 == 0),
                                  stop=False, skip_group_check=True)
                    hidden(0)
                    for j in range(HB):
                        if j + 1 < HB:
                            hidden(j + 1)
                        pe.wait_ge(hm_done, c * HB + (j + 1))
                        for i in range(B):
                            last = pe.matmul(half(4, i), hm_ring[j % 2][:, i * P:(i + 1) * P],
                                             w2_s[:, j * D:(j + 1) * D], start=False, stop=(j == HB - 1),
                                             skip_group_check=True)
                        last.then_inc(m2_ps, 1)
                pe.wait_ge(z_done, 1)
                pe.matmul(psC, zeros, z7[:, 0:KD * (P + 1)], start=True, stop=False, skip_group_check=True)
                pe.sem_inc(gram, 1)
                with pe.Fori(0, LOOPS) as c:
                    transpose7(pe, c, CALL2)
                    pe.wait_ge(xt_done, c * 2 + (2 * CALL2 + 2))
                    for i in range(B):
                        for k in range(KD):
                            last = pe.matmul(bank(i, ROW1), xt7v[:, i, k, :], g1_w[:, k * ROW1:(k + 1) * ROW1],
                                             start=(k == 0), stop=(k == KD - 1))
                    last.then_inc(h_ps, 1)
                    pe.wait_ge(z_done, c + 2)
                    for i in range(B):
                        for k in range(KD):
                            last = pe.matmul(psC[:, k * (P + 1):(k + 1) * (P + 1)], z7v[:, i, k, 0:P], z7v[:, i, k, :],
                                             start=False, stop=False, skip_group_check=True)
                    last.then_inc(gram, 1)
                    pe.wait_ge(h_sb, c + (CALL1 + 1))
                pe.wait_ge(s_done, 1)
                for k in range(KD):
                    last = pe.matmul(bank(0, P, k * P), s_bc[:, k * P:(k + 1) * P], ident, start=True, stop=True)
                last.then_inc(s_ps, 1)
                pe.wait_ge(kvm_done, 1)
                pe.sem_inc(mx_ps, 1)
                pe.sem_inc(mx_add, 1)
                with pe.Fori(0, LOOPS) as c:
                    pe.wait_ge(xs_done, c + 2)
                    pe.wait_ge(mx_add, c + 1)
                    for i in range(B):
                        for k in range(KD):
                            last = pe.matmul(half(4, i)[:, k * P:(k + 1) * P], xt7v[:, i, k, :],
                                             kvm[:, k * P:(k + 1) * P], start=True, stop=True)
                    last.then_inc(mx_ps, 1)

        scratch(XNT, ACC)
        vv = visit_views()
        rows = take(2 * U * ROW1).rearrange("p (b u w) -> p b u w", b=2, u=U)
        scratch(ACC + BUCKETS * ACC_W)
        hot_b, hot_t = take(U * P // 2).bitcast(BF16), take(U * P // 2).bitcast(BF16)
        ident_b = take(P // 2).bitcast(BF16)
        lc = take(BUCKETS * 2 * GH)
        lc_parts = take(BUCKETS * PARTS * 2 * GH // 2).bitcast(BF16)
        look = take(U * 2 * GH).rearrange("p (u w) -> p u w", u=U)
        r_max, r_rows = take(GH), take(GH * P)
        score = take(U * GH).rearrange("p (u h) -> p u h", u=U)
        assert place["at"] <= FREE
        scratch(FREE)
        hot = take(2 * U * P).rearrange("p (b u n) -> p b u n", b=2, u=U)
        idx_ring = take(2 * U).bitcast(I32)
        den7, t7 = take(B * GH), take(B * D)
        lc3 = lc.rearrange("p (t w) -> p t w", w=2 * GH)
        rl3 = rl_all.rearrange("p (t w) -> p t w", w=2 * GH)
        lcp = lc_parts.rearrange("p (t q w) -> p t q w", q=PARTS, w=2 * GH)
        LW = PARTS * 2 * GH
        (rm_done, rm_ps, lc_done, hots_done, hott_ps, hott_done, look_ps, score_done, ex_done, msg_done,
         hot_done32) = (
            sem(n) for n in ("rm_done rm_ps lc_done hots_done hott_ps hott_done look_ps score_done ex_done "
                             "msg_done hot_done32").split())

        with nc.Block() as block:
            @block.sync
            def _(sp):
                visits_sync(sp, 1, vv)
                sp.sem_inc(tiles_ready, 1)

            @block.gpsimd
            def _(pool):
                visits_pool(pool, 1, vv)
                gather_rows(pool, 1, h1_table, ROW1)

            @block.scalar
            def _(act):
                def keep_hot(g):
                    act.wait_ge(hott_ps, g + 1)
                    act.copy(hot_t, bank(0, U * P // 2).bitcast(BF16)).then_inc(hott_done, 1)

                def widen_hot(g, b):
                    act.wait_ge(hots_done, g + 1)
                    act.copy(hot[:, b, :, :].rearrange("p u n -> p (u n)"), hot_b).then_inc(hot_done32, 1)

                for g in range(2):
                    keep_hot(g)
                    widen_hot(g, g)
                with act.Fori(0, GROUP_LOOPS) as j:
                    for b in range(2):
                        act.wait_ge(score_done, j * 2 + (b + 1))
                        act.activation(rows[:, b, :, D:D + GH], score, ACT.Exp).then_inc(ex_done, 1)
                        keep_hot(j * 2 + (b + 2))
                        act.wait_ge(gnn_ps, j * (2 * U) + (NVIS + 4 * U + (b + 1) * U))
                        widen_hot(j * 2 + (b + 2), b)

            @block.vector
            def _(dve):
                V.then(dve.tensor_reduce(r_max, rl3[:, 0:T, 0:GH].rearrange("p t h -> p h t"), AX_X, ALU.max))
                dve.tensor_copy(r_rows.rearrange("p (h n) -> p h n", h=GH),
                                r_max.unsqueeze(2).to_broadcast([P, GH, P])).then_inc(rm_done, 1)
                dve.wait_ge(rm_ps, 1)
                V.then(dve.tensor_reduce(r_max, bank(3, GH * P).rearrange("p (h n) -> p h n", h=GH), AX_X, ALU.max))
                V.then(dve.memset(lc, 0.0))
                V.add(dve.tensor_copy(lc3[:, 0:T, 0:GH], rl3[:, 0:T, GH:]))
                bound = lc3[:, 0:T, GH:]
                V.then(dve.tensor_tensor(bound, rl3[:, 0:T, GH:], r_max.unsqueeze(1).to_broadcast([P, T, GH]), ALU.add))
                V.then(dve.scalar_tensor_tensor(bound, bound, ALPHA, bound, ALU.mult, ALU.max))
                V.then(dve.tensor_scalar(bound, bound, -LIFT, None, ALU.add))
                for q in range(PARTS):
                    V.then(dve.tensor_copy(lcp[:, :, q, :], lc3))
                    if q + 1 < PARTS:
                        V.then(dve.tensor_tensor(lc3, lc3, lcp[:, :, q, :], ALU.subtract))
                V.then(dve.tensor_copy(ident_b, ident))
                dve.sem_inc(lc_done, 1)
                visits_dve(dve, 1, vv)
                V.then(dve.memset(acc, 0.0))
                dve.sem_inc(edges_ready, 1)
                dve.sem_inc(gnn_add, GNN1_BANKS)
                dve.wait_ge(tiles_ready, 2)

                def one_hot(g, first):
                    dve.wait_ge(hot_done32, g)
                    wide = [P, U, P]
                    dve.tensor_tensor(hot_b.rearrange("p (u n) -> p u n", u=U), iota.unsqueeze(1).to_broadcast(wide),
                                      v_loc[:, ds(first, U)].unsqueeze(2).to_broadcast(wide), ALU.is_equal
                                      ).then_inc(hots_done, 1)

                one_hot(0, 0)
                one_hot(1, U)
                with V.loop(GROUP_LOOPS, 2 * 4) as j:
                    for b in range(2):
                        for u in range(U):
                            gathered(dve, 1, j, b, u)
                        dve.wait_ge(look_ps, j * 2 + (b + 1))
                        V.then(dve.tensor_reduce(look, bank(2 + b, U * LW).rearrange(
                            "p (u q w) -> p u w q", u=U, q=PARTS), AX_X, ALU.add))
                        V.then(dve.tensor_tensor(score, look[:, :, 0:GH], rows[:, b, :, D:D + GH], ALU.add))
                        V.then(dve.scalar_tensor_tensor(score, score, ALPHA, score, ALU.mult, ALU.max))
                        V.then(dve.tensor_tensor(score, score, look[:, :, GH:], ALU.subtract))
                        dve.tensor_scalar(score, score, LIFT, None, ALU.min).then_inc(score_done, 1)
                        dve.wait_ge(ex_done, j * 2 + (b + 1))
                        for q in range(0, U, HALF_U):
                            msg = rows[:, b, q:q + HALF_U, 0:D].rearrange("p u (h f) -> p u h f", h=GH)
                            ex = rows[:, b, q:q + HALF_U, D:D + GH].unsqueeze(3).to_broadcast([P, HALF_U, GH, GF])
                            dve.tensor_tensor(msg, msg, ex, ALU.mult).then_inc(msg_done, 1)
                        one_hot(j * 2 + (b + 2), j * (2 * U) + (b + 2) * U)
                        tiles = load_tiles(dve, j * (2 * U) + b * U)
                        for u in range(U):
                            add_sums(dve, 1, j, b, u, tiles[u], ACC_W, (4, GNN1_BANKS))
                dve.wait_ge(gnn_add, 2 * NVIS + GNN0_BANKS + GNN1_BANKS)
                with V.loop(LOOPS, 4) as c:
                    got = acc[:, ds(c * (B * ACC_W), B * ACC_W)].rearrange("p (i w) -> p i w", i=B)
                    den = den7.rearrange("p (i h) -> p i h", i=B)
                    V.then(dve.tensor_scalar(den, got[:, :, D:], DEN_MIN, None, ALU.max))
                    V.then(dve.reciprocal(den7, den7))
                    V.then(dve.tensor_tensor(t7.rearrange("p (i h f) -> p i h f", i=B, h=GH),
                                             got[:, :, 0:D].rearrange("p i (h f) -> p i h f", h=GH),
                                             den.unsqueeze(3).to_broadcast([P, B, GH, GF]), ALU.mult))
                    a = xres[:, ds(c * (B * D), B * D)]
                    V.then(dve.tensor_tensor(a, a, t7, ALU.add))

            @block.tensor
            def _(pe):
                pe.wait_ge(rm_done, 1)
                for h in range(GH):
                    last = pe.transpose(bank(3, P, h * P), r_rows[:, h * P:(h + 1) * P], ident)
                last.then_inc(rm_ps, 1)
                pe.wait_ge(lc_done, 1)
                visits_pe(pe, 1, vv)
                pe.sem_inc(gnn_ps, 2 * U)
                pe.wait_ge(edges_ready, 2)
                pe.wait_ge(tiles_ready, 2)

                def flip_hot(g):
                    pe.wait_ge(hots_done, g + 1)
                    for u in range(U):
                        last = pe.transpose(bank(0, P // 2, u * P // 2).bitcast(BF16), hot_b[:, u * P:(u + 1) * P],
                                            ident_b)
                    last.then_inc(hott_ps, 1)

                def look_up(g, first, b):
                    tiles = load_tiles(pe, first)
                    pe.wait_ge(hott_done, g + 1)
                    for u in range(U):
                        last = pe.matmul(bank(2 + b, LW, u * LW), hot_t[:, u * P:(u + 1) * P],
                                         lc_parts[:, ds(tiles[u] * LW, LW)], start=True, stop=True)
                    last.then_inc(look_ps, 1)

                flip_hot(0)
                look_up(0, 0, 0)
                flip_hot(1)
                with pe.Fori(0, GROUP_LOOPS) as j:
                    for b in range(2):
                        look_up(j * 2 + (b + 1), j * (2 * U) + (b + 1) * U, 1 - b)
                        pe.wait_ge(hot_done32, j * 2 + (b + 1))
                        for u in range(U):
                            if u % HALF_U == 0:
                                pe.wait_ge(msg_done, j * 4 + (2 * b + u // HALF_U + 1))
                            if u == HALF_U:
                                flip_hot(j * 2 + (b + 2))
                            n = j * (2 * U) + b * U + u
                            pe.wait_ge(gnn_add, n + (NVIS + GNN0_BANKS + 1))
                            pe.matmul(bank(4 + u % GNN1_BANKS, ACC_W), hot[:, b, u, :], rows[:, b, u, 0:ACC_W],
                                      start=True, stop=True).then_inc(gnn_ps, 1)

        W_E = KD * F1
        assert W_E == FB * D
        TILES_LO = (T + 1) // 2
        HALVES = [(k, t0, t1) for k in range(K1) for t0, t1 in ((0, TILES_LO), (TILES_LO, T))]
        SLOT_PAIRS = SLOT_TILES // 2
        assert SLOT_PAIRS * 2 == SLOT_TILES
        W1_AT, W2_AT = arena_words - 2 * E1 * W_E, arena_words - E1 * W_E
        scratch(GRAPH, W1_AT)
        pos_i, back_i = take(K1 * T).bitcast(I32), take(K1 * T).bitcast(I32)
        top_w = take(K1 * T)
        mix_w = take(T * E1)
        slot_e = take(SLOT_TILES + K1).bitcast(I32)
        b1_t = take(E1 * FB)
        RINGS = place["at"]
        x_in, x_t = [take(D) for _ in range(2)], [take(D) for _ in range(2)]
        w1_ring = [take(W_E) for _ in range(2)]
        h_t = [take(F1) for _ in range(2)]
        y_ring = [take(D) for _ in range(2)]
        scratch(RINGS, W1_AT)
        xs7 = take(B * D)
        slot_idx = take(K1 * B).bitcast(I32)
        scratch(W1_AT)
        w1_all, w2_all = take(E1 * W_E), take(E1 * W_E)
        scratch(W2_AT)
        xn7, xt7 = take(B * D), take(B * D)
        gw, gate_b, b1_raw = take(KD * E1), take(E1), take(P)
        gates, picks, rev = take(T * E1), take(K1 * T * E1), take(E1)
        eq, top_v, first = take(T * E1), take(K1 * T), take(T)
        counts, cum, place_f = take(K1 * T * E1), take(K1 * T * E1), take(K1 * T * E1)
        e_n, e_i, e_tiles, e_cum, e_off = (take(E1) for _ in range(5))
        e_start = take(E1)
        dump, not_node, pos_f = take(K1), take(1), take(K1 * T)
        grid = take((SLOT_TILES + K1) * E1)
        xn7v = xn7.rearrange("p (i k n) -> p i k n", i=B, k=KD)
        xt7v = xt7.rearrange("p (i k n) -> p i k n", i=B, k=KD)
        picks4 = picks.rearrange("p (k t e) -> p k t e", k=K1, e=E1)
        (ld_m, ld_m1, ld_m2, b1_ps, tw_in, tw_exp, picks_done, cnt_ps, pos_done, xs_ready, xs_free) = (
            sem(n) for n in ("ld_m ld_m1 ld_m2 b1_ps tw_in tw_exp picks_done cnt_ps pos_done xs_ready xs_free"
                             ).split())
        moved = gather_done[0]
        MOVED = 2 * GROUP_LOOPS * 16
        CALL3 = 3 * LOOPS

        with nc.Block() as block:
            @block.sync
            def _(sp):
                sp.dma_start(gw.rearrange("p (k e) -> p k e", k=KD),
                             L1_ffn_gate_w.rearrange("(k p) e -> p k e", p=P)).then_inc(ld_m, 16)
                sp.dma_start(gate_b, L1_ffn_gate_b.partition_broadcast(P)).then_inc(ld_m, 16)
                sp.dma_start(b1_raw[0:E1 * FB, :], L1_ffn_b1.rearrange("e (f p) -> (e f) p", p=P)).then_inc(ld_m, 16)
                with sp.Fori(0, E1) as e:
                    sp.dma_start(w1_all[:, ds(e * W_E, W_E)].rearrange("p (k f) -> p k f", k=KD),
                                 L1_ffn_w1[ds(e, 1), :, :].rearrange("o (k p) f -> p (o k) f", p=P)).then_inc(ld_m1, 16)
                sp.wait_ge(pos_done, 1)
                with sp.Fori(0, E1) as e:
                    sp.dma_start(w2_all[:, ds(e * W_E, W_E)].rearrange("p (f d) -> p f d", f=FB),
                                 L1_ffn_w2[ds(e, 1), :, :].rearrange("o (f p) d -> p (o f) d", p=P)).then_inc(ld_m2, 16)
                sp.wait_ge(ld_m1, E1 * 16)
                sp.wait_ge(ld_m2, E1 * 16)

            @block.gpsimd
            def _(pool):
                pool.sem_inc(xs_free, 1)
                pool.wait_ge(pos_done, 1)
                with G.loop(LOOPS, 1) as c:
                    G.then(pool.tensor_copy(slot_idx.rearrange("p (k i) -> p k i", k=K1),
                                            pos_i.rearrange("p (k t) -> p k t", k=K1)[:, :, ds(c * B, B)]))
                    for i in range(B):
                        pool.wait_ge(xs_ready, c * B + (i + 1))
                        pool.sem_inc(dma_turn, 1)
                        for k in range(K1):
                            pool.indirect_dma_start(slot_rows, bass.IndirectOffsetOnAxis(
                                ap=slot_idx[:, k * B + i:k * B + i + 1], axis=0), xs7[:, i * D:(i + 1) * D], None
                            ).then_inc(moved[i], 16)
                    for i in range(B):
                        pool.wait_ge(moved[i], c * (16 * K1) + (MOVED + 16 * K1))
                    pool.sem_inc(xs_free, 1)

            @block.scalar
            def _(act):
                ln_root(act)
                act.wait_ge(b1_ps, 1)
                act.copy(b1_t, bank(7, E1 * FB))
                with act.Fori(0, LOOPS) as c:
                    act.wait_ge(tp_done, c + (CALL3 + 2))
                    act.copy(xt7, psA).then_inc(xt_done, 1)
                act.wait_ge(tw_in, 1)
                act.activation(top_v[:, T:], top_v[:, T:], ACT.Exp).then_inc(tw_exp, 1)

            @block.vector
            def _(dve):
                ln_stats(dve)
                with V.loop(LOOPS, 1) as c:
                    norm7(dve, c, CALL3)
                    dve.wait_ge(lg_ps, c + (LOOPS + 1))
                    V.then(dve.tensor_copy(gates[:, ds(c * (B * E1), B * E1)], bank(4, B * E1)))
                wide = [P, T, E1]
                g3, eq3 = (a.rearrange("p (t e) -> p t e", e=E1) for a in (gates, eq))
                V.then(dve.tensor_scalar(rev, iota[:, 0:E1], -1.0, float(E1), ALU.mult, ALU.add))
                for k in range(K1):
                    best = top_v[:, k * T:(k + 1) * T]
                    V.then(dve.tensor_reduce(best, g3, AX_X, ALU.max))
                    V.then(dve.tensor_tensor(eq3, g3, best.unsqueeze(2).to_broadcast(wide), ALU.is_ge))
                    V.then(dve.tensor_tensor(eq3, eq3, rev.unsqueeze(1).to_broadcast(wide), ALU.mult))
                    V.then(dve.tensor_reduce(first, eq3, AX_X, ALU.max))
                    V.then(dve.tensor_tensor(picks4[:, k], rev.unsqueeze(1).to_broadcast(wide),
                                             first.unsqueeze(2).to_broadcast(wide), ALU.is_equal))
                    if k == 0:
                        V.then(dve.scalar_tensor_tensor(g3, picks4[:, k], -3.0e38, g3, ALU.mult, ALU.add))
                for k in range(K1):
                    V.add(dve.tensor_scalar(picks4[:, k, T - 1, :], picks4[:, k, T - 1, :], rowmask, None, ALU.mult))
                V.settle()
                dve.sem_inc(picks_done, 1)
                dve.tensor_tensor(top_v[:, T:], top_v[:, T:], top_v[:, 0:T], ALU.subtract).then_inc(tw_in, 1)
                dve.wait_ge(tw_exp, 1)
                V.then(dve.tensor_scalar(first, top_v[:, T:], 1.0, None, ALU.add))
                V.then(dve.reciprocal(top_w[:, 0:T], first))
                V.then(dve.tensor_tensor(top_w[:, T:], top_v[:, T:], top_w[:, 0:T], ALU.mult))
                mix3 = mix_w.rearrange("p (t e) -> p t e", e=E1)
                V.add(dve.tensor_tensor(mix3, picks4[:, 0], top_w[:, 0:T].unsqueeze(2).to_broadcast(wide), ALU.mult))
                V.then(dve.tensor_tensor(eq3, picks4[:, 1], top_w[:, T:].unsqueeze(2).to_broadcast(wide), ALU.mult))
                V.add(dve.tensor_tensor(mix3, mix3, eq3, ALU.add))
                dve.wait_ge(cnt_ps, 1)
                by_e = [a.rearrange("p (e k t) -> p k t e", e=E1, k=K1) for a in (counts, cum)]
                for n, (k, t0, t1) in enumerate(HALVES):
                    V.add(dve.tensor_copy(by_e[0][:, k, t0:t1, :],
                                          bank(4 + n, (t1 - t0) * E1).rearrange("p (t e) -> p t e", e=E1)))
                V.settle()
                V.then(dve.tensor_tensor_scan(cum, counts, counts, 0.0, ALU.add, ALU.bypass))
                ends = cum.rearrange("p (e m) -> p e m", e=E1)
                V.then(dve.tensor_copy(e_n, ends[:, :, K1 * T - 1]))
                V.then(dve.tensor_tensor(cum, cum, counts, ALU.subtract))
                V.then(dve.tensor_copy(e_start, ends[:, :, 0]))
                V.then(dve.tensor_tensor(e_n, e_n, e_start, ALU.subtract))
                V.then(dve.tensor_scalar(e_n, e_n, float(P - 1), None, ALU.add))
                V.then(dve.tensor_copy(e_i.bitcast(I32), e_n))
                V.then(dve.tensor_scalar(e_off.bitcast(I32), e_i.bitcast(I32), 7, None, ALU.arith_shift_right))
                V.then(dve.tensor_copy(e_tiles, e_off.bitcast(I32)))
                V.then(dve.tensor_tensor_scan(e_cum, e_tiles, e_tiles, 0.0, ALU.add, ALU.bypass))
                V.then(dve.tensor_tensor(e_off, e_cum, e_tiles, ALU.subtract))
                V.then(dve.scalar_tensor_tensor(e_off, e_off, float(P), e_start, ALU.mult, ALU.subtract))
                V.then(dve.tensor_tensor(ends, ends, e_off.unsqueeze(2).to_broadcast([P, E1, K1 * T]), ALU.add))
                place4 = place_f.rearrange("p (k t e) -> p k t e", k=K1, e=E1)
                for n, (k, t0, t1) in enumerate(HALVES):
                    V.add(dve.tensor_tensor(place4[:, k, t0:t1, :], by_e[1][:, k, t0:t1, :],
                                            bank(n, (t1 - t0) * E1).rearrange("p (t e) -> p t e", e=E1), ALU.add))
                V.settle()
                V.then(dve.tensor_tensor(place_f, place_f, picks, ALU.mult))
                V.then(dve.tensor_reduce(pos_f, place_f.rearrange("p (m e) -> p m e", e=E1), AX_X, ALU.add))
                V.add(dve.tensor_scalar(not_node, rowmask, -1.0, 1.0, ALU.mult, ALU.add))
                for k in range(K1):
                    V.add(dve.tensor_scalar(dump[:, k:k + 1], lane, float(SLOTS + k * P), None, ALU.add))
                V.settle()
                for k in range(K1):
                    at = pos_f[:, k * T + T - 1:k * T + T]
                    V.add(dve.scalar_tensor_tensor(at, dump[:, k:k + 1], not_node, at, ALU.mult, ALU.add))
                V.settle()
                V.then(dve.tensor_copy(pos_i, pos_f))
                V.then(dve.tensor_scalar(pos_f, pos_f, float(SLOTS - 1), None, ALU.min))
                V.add(dve.tensor_copy(back_i, pos_f))
                tiles = [P, SLOT_TILES + K1, E1]
                grid3 = grid.rearrange("p (s e) -> p s e", e=E1)
                V.then(dve.tensor_tensor(grid3, iota[:, 0:SLOT_TILES + K1].unsqueeze(2).to_broadcast(tiles),
                                         e_cum.unsqueeze(1).to_broadcast(tiles), ALU.is_ge))
                V.then(dve.tensor_reduce(cum[:, 0:SLOT_TILES + K1], grid3, AX_X, ALU.add))
                V.then(dve.tensor_scalar(cum[:, 0:SLOT_TILES + K1], cum[:, 0:SLOT_TILES + K1], float(E1 - 1), None,
                                         ALU.min))
                V.then(dve.tensor_copy(slot_e, cum[:, 0:SLOT_TILES + K1]))
                dve.sem_inc(pos_done, 1)
                with dve.Fori(0, LOOPS) as c:
                    dve.wait_ge(xs_free, c + 1)
                    for i in range(B):
                        normalise(dve, xs7[:, i * D:(i + 1) * D], c * B + i).then_inc(xs_ready, 1)

            @block.tensor
            def _(pe):
                pe.wait_ge(ld_m, 48)
                pe.transpose(bank(7, E1 * FB), b1_raw[0:E1 * FB, :], ident[0:E1 * FB, 0:E1 * FB]).then_inc(b1_ps, 1)
                with pe.Fori(0, LOOPS) as c:
                    transpose7(pe, c, CALL3)
                    pe.wait_ge(xt_done, c + (2 * CALL3 + 1))
                    for i in range(B):
                        to = bank(4, E1, i * E1)
                        for k in range(KD):
                            pe.matmul(to, xt7v[:, i, k, :], gw[:, k * E1:(k + 1) * E1], start=(k == 0), stop=False)
                        last = pe.matmul(to, ones[0:1, :], gate_b[0:1, :], start=False, stop=True)
                    last.then_inc(lg_ps, 1)
                pe.wait_ge(picks_done, 1)
                for at, m in ((0, tri), (4, ones)):
                    for n, (k, t0, t1) in enumerate(HALVES):
                        last = pe.matmul(bank(at + n, (t1 - t0) * E1), m,
                                         picks4[:, k, t0:t1, :].rearrange("p t e -> p (t e)"), start=True, stop=True)
                last.then_inc(cnt_ps, 1)

        (in_ps, in_done, m1h_ps, h_done, w1_done, m2h_ps, y_done, y_free) = (
            sem(n) for n in "in_ps in_done m1h_ps h_done w1_done m2h_ps y_done y_free".split())
        x_ld = [sem(f"x_ld{b}") for b in range(2)]

        with nc.Block() as block:
            @block.sync
            def _(sp):
                sp.sem_inc(y_free, 32)
                sp.dma_start(x_in[0], slot_rows[0:P, :]).then_inc(x_ld[0], 16)
                with sp.Fori(0, SLOT_PAIRS) as j:
                    for b in range(2):
                        s = j * 2 + b
                        sp.wait_ge(in_ps, s + 1)
                        sp.dma_start(x_in[1 - b], slot_rows[ds((s + 1) * P, P), :]).then_inc(x_ld[1 - b], 16)
                        sp.wait_ge(y_done, s + 3)
                        sp.dma_start(slot_out[ds(s * P, P), :], y_ring[b]).then_inc(y_free, 16)
                sp.wait_ge(y_free, SLOT_TILES * 16 + 32)
                sp.wait_ge(x_ld[0], SLOT_PAIRS * 16 + 16)

            @block.scalar
            def _(act):
                def expert(s):
                    return act.value_load(slot_e[0:1, ds(s, 1)], min_val=0, max_val=E1 - 1)

                def take_w1(s, b):
                    act.copy(w1_ring[b], w1_all[:, ds(expert(s) * W_E, W_E)]).then_inc(w1_done, 1)

                take_w1(0, 0)
                with act.Fori(0, SLOT_PAIRS) as j:
                    for b in range(2):
                        s = j * 2 + b
                        e = expert(s)
                        for f in range(FB):
                            act.wait_ge(m1h_ps, s * 2 + (f // 2 + 1))
                            act.activation(h_t[b][:, f * P:(f + 1) * P], bank(2 + 2 * b + f // 2, P, f % 2 * P), ACT.Relu,
                                           bias=b1_t[:, ds(e * FB + f, 1)]).then_inc(h_done, 1)
                        take_w1(s + 1, 1 - b)

            @block.vector
            def _(dve):
                def take_in(s, b):
                    dve.wait_ge(in_ps, s + 1)
                    dve.tensor_copy(x_t[b], bank(b, D)).then_inc(in_done, 1)

                dve.sem_inc(y_done, 2)
                take_in(0, 0)
                with dve.Fori(0, SLOT_PAIRS) as j:
                    for b in range(2):
                        s = j * 2 + b
                        take_in(s + 1, 1 - b)
                        dve.wait_ge(m2h_ps, s + 1)
                        dve.wait_ge(y_free, s * 16 + 16)
                        dve.tensor_copy(y_ring[b], bank(6 + b, D)).then_inc(y_done, 1)

            @block.tensor
            def _(pe):
                def flip(b, nth):
                    pe.wait_ge(x_ld[b], nth * 16 + 16)
                    for k in range(KD):
                        last = pe.transpose(bank(b, P, k * P), x_in[b][:, k * P:(k + 1) * P], ident)
                    last.then_inc(in_ps, 1)

                flip(0, 0)
                with pe.Fori(0, SLOT_PAIRS) as j:
                    for b in range(2):
                        s = j * 2 + b
                        e = pe.value_load(slot_e[0:1, ds(s, 1)], min_val=0, max_val=E1 - 1)
                        pe.wait_ge(in_done, s + 1)
                        pe.wait_ge(w1_done, s + 1)
                        for f in range(FB):
                            for k in range(KD):
                                last = pe.matmul(bank(2 + 2 * b + f // 2, P, f % 2 * P),
                                                 w1_ring[b][:, k * F1 + f * P:k * F1 + (f + 1) * P],
                                                 x_t[b][:, k * P:(k + 1) * P], start=(k == 0), stop=(k == KD - 1))
                            if f % 2:
                                last.then_inc(m1h_ps, 1)
                        flip(1 - b, j + b)
                        pe.wait_ge(y_done, s + 1)
                        for f in range(FB):
                            pe.wait_ge(h_done, s * FB + (f + 1))
                            last = pe.matmul(bank(6 + b, D), h_t[b][:, f * P:(f + 1) * P],
                                             w2_all[:, ds(e * W_E + f * D, D)], start=(f == 0), stop=(f == FB - 1))
                        last.then_inc(m2h_ps, 1)

        scratch(RINGS)
        got_k = [[take(D) for _ in range(B)] for _ in range(K1)]
        back_idx = take(K1 * B).bitcast(I32)
        y7, t7 = take(B * D), take(B * D)
        mix7, mix_t = take(B * E1), take(B * P)
        b2_s, gamma_b, beta_b = take(D), take(D), take(D)
        y_all = take(T * D)
        (ld_o, back_free, mix_in, mixt_ps, mixt_done, b2_ps, y_sum, out_done, out_st) = (
            sem(n) for n in "ld_o back_free mix_in mixt_ps mixt_done b2_ps y_sum out_done out_st".split())

        with nc.Block() as block:
            @block.sync
            def _(sp):
                sp.dma_start(b2_s[0:E1, :], L1_ffn_b2).then_inc(ld_o, 16)
                sp.dma_start(gamma_b, L1_ffn_gamma.partition_broadcast(P)).then_inc(ld_o, 16)
                sp.dma_start(beta_b, L1_ffn_beta.partition_broadcast(P)).then_inc(ld_o, 16)

                def store(c, tiles):
                    sp.dma_start(out[ds(c * (B * P), tiles * P), :].rearrange("(i p) d -> p i d", p=P),
                                 xres[:, ds(c * (B * D), tiles * D)].rearrange("p (i d) -> p i d", d=D)
                                 ).then_inc(out_st, 16)

                with sp.Fori(0, LOOPS - 1) as c:
                    sp.wait_ge(out_done, c + 2)
                    store(c, B)
                sp.wait_ge(out_done, LOOPS + 1)
                store(LOOPS - 1, B - 1)
                sp.dma_start(out[(T - 1) * P:, :], xres[0:TAIL, (T - 1) * D:]).then_inc(out_st, 16)
                sp.wait_ge(out_st, (LOOPS + 1) * 16)

            @block.gpsimd
            def _(pool):
                with G.loop(LOOPS, 1) as c:
                    pool.wait_ge(back_free, c + 1)
                    G.then(pool.tensor_copy(back_idx.rearrange("p (k i) -> p k i", k=K1),
                                            back_i.rearrange("p (k t) -> p k t", k=K1)[:, :, ds(c * B, B)]))
                    pool.sem_inc(dma_turn, 1)
                    for i in range(B):
                        for k in range(K1):
                            pool.indirect_dma_start(got_k[k][i], None, slot_out, bass.IndirectOffsetOnAxis(
                                ap=back_idx[:, k * B + i:k * B + i + 1], axis=0)).then_inc(moved[i], 16)

            @block.scalar
            def _(act):
                with act.Fori(0, LOOPS) as c:
                    act.wait_ge(mixt_ps, c + 1)
                    act.copy(mix_t[0:E1, :], ps[0:E1, 0:B * P]).then_inc(mixt_done, 1)
                ln_root(act)

            @block.vector
            def _(dve):
                dve.sem_inc(back_free, 1)
                with V.loop(LOOPS, B + 1) as c:
                    dve.tensor_copy(mix7, mix_w[:, ds(c * (B * E1), B * E1)]).then_inc(mix_in, 1)
                    for i in range(B):
                        V.add(normalise(dve, y7[:, i * D:(i + 1) * D], c * B + i))
                    V.settle()
                    dve.wait_ge(b2_ps, c + 1)
                    V.then(dve.tensor_tensor(y7, y7, psB, ALU.add))
                    for i in range(B):
                        y = y7[:, i * D:(i + 1) * D]
                        dve.wait_ge(moved[i], c * (16 * K1) + (MOVED + (LOOPS + 1) * 16 * K1))
                        dve.scalar_tensor_tensor(y, got_k[0][i], top_w[:, ds(c * B + i, 1)], y, ALU.mult, ALU.add
                                                 ).then_inc(y_sum, 1)
                    for i in range(B):
                        y = y7[:, i * D:(i + 1) * D]
                        dve.wait_ge(y_sum, c * (2 * B) + B)
                        dve.scalar_tensor_tensor(y_all[:, ds((c * B + i) * D, D)], got_k[1][i],
                                                 top_w[:, ds(c * B + (T + i), 1)], y, ALU.mult, ALU.add
                                                 ).then_inc(y_sum, 1)
                    dve.wait_ge(y_sum, c * (2 * B) + 2 * B)
                    dve.sem_inc(back_free, 1)
                ln_stats(dve, y_all)
                dve.wait_ge(ld_o, 48)
                dve.sem_inc(out_done, 1)
                with V.loop(LOOPS, B + 2) as c:
                    dve.wait_ge(out_done, c + 1)
                    for i in range(B):
                        V.add(normalise(dve, t7[:, i * D:(i + 1) * D], c * B + i, y_all))
                    V.settle()
                    t = t7.rearrange("p (i d) -> p i d", i=B)
                    V.then(dve.tensor_tensor(t, t, gamma_b.unsqueeze(1).to_broadcast([P, B, D]), ALU.mult))
                    V.then(dve.tensor_tensor(t, t, beta_b.unsqueeze(1).to_broadcast([P, B, D]), ALU.add))
                    a = xres[:, ds(c * (B * D), B * D)]
                    dve.tensor_tensor(a, a, t7, ALU.add).then_inc(out_done, 1)

            @block.tensor
            def _(pe):
                pe.wait_ge(ld_o, 48)
                with pe.Fori(0, LOOPS) as c:
                    pe.wait_ge(mix_in, c + 1)
                    for i in range(B):
                        last = pe.transpose(ps[0:E1, i * P:(i + 1) * P], mix7[:, i * E1:(i + 1) * E1], ident)
                    last.then_inc(mixt_ps, 1)
                    pe.wait_ge(mixt_done, c + 1)
                    pe.wait_ge(back_free, c + 1)
                    for i in range(B):
                        last = pe.matmul(half(4, i), mix_t[0:E1, i * P:(i + 1) * P], b2_s[0:E1, :],
                                         start=True, stop=True)
                    last.then_inc(b2_ps, 1)


_INS = ['x', 'src', 'dst', 'edge_weight', 'L0_gnn_W', 'L0_gnn_b', 'L0_mix_Wq', 'L0_mix_Wkv', 'L0_mix_Wproj',
        'L0_mix_bproj', 'L0_ffn_router_w', 'L0_ffn_router_b', 'L0_ffn_W1', 'L0_ffn_b1', 'L0_ffn_W2', 'L0_ffn_b2',
        'L1_gnn_W', 'L1_gnn_a_l', 'L1_gnn_a_r', 'L1_mix_kln_weight', 'L1_mix_kln_bias', 'L1_mix_vln_weight',
        'L1_mix_vln_bias', 'L1_ffn_gate_w', 'L1_ffn_gate_b', 'L1_ffn_w1', 'L1_ffn_b1', 'L1_ffn_w2', 'L1_ffn_b2',
        'L1_ffn_gamma', 'L1_ffn_beta']


def kernel(**inputs):
    import numpy as _np
    import concourse.bacc as _bacc
    from concourse import mybir as _mybir
    from concourse.bass_utils import run_bass_kernel_spmd as _run

    nc = _bacc.Bacc("TRN2", target_bir_lowering=False, num_devices=1)
    arrays, args = {}, []
    for name in _INS:
        a = _np.ascontiguousarray(inputs[name])
        arrays[f"in_{name}"] = a
        args.append(nc.dram_tensor(f"in_{name}", a.shape, _mybir.dt.from_np(a.dtype), kind="ExternalInput").ap())
    out = nc.dram_tensor("out_x", (NODES, D), F32, kind="ExternalOutput").ap()
    gps_two_layers(nc, *args, out)
    r = _run(nc, [arrays], core_ids=[0])
    return r.results[0]["out_x"]
```

```python
from contextlib import ExitStack, contextmanager

import concourse.bass as bass
from concourse import mybir

F32 = mybir.dt.float32
I32 = mybir.dt.int32
U32 = mybir.dt.uint32
BF16 = mybir.dt.bfloat16
ALU = mybir.AluOpType
ACT = mybir.ActivationFunctionType
AX_X = mybir.AxisListType.X
RMAX = bass.bass_isa.ReduceOp.max
ds = bass.ds

P = 128
NODES, D, EDGES = 6250, 256, 100000
T = -(-NODES // P)
NP = T * P
TAIL = NODES - (T - 1) * P
B = 7
LOOPS = T // B
assert LOOPS * B == T
KD = D // P
C = -(-EDGES // P)
EP = C * P
BUCKETS = T + 1
SCAT = 17
SCAT_LOOPS = C // (2 * SCAT)
assert SCAT_LOOPS * 2 * SCAT == C
U = 8
HALF_U = U // 2
GROUP_LOOPS = -(-(C + T - 1) // (2 * U))
R = 4
RINGS_OF_R = GROUP_LOOPS * 2 // R
assert RINGS_OF_R * R == GROUP_LOOPS * 2
VT = -(-(GROUP_LOOPS * 2 * U) // P)
NV = VT * P
HC = 32
GH, GF = 4, 64
ROW1 = D + 2 * GH
ACC_W = D + GH
E0, H0 = 32, 64
HB = E0 * H0 // P
HALF = B * P // 2
E1, F1, K1 = 16, 512, 2
FB = F1 // P
SLOT_TILES = K1 * T + E1
SLOTS = SLOT_TILES * P
SPARE = K1 + 1
COUNTS = -(-BUCKETS // LOOPS)
LN_EPS, KV_EPS, D_MIN = 1e-5, 1e-5, 1e-6
ALPHA = 0.2
LIFT = 60.0
OTHER = 4096.0
DEN_MIN = 1e-30
PARTS = 3


class Steps:

    def __init__(self, engine, sem):
        self.engine, self.sem, self.n, self.i, self.per = engine, sem, 0, None, 0

    def add(self, ins):
        ins.then_inc(self.sem, 1)
        self.n += 1

    def settle(self):
        self.engine.wait_ge(self.sem, self.n if self.i is None else self.n + self.i * self.per)

    def then(self, ins):
        self.add(ins)
        self.settle()

    @contextmanager
    def loop(self, count, per):
        first = self.n
        with self.engine.Fori(0, count) as i:
            self.i, self.per = i, per
            yield i
            assert self.n - first == per, (self.n - first, per)
        self.i, self.n = None, first + per * count


def gps_two_layers(nc, x, src, dst, edge_weight, L0_gnn_W, L0_gnn_b, L0_mix_Wq, L0_mix_Wkv, L0_mix_Wproj,
                   L0_mix_bproj, L0_ffn_router_w, L0_ffn_router_b, L0_ffn_W1, L0_ffn_b1, L0_ffn_W2, L0_ffn_b2,
                   L1_gnn_W, L1_gnn_a_l, L1_gnn_a_r, L1_mix_kln_weight, L1_mix_kln_bias, L1_mix_vln_weight,
                   L1_mix_vln_bias, L1_ffn_gate_w, L1_ffn_gate_b, L1_ffn_w1, L1_ffn_b1, L1_ffn_w2, L1_ffn_b2,
                   L1_ffn_gamma, L1_ffn_beta, out):
    with ExitStack() as ctx:
        def sem(name):
            return ctx.enter_context(nc.semaphore(name))

        def dram(name, shape, dt=F32):
            return nc.dram_tensor(name, shape, dt, kind="Internal").ap()

        h0_table = dram("h0_table", (NP, D))
        h1_table = dram("h1_table", (NP, ROW1))
        edges_by = [dram("edges_by_dst", (EP, 4)), dram("edges_by_src", (EP, 4))]
        visit_tiles = dram("visit_tiles", (2, NV), I32)
        slot_rows = dram("slot_rows", (SLOTS + SPARE * P, D))
        slot_out = dram("slot_out", (SLOTS, D))

        arena_words = 53200
        arena = ctx.enter_context(nc.sbuf_tensor("arena", [P, arena_words], F32))
        place = {"at": 0}

        def take(words):
            at = place["at"]
            place["at"] = at + words
            assert place["at"] <= place.get("end", arena_words), place
            return arena[:, at:at + words]

        def scratch(at, end=arena_words):
            place["at"], place["end"] = at, end

        xres = take(T * D)
        ident, tri, ones, iota = take(P), take(P), take(P), take(P)
        zeros = take(P)
        blk = take(P)
        lane, rowmask = take(1), take(1)
        stats, mean, rstd, lnt = take(6 * T), take(T), take(T), take(4 * T)
        tot_all, base_all = take(COUNTS * LOOPS), take(GROUP_LOOPS)
        tot = tot_all[:, 0:BUCKETS]
        base = base_all[:, 0:BUCKETS]
        unsorted_f, unsorted = take(2), take(1).bitcast(I32)
        cnt = [take(2 * BUCKETS), take(2 * BUCKETS)]
        GRAPH = place["at"]
        rl_all = take(BUCKETS * 2 * GH)
        v_loc, v_w = take(NV), take(NV)
        v_idx = take(NV).bitcast(I32)
        tile_row = take(NV).bitcast(I32)
        XNT = place["at"]
        xnT = take(KD * NP)
        ACC = place["at"]
        acc = take(BUCKETS * ACC_W)
        src_f, dst_f, pos_src = take(C), take(C), take(C)
        w_f, pos_dst = take(C), take(C)
        FREE = place["at"]
        xnT3 = xnT.rearrange("p (k n) -> p k n", k=KD)
        acc3 = acc.rearrange("p (t w) -> p t w", w=ACC_W)

        ps = ctx.enter_context(nc.psum_tensor("ps", [P, 8 * 512], F32))

        def bank(b, width=512, at=0):
            return ps[:, b * 512 + at:b * 512 + at + width]

        def half(b, i, width=D):
            return ps[:, b * 512 + i * 256:b * 512 + i * 256 + width]

        V, G = Steps(nc.vector, sem("dve_step")), Steps(nc.gpsimd, sem("pool_step"))
        V_SORT, G_SORT = Steps(nc.vector, sem("dve_sort_step")), Steps(nc.gpsimd, sem("pool_sort_step"))

        var_ready, std_ready = sem("var_ready"), sem("std_ready")
        calls = {"ln_dve": 0, "ln_act": 0}

        def ln_stats(dve):
            with V.loop(T, 1) as t:
                V.add(dve.bn_stats(stats[:, ds(t * 6, 6)], xres[:, ds(t * D, D)]))
            V.settle()
            ln_roots(dve, T, mean, rstd, calls["ln_dve"] + 1)
            calls["ln_dve"] += 1

        def ln_roots(dve, tiles, mean, rstd, nth):
            s = stats[:, 0:6 * tiles].rearrange("p (t s) -> p t s", s=6)
            a, b, c, d = (lnt[:, i * T:i * T + tiles] for i in range(4))
            V.add(dve.tensor_tensor(a, s[:, :, 1], s[:, :, 4], ALU.add))
            V.add(dve.tensor_tensor(b, s[:, :, 1], s[:, :, 4], ALU.subtract))
            V.then(dve.tensor_tensor(c, s[:, :, 2], s[:, :, 5], ALU.add))
            V.add(dve.tensor_scalar(mean, a, 0.5, None, ALU.mult))
            V.then(dve.tensor_tensor(d, b, b, ALU.mult))
            V.then(dve.scalar_tensor_tensor(b, d, D / 4, c, ALU.mult, ALU.add))
            dve.tensor_scalar(a, b, 1.0 / D, LN_EPS, ALU.mult, ALU.add).then_inc(var_ready, 1)
            dve.wait_ge(std_ready, nth)
            V.then(dve.reciprocal(c, b))
            V.then(dve.tensor_tensor(d, c, c, ALU.mult))
            V.then(dve.tensor_tensor(b, d, a, ALU.mult))
            V.then(dve.tensor_scalar(d, b, -0.5, 1.5, ALU.mult, ALU.add))
            V.then(dve.tensor_tensor(rstd, d, c, ALU.mult))

        def ln_root(act):
            calls["ln_act"] += 1
            root(act, T, calls["ln_act"])

        def root(act, tiles, nth):
            act.wait_ge(var_ready, nth)
            act.activation(lnt[:, T:T + tiles], lnt[:, 0:tiles], ACT.Sqrt).then_inc(std_ready, 1)

        def normalise(dve, to, t):
            return dve.tensor_scalar(to, xres[:, ds(t * D, D)], mean[:, ds(t, 1)], rstd[:, ds(t, 1)],
                                     ALU.subtract, ALU.mult)

        tot_ready, base_ps = sem("tot_ready"), sem("base_ps")

        def rank_keys(dve, keys, temps):
            key_t, eq = temps[0:2]
            V.then(dve.tensor_copy(key_t.bitcast(I32), keys))
            V.then(dve.tensor_scalar(eq.bitcast(I32), key_t.bitcast(I32), 7, None, ALU.arith_shift_right))
            V.then(dve.tensor_copy(key_t, eq.bitcast(I32)))

        def rank_count(dve, b, temps):
            key_t, eq = temps[0:2]
            V.then(dve.tensor_scalar(eq, key_t, iota[:, ds(b, 1)], None, ALU.is_equal))
            V.then(dve.tensor_reduce(tot_all[:, ds(b, 1)], eq, AX_X, ALU.add))

        def rank_bases(dve, call, pos):
            dve.memset(pos, 0.0).then_inc(tot_ready, 1)
            dve.wait_ge(base_ps, call + 1)
            count, cum = cnt[call][:, 0:BUCKETS], cnt[call][:, BUCKETS:]
            V.then(dve.tensor_copy(count, bank(7, BUCKETS, 64)))
            V.then(dve.tensor_tensor_scan(cum, count, count, 0.0, ALU.add, ALU.bypass))
            V.then(dve.tensor_tensor(base, cum, count, ALU.subtract))
            V.then(dve.scalar_tensor_tensor(base, base, -1.0, bank(7, BUCKETS), ALU.add, ALU.add))

        def rank_step(dve, steps, b, step, pos, temps):
            key_t, eq, scan, part = temps
            if step == 0:
                steps.then(dve.tensor_scalar(eq, key_t, iota[:, ds(b, 1)], None, ALU.is_equal))
            elif step == 1:
                steps.then(dve.tensor_tensor_scan(scan, eq, eq, 0.0, ALU.add, ALU.bypass))
            elif step == 2:
                steps.then(dve.scalar_tensor_tensor(part, scan, base_all[:, ds(b, 1)], eq, ALU.add, ALU.mult))
            else:
                steps.then(dve.tensor_tensor(pos, pos, part, ALU.add))

        def rank_sums(pe, call):
            pe.wait_ge(tot_ready, call + 1)
            pe.matmul(bank(7, BUCKETS), tri, tot, start=True, stop=True)
            pe.matmul(bank(7, BUCKETS, 64), ones, tot, start=True, stop=True).then_inc(base_ps, 1)

        scat_done = [[sem(f"scat{c}_done{b}") for b in range(2)] for c in range(2)]
        dma_turn = sem("dma_turn")

        def scatter(pool, G, call, pos, fields, ring):
            offs = ring[:, 0:2 * SCAT].bitcast(I32).rearrange("p (b s) -> p b s", b=2)
            load = ring[:, 2 * SCAT:10 * SCAT].rearrange("p (b s f) -> p b s f", b=2, s=SCAT)
            G.then(pool.memset(ring[:, 2 * SCAT:10 * SCAT], 0.0))

            def fill(b, first):
                G.add(pool.tensor_copy(offs[:, b, :], pos[:, ds(first, SCAT)]))
                for f, field in enumerate(fields):
                    G.add(pool.tensor_copy(load[:, b, :, f], field[:, ds(first, SCAT)]))
                G.settle()

            def send(b):
                pool.sem_inc(dma_turn, 1)
                for s in range(SCAT):
                    pool.indirect_dma_start(edges_by[call], bass.IndirectOffsetOnAxis(ap=offs[:, b, s:s + 1], axis=0),
                                            load[:, b, s, :], None).then_inc(scat_done[call][b], 16)

            per = 1 + len(fields)
            for b in range(2):
                fill(b, b * SCAT)
                send(b)
            with G.loop(SCAT_LOOPS - 1, 2 * per) as j:
                for b in range(2):
                    pool.wait_ge(scat_done[call][b], (j + 1) * (16 * SCAT))
                    fill(b, (j + 1) * (2 * SCAT) + b * SCAT)
                    send(b)
            for b in range(2):
                pool.wait_ge(scat_done[call][b], SCAT_LOOPS * 16 * SCAT)

        vis_done, vis_rows, vis_cols, vis_ps, vis_tile, vis_out, vis_back = (sem(n) for n in (
            "vis_done", "vis_rows", "vis_cols", "vis_ps", "vis_tile", "vis_out", "vis_back"))

        def visit_views():
            v = {n: take(w) for n, w in (("grid", VT * T), ("tmp", 8 * T), ("vid", VT), ("tile", VT),
                                         ("chunk", VT), ("rows", VT * 4 * P), ("cols", VT * 3 * P))}
            v.update({n: take(VT).bitcast(I32) for n in ("chunk_i", "tile_i", "vid_i")})
            return v

        def visits_dve(dve, call, v):
            count, cum = cnt[call][:, 0:T], cnt[call][:, BUCKETS:BUCKETS + T]
            t = [v["tmp"][:, i * T:(i + 1) * T] for i in range(8)]
            ti = [a.bitcast(I32) for a in t]
            V.add(dve.tensor_tensor(t[0], cum, count, ALU.subtract))
            V.then(dve.tensor_scalar(t[1], cum, float(P - 1), None, ALU.add))
            V.add(dve.tensor_copy(ti[2], t[0]))
            V.then(dve.tensor_copy(ti[3], t[1]))
            V.add(dve.tensor_scalar(ti[4], ti[2], 7, None, ALU.arith_shift_right))
            V.then(dve.tensor_scalar(ti[5], ti[3], 7, None, ALU.arith_shift_right))
            V.add(dve.tensor_copy(t[0], ti[4]))
            V.then(dve.tensor_copy(t[1], ti[5]))
            V.add(dve.tensor_scalar(t[2], count, 0.0, None, ALU.is_gt))
            V.then(dve.tensor_tensor(t[3], t[1], t[0], ALU.subtract))
            V.then(dve.tensor_tensor(t[3], t[3], t[2], ALU.mult))
            V.then(dve.tensor_tensor_scan(t[4], t[3], t[3], 0.0, ALU.add, ALU.bypass))
            V.then(dve.tensor_tensor(t[5], t[4], t[3], ALU.subtract))
            V.add(dve.memset(t[7], 0.0))
            V.then(dve.tensor_tensor(t[6], t[0], t[5], ALU.subtract))
            V.add(dve.tensor_tensor(t[7][:, 0:T - 1], t[6][:, 1:T], t[6][:, 0:T - 1], ALU.subtract))
            dve.wait_ge(vis_back, call + 1)
            V.then(dve.tensor_copy(v["vid"], v["vid_i"]))
            grid = v["grid"].rearrange("p (v t) -> p v t", t=T)
            V.then(dve.tensor_tensor(grid, v["vid"].unsqueeze(2).to_broadcast([P, VT, T]),
                                     t[4].unsqueeze(1).to_broadcast([P, VT, T]), ALU.is_ge))
            V.then(dve.tensor_reduce(v["tile"], grid, AX_X, ALU.add))
            V.then(dve.tensor_tensor(grid, grid, t[7].unsqueeze(1).to_broadcast([P, VT, T]), ALU.mult))
            V.then(dve.tensor_reduce(v["chunk"], grid, AX_X, ALU.add))
            V.then(dve.tensor_tensor(v["chunk"], v["chunk"], v["vid"], ALU.add))
            V.then(dve.tensor_scalar(v["chunk"], v["chunk"], t[6][:, 0:1], float(C - 1), ALU.add, ALU.min))
            dve.tensor_copy(v["tile_i"], v["tile"]).then_inc(vis_tile, 1)
            dve.tensor_copy(v["chunk_i"], v["chunk"]).then_inc(vis_done, 1)
            V.then(dve.tensor_scalar(v["tile"], v["tile"], float(P), None, ALU.mult))
            dve.wait_ge(vis_rows, (call + 1) * VT * 16)
            cols = v["cols"].rearrange("p (v f e) -> p v f e", v=VT, f=3)
            got = v["rows"].rearrange("p (v e f) -> p v f e", v=VT, f=4)
            for j in range(VT):
                dve.tensor_copy(cols[:, j, 0:3:2, :], got[:, j, 0:3:2, :]).then_inc(vis_cols, 1)
                dve.tensor_scalar(cols[:, j, 1, :], got[:, j, 1, :], v["tile"][:, j:j + 1], None,
                                  ALU.subtract).then_inc(vis_cols, 1)
            for j in range(VT):
                dve.wait_ge(vis_ps, call * VT + j + 1)
                got = bank(j, 3 * P)
                V.add(dve.tensor_scalar(v_idx[:, j * P:(j + 1) * P], got[:, 0:P], float(NP - 1), None, ALU.min))
                V.add(dve.tensor_copy(v_loc[:, j * P:(j + 1) * P], got[:, P:2 * P]))
                V.add(dve.tensor_copy(v_w[:, j * P:(j + 1) * P], got[:, 2 * P:]))

        def visits_pool(pool, call, v):
            pool.iota(v["vid_i"], [[P, VT]], base=0, channel_multiplier=1).then_inc(vis_back, 1)
            pool.wait_ge(vis_done, call + 1)
            table = edges_by[call].rearrange("(c e) f -> c (e f)", e=P)
            for j in range(VT):
                pool.indirect_dma_start(v["rows"][:, j * 4 * P:(j + 1) * 4 * P], None, table,
                                        bass.IndirectOffsetOnAxis(ap=v["chunk_i"][:, j:j + 1], axis=0)
                                        ).then_inc(vis_rows, 16)

        def visits_pe(pe, call, v):
            cols = v["cols"].rearrange("p (v f e) -> p v f e", v=VT, f=3)
            for j in range(VT):
                pe.wait_ge(vis_cols, (call * VT + j + 1) * 2)
                for f in range(3):
                    last = pe.transpose(bank(j, P, f * P), cols[:, j, f, :], ident)
                last.then_inc(vis_ps, 1)

        def visits_sync(sp, call, v):
            sp.wait_ge(vis_tile, call + 1)
            sp.dma_start(visit_tiles[call].rearrange("(v p) -> p v", p=P), v["tile_i"],
                         allow_slow_non_contiguous=True).then_inc(vis_out, 16)
            sp.wait_ge(vis_out, 16 * (2 * call + 1))
            sp.dma_start(tile_row[0:1, :], visit_tiles[call].rearrange("(o v) -> o v", o=1)).then_inc(vis_out, 16)
            sp.wait_ge(vis_out, 16 * (2 * call + 2))

        z_x, z_e, ld_x, ld_e, kc, zero_done, z_slots = (sem(n) for n in "z_x z_e ld_x ld_e kc zero_done z_slots".split())
        scratch(FREE)
        temps = [take(C) for _ in range(4)]
        iota_i, lane_i, shift_i, shift_f = (take(n) for n in (P, 1, P + 1, P + 1))
        scratch(ACC, FREE)
        inter = take(4 * C)
        inter_done, edges_out, sort_in, sort_ps, unsorted_done, ranked = (
            sem(n) for n in "inter_done edges_out sort_in sort_ps unsorted_done ranked".split())
        iota_i, lane_i, shift_i = (a.bitcast(I32) for a in (iota_i, lane_i, shift_i))

        def load_edges(sp, to, a):
            full, at = EDGES // C, 0
            for n in (full // 16 * 16, full % 16):
                sp.dma_start(to[at:at + n, :], a[at * C:(at + n) * C].rearrange("(p c) -> p c", c=C)).then_inc(ld_e, 16)
                at += n
            sp.dma_start(to[full:full + 1, 0:EDGES - full * C],
                         a[full * C:EDGES].rearrange("(o c) -> o c", o=1)).then_inc(ld_e, 16)

        with nc.Block() as block:
            @block.sync
            def _(sp):
                sp.wait_ge(z_e, 3)
                load_edges(sp, dst_f.bitcast(I32), dst)
                load_edges(sp, src_f.bitcast(I32), src)
                load_edges(sp, w_f, edge_weight)
                sp.wait_ge(z_x, 1)
                sp.dma_start(xres[:, 0:(T - 1) * D].rearrange("p (t d) -> p t d", d=D),
                             x[0:(T - 1) * P, :].rearrange("(t p) d -> p t d", p=P)).then_inc(ld_x, 16)
                sp.dma_start(xres[0:TAIL, (T - 1) * D:], x[(T - 1) * P:, :]).then_inc(ld_x, 16)
                sp.wait_ge(inter_done, 1)
                sp.dma_start(edges_by[0].rearrange("(p c) f -> p (c f)", p=P), inter).then_inc(edges_out, 16)
                sp.wait_ge(zero_done, 1)
                tiles = SLOT_TILES + SPARE
                sp.dma_start(slot_rows.rearrange("(p t) (k d) -> p (t k) d", p=P, k=KD),
                             zeros.unsqueeze(1).to_broadcast([P, tiles * KD, P])).then_inc(z_slots, 16)
                sp.wait_ge(ld_x, 32)
                sp.wait_ge(z_slots, 16)
                sp.wait_ge(edges_out, 16)

            @block.gpsimd
            def _(pool):
                G.add(pool.memset(ident, 0.0))
                G.add(pool.memset(tri, 1.0))
                pool.iota(iota_i, [[1, P]], base=0, channel_multiplier=0).then_inc(kc, 1)
                pool.iota(lane_i, [[0, 1]], base=0, channel_multiplier=1).then_inc(kc, 1)
                G.settle()
                pool.affine_select(out=ident, in_=ident, compare_op=ALU.not_equal, fill=1.0, base=0,
                                   pattern=[[-1, P]], channel_multiplier=1).then_inc(kc, 1)
                pool.affine_select(out=tri, in_=tri, compare_op=ALU.is_gt, fill=0.0, base=0,
                                   pattern=[[1, P]], channel_multiplier=-1).then_inc(kc, 1)

            @block.vector
            def _(dve):
                dve.memset(dst_f.bitcast(I32), NP).then_inc(z_e, 1)
                dve.memset(src_f.bitcast(I32), NP).then_inc(z_e, 1)
                dve.memset(w_f, 0.0).then_inc(z_e, 1)
                dve.memset(xres[:, (T - 1) * D:], 0.0).then_inc(z_x, 1)
                V.add(dve.memset(ones, 1.0))
                V.add(dve.memset(base_all, 0.0))
                dve.memset(zeros, 0.0).then_inc(zero_done, 1)
                dve.wait_ge(kc, 4)
                V.add(dve.tensor_copy(iota, iota_i))
                V.add(dve.tensor_copy(lane, lane_i))
                V.add(dve.tensor_scalar(shift_i[:, 0:P], iota_i, 5, None, ALU.arith_shift_right))
                V.then(dve.tensor_scalar(shift_i[:, P:], lane_i, 5, None, ALU.arith_shift_right))
                V.add(dve.tensor_scalar(rowmask, lane, float(TAIL), None, ALU.is_lt))
                V.then(dve.tensor_copy(shift_f, shift_i))
                V.then(dve.tensor_scalar(blk, shift_f[:, 0:P], shift_f[:, P:], None, ALU.is_equal))
                dve.wait_ge(ld_e, 9 * 16)
                for a in (dst_f, src_f):
                    V.then(dve.tensor_copy(temps[0], a.bitcast(I32)))
                    V.then(dve.tensor_copy(a, temps[0]))
                rows4 = inter.rearrange("p (c f) -> p c f", f=4)
                for f, a in enumerate((src_f, dst_f, w_f)):
                    V.add(dve.tensor_copy(rows4[:, :, f], a))
                V.then(dve.memset(rows4[:, :, 3], 0.0))
                dve.sem_inc(inter_done, 1)
                rank_keys(dve, dst_f, temps)
                key_t, eq = temps[0], temps[1]
                dve.memset(unsorted_f, 0.0).then_inc(sort_in, 1)
                V.then(dve.tensor_tensor(eq[:, 1:], key_t[:, 1:], key_t[:, 0:C - 1], ALU.is_lt))
                dve.wait_ge(sort_ps, 1)
                V.add(dve.tensor_reduce(unsorted_f[:, 0:1], eq[:, 1:], AX_X, ALU.max))
                V.add(dve.tensor_tensor(unsorted_f[0:P - 1, 1:2], ps[0:P - 1, 0:1], key_t[0:P - 1, C - 1:], ALU.is_lt))
                V.settle()
                dve.sem_inc(sort_in, 1)
                dve.wait_ge(sort_ps, 2)
                V.then(dve.tensor_reduce(unsorted_f[:, 0:1], bank(1, 2), AX_X, ALU.add))
                V.then(dve.tensor_copy(unsorted, unsorted_f[:, 0:1]))
                dve.sem_inc(unsorted_done, 1)
                with V.loop(BUCKETS, 2) as b:
                    rank_count(dve, b, temps)
                rank_bases(dve, 0, pos_dst)
                with dve.If(dve.value_load(unsorted[0:1, 0:1], min_val=0, max_val=2 * P) > 0):
                    with V_SORT.loop(BUCKETS, 4) as b:
                        for step in range(4):
                            rank_step(dve, V_SORT, b, step, pos_dst, temps)

            @block.tensor
            def _(pe):
                pe.wait_ge(kc, 4)
                pe.wait_ge(sort_in, 1)
                pe.matmul(ps[0:P - 1, 0:1], ident[:, 1:], temps[0][:, 0:1], start=True, stop=True).then_inc(sort_ps, 1)
                pe.wait_ge(sort_in, 2)
                pe.matmul(bank(1, 2), ones, unsorted_f, start=True, stop=True).then_inc(sort_ps, 1)
                rank_sums(pe, 0)

        scratch(ACC, ACC + BUCKETS * ACC_W)
        w0, wq_r, wkv_r, wp_r = (take(n * D) for n in (KD, KD, 2 * KD, KD))
        wqT, wkvT, wpT = (take(n * D) for n in (KD, 2 * KD, KD))
        xn7 = take(B * D)
        xt7 = take(B * D)
        ring_a, ring_b = take(B * D), take(B * D)
        rank_temps = [take(C), pos_src]
        scratch(FREE)
        h7 = take(B * D)
        v7 = take(B * KD * (P + 1))
        scat_ring = take(10 * SCAT)
        ctx_m, ctx_t, ksum, ksum_b, kv_out = take(KD * P), take(KD * P), take(KD), take(KD * P), take(KD * D)
        xn7v = xn7.rearrange("p (i k n) -> p i k n", i=B, k=KD)
        xt7v = xt7.rearrange("p (i k n) -> p i k n", i=B, k=KD)
        v7v = v7.rearrange("p (i k n) -> p i k n", i=B, k=KD)
        psA, psB = bank(0, B * D), bank(4, B * D)
        psV = half(0, B, B * D)
        LATE = [*range(1, B), 0]
        psC = bank(7, KD * (P + 1))
        (ld_w, w_ps, w_sb, xn_done, tp_done, xt_done, h_ps, h_sb, h_st, h_free, k_ps, v_ps, k_min, k_exp, k_done, v_done,
         c_done, c_sb, c_ps, c_back, q_ps, q_min, q_exp, q_done, den_ps, qn_done, mix_ps, mix_add) = (
            sem(n) for n in ("ld_w w_ps w_sb xn_done tp_done xt_done h_ps h_sb h_st h_free k_ps v_ps k_min k_exp k_done "
                             "v_done c_done c_sb c_ps c_back q_ps q_min q_exp q_done den_ps qn_done mix_ps mix_add"
                             ).split())

        def norm7(dve, c, base):
            dve.wait_ge(tp_done, c + (base + 1))
            for i in range(B):
                last = normalise(dve, xn7[:, i * D:(i + 1) * D], c * B + i)
            last.then_inc(xn_done, 1)

        def transpose7(pe, c, base):
            pe.wait_ge(xn_done, c + (base + 1))
            for i in range(B):
                for k in range(KD):
                    last = pe.transpose(half(0, i)[:, k * P:(k + 1) * P], xn7v[:, i, k, :], ident)
            last.then_inc(tp_done, 1)

        def keep7(act, c, base):
            act.wait_ge(tp_done, c + (base + 2))
            act.copy(xt7, psA).then_inc(xt_done, 1)
            act.copy(xnT3[:, :, ds(c * (B * P), B * P)].rearrange("p k (i n) -> p i k n", i=B),
                     psA.rearrange("p (i k n) -> p i k n", i=B, k=KD)).then_inc(xt_done, 1)

        def store7(sp, c, base, ring, table, width):
            sp.wait_ge(h_sb, c + (base + 1))
            sp.dma_start(table[ds(c * (B * P), B * P), :].rearrange("(i p) d -> p i d", p=P),
                         ring.rearrange("p (i d) -> p i d", i=B)[:, :, 0:width]).then_inc(h_st, 16)
            sp.wait_ge(h_st, c * 16 + (base + 1) * 16)
            sp.sem_inc(h_free, 1)

        with nc.Block() as block:
            @block.sync
            def _(sp):
                for to, w in ((w0, L0_gnn_W), (wq_r, L0_mix_Wq), (wkv_r, L0_mix_Wkv), (wp_r, L0_mix_Wproj)):
                    sp.dma_start(to.rearrange("p (k c) -> p k c", c=D),
                                 w.rearrange("(k p) c -> p k c", p=P)).then_inc(ld_w, 16)
                sp.sem_inc(h_free, 1)
                with sp.Fori(0, LOOPS) as c:
                    store7(sp, c, 0, h7, h0_table, D)

            @block.gpsimd
            def _(pool):
                with pool.If(pool.value_load(unsorted[0:1, 0:1], min_val=0, max_val=2 * P) > 0):
                    scatter(pool, G_SORT, 0, pos_dst, (src_f, dst_f, w_f), scat_ring)

            @block.scalar
            def _(act):
                ln_root(act)
                for n, (to, b, width) in enumerate(((wqT, 0, 512), (wkvT, 1, 1024), (wpT, 3, 512))):
                    act.wait_ge(w_ps, n + 1)
                    act.copy(to, bank(b, width)).then_inc(w_sb, 1)
                act.wait_ge(v_done, 1)
                with act.Fori(0, LOOPS) as c:
                    keep7(act, c, 0)
                    act.wait_ge(h_ps, c + 1)
                    act.wait_ge(h_free, c + 1)
                    act.copy(h7, psV).then_inc(h_sb, 1)
                    act.wait_ge(k_min, c + 1)
                    act.activation(ring_a, ring_a, ACT.Exp).then_inc(k_exp, 1)
                    act.wait_ge(c_done, c + 1)
                    act.wait_ge(v_ps, c + 1)
                    act.copy(v7v[:, :, :, 0:P], psV.rearrange("p (i k n) -> p i k n", i=B, k=KD)).then_inc(v_done, 1)
                act.wait_ge(c_ps, 1)
                act.copy(ctx_t, bank(0, KD * P)).then_inc(c_back, 1)
                act.wait_ge(c_ps, 2)
                act.copy(kv_out, bank(1, KD * D)).then_inc(c_back, 1)
                with act.Fori(0, LOOPS) as c:
                    act.wait_ge(q_min, c + 1)
                    act.activation(ring_a, ring_a, ACT.Exp).then_inc(q_exp, 1)

            @block.vector
            def _(dve):
                ln_stats(dve)
                dve.memset(v7, 1.0).then_inc(v_done, 1)
                rank_keys(dve, src_f, rank_temps)
                with V.loop(LOOPS, 2 * COUNTS) as c:
                    norm7(dve, c, 0)
                    for i in range(COUNTS):
                        rank_count(dve, c * COUNTS + i, rank_temps)
                    dve.wait_ge(k_ps, c + 1)
                    dve.tensor_scalar(ring_a, psA, 0.0, None, ALU.min).then_inc(k_min, 1)
                    dve.wait_ge(k_exp, c + 1)
                    dve.wait_ge(c_done, c + 1)
                    dve.scalar_tensor_tensor(ring_b, psA, 0.0, ring_a, ALU.max, ALU.add).then_inc(k_done, 1)
                dve.wait_ge(c_done, LOOPS + 1)
                for j in range(KD):
                    V.add(dve.tensor_tensor(ctx_m[:, j * P:(j + 1) * P], psC[:, j * (P + 1):j * (P + 1) + P], blk,
                                            ALU.mult))
                last = dve.tensor_scalar(ksum, psC[:, P::P + 1], float(NODES - NP), None, ALU.add)
                V.then(last)
                for j in range(KD):
                    last = dve.tensor_scalar(ksum_b[:, j * P:(j + 1) * P], blk, ksum[:, j:j + 1], None, ALU.mult)
                last.then_inc(c_sb, 1)

                def queries(c):
                    dve.wait_ge(q_ps, c + 1)
                    dve.tensor_scalar(ring_a, psA, 0.0, None, ALU.min).then_inc(q_min, 1)
                    dve.wait_ge(q_exp, c + 1)
                    dve.scalar_tensor_tensor(ring_b, psA, 0.0, ring_a, ALU.max, ALU.add).then_inc(q_done, 1)

                def attend(c, last=False):
                    dve.wait_ge(den_ps, c + 1)
                    V.then(dve.tensor_scalar(xn7, psB, D_MIN, None, ALU.max))
                    V.then(dve.reciprocal(xn7, xn7))
                    dve.tensor_tensor(xn7, ring_b, xn7, ALU.mult).then_inc(qn_done, 1)
                    if not last:
                        dve.wait_ge(qn_done, c + 1)
                        queries(c + 1)
                    dve.wait_ge(mix_ps, c + 1)
                    a = xres[:, ds(c * (B * D), B * D)]
                    dve.tensor_tensor(a, a, psB, ALU.add).then_inc(mix_add, 1)

                queries(0)
                with V.loop(LOOPS - 1, 2) as c:
                    attend(c)
                attend(LOOPS - 1, last=True)
                rank_bases(dve, 1, pos_src)

            @block.tensor
            def _(pe):
                pe.sem_inc(tp_done, 1)
                pe.wait_ge(ld_w, 64)
                for n, (raw, b, blocks) in enumerate(((wq_r, 0, KD), (wkv_r, 1, 2 * KD), (wp_r, 3, KD))):
                    for k in range(KD):
                        for o in range(blocks):
                            last = pe.transpose(bank(b, P, (k * blocks + o) * P),
                                                raw[:, o * D + k * P:o * D + (k + 1) * P], ident)
                    last.then_inc(w_ps, 1)
                pe.wait_ge(w_sb, 3)
                pe.wait_ge(v_done, 1)
                pe.matmul(psC, zeros, v7[:, 0:KD * (P + 1)], start=True, stop=False, skip_group_check=True)
                pe.sem_inc(c_done, 1)
                with pe.Fori(0, LOOPS) as c:
                    transpose7(pe, c, 0)
                    pe.wait_ge(xt_done, c * 2 + 1)
                    for i in LATE:
                        if i == LATE[-1]:
                            pe.wait_ge(xt_done, c * 2 + 2)
                        for k in range(KD):
                            last = pe.matmul(half(0, B + i), xt7v[:, i, k, :], w0[:, k * D:(k + 1) * D],
                                             start=(k == 0), stop=(k == KD - 1))
                    last.then_inc(h_ps, 1)
                    for i in range(B):
                        if i == B - 1:
                            pe.wait_ge(h_sb, c + 1)
                        for k in range(KD):
                            last = pe.matmul(half(0, i), xt7v[:, i, k, :], wkvT[:, k * 2 * D:k * 2 * D + D],
                                             start=(k == 0), stop=(k == KD - 1))
                    last.then_inc(k_ps, 1)
                    for i in LATE:
                        if i == LATE[-1]:
                            pe.wait_ge(k_done, c + 1)
                        for k in range(KD):
                            last = pe.matmul(half(0, B + i), xt7v[:, i, k, :], wkvT[:, k * 2 * D + D:(k + 1) * 2 * D],
                                             start=(k == 0), stop=(k == KD - 1))
                    last.then_inc(v_ps, 1)
                    pe.wait_ge(v_done, c + 2)
                    for i in range(B):
                        for k in range(KD):
                            last = pe.matmul(psC[:, k * (P + 1):(k + 1) * (P + 1)],
                                             ring_b[:, i * D + k * P:i * D + (k + 1) * P], v7v[:, i, k, :],
                                             start=False, stop=False, skip_group_check=True)
                    last.then_inc(c_done, 1)
                pe.wait_ge(c_sb, 1)
                for j in range(KD):
                    last = pe.transpose(bank(0, P, j * P), ctx_m[:, j * P:(j + 1) * P], ident)
                last.then_inc(c_ps, 1)
                pe.wait_ge(c_back, 1)
                for j in range(KD):
                    last = pe.matmul(bank(1, D, j * D), ctx_t[:, j * P:(j + 1) * P], wpT[:, j * D:(j + 1) * D],
                                     start=True, stop=True)
                last.then_inc(c_ps, 1)
                pe.wait_ge(c_back, 2)
                pe.sem_inc(mix_add, 1)

                def queries(c):
                    for i in range(B):
                        for o in range(KD):
                            for k in range(KD):
                                last = pe.matmul(half(0, i)[:, o * P:(o + 1) * P],
                                                 wqT[:, k * D + o * P:k * D + (o + 1) * P],
                                                 xnT3[:, k, ds((c * B + i) * P, P)], start=(k == 0), stop=(k == KD - 1))
                    last.then_inc(q_ps, 1)

                def attend(c, last=False):
                    pe.wait_ge(q_done, c + 1)
                    pe.wait_ge(mix_add, c + 1)
                    for i in range(B):
                        for k in range(KD):
                            q = ring_b[:, i * D + k * P:i * D + (k + 1) * P]
                            ins = pe.matmul(half(4, i)[:, k * P:(k + 1) * P], ksum_b[:, k * P:(k + 1) * P], q,
                                            start=True, stop=True)
                    ins.then_inc(den_ps, 1)
                    if not last:
                        queries(c + 1)
                    pe.wait_ge(qn_done, c + 1)
                    for i in range(B):
                        for k in range(KD):
                            ins = pe.matmul(half(4, i), xn7[:, i * D + k * P:i * D + (k + 1) * P],
                                            kv_out[:, k * D:(k + 1) * D], start=(k == 0), stop=(k == KD - 1))
                    ins.then_inc(mix_ps, 1)

                queries(0)
                with pe.Fori(0, LOOPS - 1) as c:
                    attend(c)
                attend(LOOPS - 1, last=True)
                rank_sums(pe, 1)

        gather_done = [[sem(f"gather{b}{u}_done") for u in range(U)] for b in range(2)]
        edges_ready, tiles_ready, hot_done, gnn_ps, gnn_add = (sem(n) for n in (
            "edges_ready", "tiles_ready", "hot_done", "gnn_ps", "gnn_add"))
        scratch(XNT, ACC)
        vv = visit_views()
        rows = take(2 * U * ROW1).rearrange("p (b u w) -> p b u w", b=2, u=U)
        scratch(FREE)
        hot = take(2 * U * P).rearrange("p (b u n) -> p b u n", b=2, u=U)
        idx_ring = take(2 * U).bitcast(I32)
        rank_temps = [w_f, pos_dst, take(C), take(C)]
        NVIS = GROUP_LOOPS * 2 * U
        assert GROUP_LOOPS >= BUCKETS
        GNN0_BANKS, GNN1_BANKS = 8, 4

        def gather_row(pool, slot, width, idx, table, done):
            pool.indirect_dma_start(slot[:, 0:width], None, table, bass.IndirectOffsetOnAxis(ap=idx, axis=0)
                                    ).then_inc(done, 16)

        def load_tiles(engine, first):
            return nc.values_load_multi_w_load_instructions(
                tile_row[0:1, ds(first, U)], engines=[engine.engine], min_val=0, max_val=T,
                skip_runtime_bounds_check_because="a visit's tile is a count of at most T tiles")[1]

        def add_sums(dve, n, tile, width, b, sums_before, adds_before):
            dve.wait_ge(gnn_ps, n + (sums_before + 1))
            dve.wait_ge(gnn_add, n + adds_before)
            to = acc[:, ds(tile * ACC_W, width)]
            dve.tensor_tensor(to, to, bank(b, width), ALU.add).then_inc(gnn_add, 1)

        with nc.Block() as block:
            @block.sync
            def _(sp):
                visits_sync(sp, 0, vv)
                sp.sem_inc(tiles_ready, 1)

            @block.gpsimd
            def _(pool):
                visits_pool(pool, 0, vv)
                pool.wait_ge(edges_ready, 1)
                with G.loop(GROUP_LOOPS, 2) as j:
                    for b in range(2):
                        pool.wait_ge(gnn_ps, j * (2 * U) + (b + 1) * U)
                        G.then(pool.tensor_copy(idx_ring[:, b * U:(b + 1) * U], v_idx[:, ds(j * (2 * U) + b * U, U)]))
                        pool.sem_inc(dma_turn, 1)
                        for u in range(U):
                            gather_row(pool, rows[:, b, u, :], D, idx_ring[:, b * U + u:b * U + u + 1], h0_table,
                                       gather_done[b][u])

            @block.vector
            def _(dve):
                visits_dve(dve, 0, vv)
                V.then(dve.memset(acc, 0.0))
                dve.sem_inc(edges_ready, 1)
                dve.sem_inc(gnn_add, GNN0_BANKS)
                rank_keys(dve, src_f, rank_temps)
                dve.wait_ge(tiles_ready, 1)
                def weighted_hot(n, b, u):
                    dve.tensor_scalar(hot[:, b, u, :], iota, v_loc[:, ds(n, 1)], v_w[:, ds(n, 1)],
                                      ALU.is_equal, ALU.mult).then_inc(hot_done, 1)

                for u in range(U):
                    weighted_hot(u, 0, u)
                with V.loop(GROUP_LOOPS, 4) as j:
                    for b in range(2):
                        tiles = load_tiles(dve, j * (2 * U) + b * U)
                        for u in range(U):
                            weighted_hot(j * (2 * U) + (b + 1) * U + u, 1 - b, u)
                            add_sums(dve, j * (2 * U) + b * U + u, tiles[u], D, u, 2 * U, GNN0_BANKS)
                            if u % HALF_U == 1:
                                rank_step(dve, V, j, 2 * b + u // HALF_U, pos_src, rank_temps)

            @block.tensor
            def _(pe):
                visits_pe(pe, 0, vv)
                pe.sem_inc(gnn_ps, 2 * U)
                pe.wait_ge(edges_ready, 1)
                with pe.Fori(0, GROUP_LOOPS) as j:
                    for b in range(2):
                        for u in range(U):
                            n = j * (2 * U) + b * U + u
                            pe.wait_ge(hot_done, n + 1)
                            pe.wait_ge(gather_done[b][u], j * 16 + 16)
                            pe.wait_ge(gnn_add, n + 1)
                            pe.matmul(bank(u, D), hot[:, b, u, :], rows[:, b, u, 0:D], start=True, stop=True
                                      ).then_inc(gnn_ps, 1)

        scratch(FREE)
        scat_ring = take(10 * SCAT)
        xn7, xt7 = take(B * D), take(B * D)
        bias_b, bproj_b = take(D), take(D)
        idx_f = take(T)
        rev = take(E0)
        rw_t, router_b, expert_of, b1_t, b2_s = take(KD * E0), take(E0), take(HB), take(HB), take(D)
        scratch(place["at"])
        mean56, std56 = take(B * D // HC), take(B * D // HC)
        scratch(ACC, ACC + BUCKETS * ACC_W)
        w1_s, w2_s = take(KD * E0 * H0), take(HB * D)
        RINGS0 = place["at"]
        h_ring = [take(B * P) for _ in range(2)]
        hm_ring = [take(B * P) for _ in range(2)]
        logits, is_top = (arena[:, RINGS0 + i * T * E0:RINGS0 + (i + 1) * T * E0] for i in range(2))
        assert RINGS0 + 2 * T * E0 <= place["at"]
        idx_b = take(B * P)
        rw_raw = idx_b[0:E0, 0:D]
        w_f_at = ACC + BUCKETS * ACC_W + 3 * C
        scratch(w_f_at, FREE)
        hot32 = take(B * P)
        g1_w = take(KD * ROW1)
        scratch(ACC, ACC + BUCKETS * ACC_W)
        z7 = take(B * KD * (P + 1))
        xc7, sq7, h7 = take(B * D), take(B * D), take(B * ROW1)
        al_b, ar_b, wa_tmp = take(D), take(D), take(D)
        wk_c, bk_c, wv_b, bv_b, kcol = take(KD), take(KD), take(D), take(D), take(2 * KD)
        s_bc, kvm, kv_t = take(KD * P), take(KD * P), take(KD * P)
        xn7v = xn7.rearrange("p (i k n) -> p i k n", i=B, k=KD)
        xt7v = xt7.rearrange("p (i k n) -> p i k n", i=B, k=KD)
        z7v = z7.rearrange("p (i k n) -> p i k n", i=B, k=KD)
        w1v = w1_s.rearrange("p (k m) -> p k m", k=KD)
        (ld_b, ld_e1, ld_e2, ld_g, x1_done, rw_ps, rw_sb, lg_ps, lg_sb, ib_done, ib_ps, hot_e, m1_ps, he_done, hm_done,
         m2_ps, x2_add, x2_done, sq_in, sq_done, ss_done, sd_done, z_done, gram, s_done, s_ps, kvm_done, xs_done,
         mx_ps, mx_add) = (sem(n) for n in (
             "ld_b ld_e1 ld_e2 ld_g x1_done rw_ps rw_sb lg_ps lg_sb ib_done ib_ps hot_e m1_ps he_done hm_done m2_ps "
             "x2_add x2_done sq_in sq_done ss_done sd_done z_done gram s_done s_ps kvm_done xs_done mx_ps mx_add"
         ).split())
        CALL1, CALL2 = LOOPS, 2 * LOOPS

        def mask_padding(dve):
            last = xres[:, (T - 1) * D:]
            V.then(dve.tensor_scalar(last, last, rowmask, None, ALU.mult))

        with nc.Block() as block:
            @block.sync
            def _(sp):
                for to, a in ((bias_b, L0_gnn_b), (bproj_b, L0_mix_bproj), (router_b, L0_ffn_router_b)):
                    sp.dma_start(to, a.partition_broadcast(P)).then_inc(ld_b, 16)
                sp.dma_start(b1_t, L0_ffn_b1.rearrange("e h -> (e h)").rearrange("(j p) -> p j", p=P),
                             allow_slow_non_contiguous=True).then_inc(ld_b, 16)
                sp.dma_start(b2_s[0:E0, :], L0_ffn_b2).then_inc(ld_b, 16)
                sp.dma_start(g1_w.rearrange("p (k w) -> p k w", k=KD)[:, :, 0:D],
                             L1_gnn_W.rearrange("(k p) w -> p k w", p=P)).then_inc(ld_b, 16)
                sp.wait_ge(x1_done, 1)
                sp.dma_start(rw_raw, L0_ffn_router_w).then_inc(ld_e1, 16)
                for k in range(KD):
                    sp.dma_start(w1v[:, k, :].rearrange("p (e h) -> p e h", h=H0),
                                 L0_ffn_W1[:, k * P:(k + 1) * P, :].rearrange("e p h -> p e h")).then_inc(ld_e2, 16)
                sp.dma_start(w2_s.rearrange("p (j d) -> p j d", d=D),
                             L0_ffn_W2.rearrange("e h d -> (e h) d").rearrange("(j p) d -> p j d", p=P)
                             ).then_inc(ld_e2, 16)
                sp.wait_ge(ld_e2, 48)
                sp.wait_ge(x2_done, 1)
                sp.dma_start(al_b, L1_gnn_a_l.rearrange("o h f -> (o h f)").partition_broadcast(P)).then_inc(ld_g, 16)
                sp.dma_start(ar_b, L1_gnn_a_r.rearrange("o h f -> (o h f)").partition_broadcast(P)).then_inc(ld_g, 16)
                for to, a in ((wk_c, L1_mix_kln_weight), (bk_c, L1_mix_kln_bias)):
                    sp.dma_start(to, a.rearrange("h o c -> (h o c)").rearrange("(k p) -> p k", p=P),
                                 allow_slow_non_contiguous=True).then_inc(ld_g, 16)
                for to, a in ((wv_b, L1_mix_vln_weight), (bv_b, L1_mix_vln_bias)):
                    sp.dma_start(to, a.rearrange("h o c -> (h o c)").partition_broadcast(P)).then_inc(ld_g, 16)
                with sp.Fori(0, LOOPS) as c:
                    store7(sp, c, CALL1, h7, h1_table, ROW1)

            @block.gpsimd
            def _(pool):
                scatter(pool, G, 1, pos_src, (dst_f, src_f), scat_ring)

            @block.scalar
            def _(act):
                ln_root(act)
                act.wait_ge(rw_ps, 1)
                act.copy(rw_t, bank(7, KD * E0)).then_inc(rw_sb, 1)
                with act.Fori(0, LOOPS) as c:
                    keep7(act, c, CALL1)
                act.wait_ge(ld_b, 6 * 16)
                with act.Fori(0, LOOPS) as c:
                    for j in range(HB):
                        act.wait_ge(m1_ps, c * HB + (j + 1))
                        if j >= 2:
                            act.wait_ge(hm_done, c * HB + (j - 1))
                        act.activation(h_ring[j % 2].rearrange("p (f n) -> p f n", f=2),
                                       bank(2 * (j % 2), 1024).rearrange("p (f n) -> p f n", f=2)[:, :, 0:HALF],
                                       ACT.Relu, bias=b1_t[:, j:j + 1]).then_inc(he_done, 1)
                ln_root(act)
                with act.Fori(0, LOOPS) as c:
                    keep7(act, c, CALL2)
                    act.wait_ge(sq_in, c + 1)
                    act.activation(sq7, xc7, ACT.Square).then_inc(sq_done, 1)
                    act.wait_ge(ss_done, c + 1)
                    act.activation(std56, std56, ACT.Sqrt, scale=1.0 / (HC - 1)).then_inc(sd_done, 1)
                    act.wait_ge(h_ps, c + (LOOPS + 1))
                    act.wait_ge(h_free, c + (LOOPS + 1))
                    got = bank(0, B * 512).rearrange("p (i w) -> p i w", w=512)
                    act.copy(rl_all[:, ds(c * (B * 2 * GH), B * 2 * GH)].rearrange("p (i w) -> p i w", i=B),
                             got[:, :, D:ROW1])
                    act.copy(h7.rearrange("p (i w) -> p i w", i=B), got[:, :, 0:ROW1]).then_inc(h_sb, 1)
                act.sem_inc(xs_done, 1)
                with act.Fori(0, LOOPS) as c:
                    act.wait_ge(mx_ps, c + 1)
                    act.copy(xt7v.rearrange("p i k n -> p k i n"),
                             xnT3[:, :, ds(c * (B * P), B * P)].rearrange("p k (i n) -> p k i n", i=B)
                             ).then_inc(xs_done, 1)

            @block.vector
            def _(dve):
                dve.wait_ge(ld_b, 6 * 16)
                with V.loop(LOOPS, 3) as c:
                    a = xres[:, ds(c * (B * D), B * D)].rearrange("p (i d) -> p i d", i=B)
                    t = xn7.rearrange("p (i d) -> p i d", i=B)
                    got = acc[:, ds(c * (B * ACC_W), B * ACC_W)].rearrange("p (i w) -> p i w", i=B)[:, :, 0:D]
                    wide = [w.unsqueeze(1).to_broadcast([P, B, D]) for w in (bias_b, bproj_b)]
                    V.then(dve.tensor_tensor(t, got, wide[0], ALU.add))
                    V.then(dve.scalar_tensor_tensor(t, t, 0.0, wide[1], ALU.max, ALU.add))
                    V.then(dve.tensor_tensor(a, a, t, ALU.add))
                dve.sem_inc(x1_done, 1)
                mask_padding(dve)
                ln_stats(dve)
                def keep_logits(c):
                    dve.wait_ge(lg_ps, c + 1)
                    dve.tensor_copy(logits[:, ds(c * (B * E0), B * E0)], bank(4, B * E0)).then_inc(lg_sb, 1)

                dve.sem_inc(lg_sb, 1)
                norm7(dve, 0, CALL1)
                with dve.Fori(0, LOOPS - 1) as c:
                    norm7(dve, c + 1, CALL1)
                    keep_logits(c)
                keep_logits(LOOPS - 1)
                dve.wait_ge(lg_sb, LOOPS + 1)
                wide = [P, T, E0]
                lg3, eq3 = (a.rearrange("p (t e) -> p t e", e=E0) for a in (logits, is_top))
                V.add(dve.tensor_tensor(lg3, lg3, router_b.unsqueeze(1).to_broadcast(wide), ALU.add))
                V.add(dve.tensor_scalar(rev, iota[:, 0:E0], -1.0, float(E0), ALU.mult, ALU.add))
                V.settle()
                V.then(dve.tensor_reduce(idx_f, lg3, AX_X, ALU.max))
                V.then(dve.tensor_tensor(eq3, lg3, idx_f.unsqueeze(2).to_broadcast(wide), ALU.is_ge))
                V.then(dve.tensor_tensor(eq3, eq3, rev.unsqueeze(1).to_broadcast(wide), ALU.mult))
                V.then(dve.tensor_reduce(idx_f, eq3, AX_X, ALU.max))
                V.then(dve.tensor_scalar(idx_f, idx_f, -1.0, float(E0), ALU.mult, ALU.add))
                V.then(dve.tensor_scalar(mean56[:, 0:1], lane, float(H0), None, ALU.is_ge))
                V.then(dve.tensor_scalar(expert_of, iota[:, 0:HB], 2.0, mean56[:, 0:1], ALU.mult, ALU.add))
                with dve.Fori(0, LOOPS) as c:
                    dve.tensor_copy(xn7[:, 0:B * P].rearrange("p (i n) -> p i n", i=B),
                                    idx_f[:, ds(c * B, B)].unsqueeze(2).to_broadcast([P, B, P])).then_inc(ib_done, 1)
                    dve.wait_ge(ib_ps, c + 1)
                    dve.tensor_copy(idx_b, bank(0, B * P)).then_inc(hot_e, 1)
                    dve.tensor_scalar(hot32[0:E0, :], ps[0:E0, 0:B * P], lane[0:E0, :], None, ALU.is_equal
                                      ).then_inc(hot_e, 1)
                    dve.wait_ge(hot_e, c * 2 + 2)
                    for j in range(HB):
                        dve.wait_ge(he_done, c * HB + (j + 1))
                        if j >= 2:
                            dve.wait_ge(m2_ps, c * HB + (j - 1))
                        dve.scalar_tensor_tensor(hm_ring[j % 2], idx_b, expert_of[:, j:j + 1], h_ring[j % 2],
                                                 ALU.is_equal, ALU.mult).then_inc(hm_done, 1)
                    dve.wait_ge(m2_ps, c * HB + HB)
                    a = xres[:, ds(c * (B * D), B * D)]
                    dve.scalar_tensor_tensor(a, psB, 0.0, a, ALU.max, ALU.add).then_inc(x2_add, 1)
                dve.wait_ge(x2_add, LOOPS + 1)
                dve.sem_inc(x2_done, 1)
                mask_padding(dve)
                ln_stats(dve)
                dve.wait_ge(ld_g, 6 * 16)
                for k in range(KD):
                    for f, a in ((0, ar_b), (1, al_b)):
                        V.then(dve.tensor_tensor(wa_tmp, g1_w[:, k * ROW1:k * ROW1 + D], a, ALU.mult))
                        at = k * ROW1 + D + f * GH
                        V.then(dve.tensor_reduce(g1_w[:, at:at + GH], wa_tmp.rearrange("p (h f) -> p h f", h=GH),
                                                 AX_X, ALU.add))
                dve.memset(z7, 1.0).then_inc(z_done, 1)
                with V.loop(LOOPS, 5) as c:
                    norm7(dve, c, CALL2)
                    dve.wait_ge(xn_done, c + (CALL2 + 1))
                    heads = xn7.rearrange("p (m e) -> p m e", e=HC)
                    cents = xc7.rearrange("p (m e) -> p m e", e=HC)
                    V.then(dve.tensor_reduce(mean56, heads, AX_X, ALU.add))
                    V.then(dve.tensor_scalar(mean56, mean56, 1.0 / HC, None, ALU.mult))
                    dve.tensor_tensor(cents, heads, mean56.unsqueeze(2).to_broadcast([P, B * D // HC, HC]),
                                      ALU.subtract).then_inc(sq_in, 1)
                    dve.wait_ge(sq_done, c + 1)
                    dve.tensor_reduce(std56, sq7.rearrange("p (m e) -> p m e", e=HC), AX_X, ALU.add
                                      ).then_inc(ss_done, 1)
                    dve.wait_ge(sd_done, c + 1)
                    V.then(dve.tensor_scalar(std56, std56, KV_EPS, None, ALU.add))
                    V.then(dve.reciprocal(std56, std56))
                    dve.wait_ge(gram, c + 1)
                    V.add(dve.tensor_tensor(
                        z7.rearrange("p (m w) -> p m w", w=P + 1)[:, :, 0:P].rearrange("p m (h e) -> p m h e", e=HC),
                        xc7.rearrange("p (m h e) -> p m h e", m=B * KD, e=HC),
                        std56.rearrange("p (m h) -> p m h", m=B * KD).unsqueeze(3).to_broadcast(
                            [P, B * KD, P // HC, HC]), ALU.mult))
                    V.settle()
                    dve.sem_inc(z_done, 1)
                dve.wait_ge(gram, LOOPS + 1)
                V.add(dve.tensor_tensor(kcol[:, 0:KD], wk_c, psC[:, P::P + 1], ALU.mult))
                V.add(dve.tensor_scalar(kcol[:, KD:], bk_c, float(NODES), None, ALU.mult))
                for k in range(KD):
                    last = dve.tensor_copy(s_bc[:, k * P:(k + 1) * P],
                                           psC[:, k * (P + 1) + P:(k + 1) * (P + 1)].to_broadcast([P, P]))
                last.then_inc(s_done, 1)
                V.settle()
                dve.wait_ge(s_ps, 1)
                for k in range(KD):
                    m, at = kvm[:, k * P:(k + 1) * P], slice(k * P, (k + 1) * P)
                    t = kv_t[:, at]
                    V.add(dve.scalar_tensor_tensor(m, psC[:, k * (P + 1):k * (P + 1) + P], wk_c[:, k:k + 1],
                                                   wv_b[:, at], ALU.mult, ALU.mult))
                    V.then(dve.tensor_tensor(t, bank(0, P, k * P), wv_b[:, at], ALU.mult))
                    V.then(dve.scalar_tensor_tensor(m, bv_b[:, at], kcol[:, k:k + 1], m, ALU.mult, ALU.add))
                    V.then(dve.scalar_tensor_tensor(m, t, bk_c[:, k:k + 1], m, ALU.mult, ALU.add))
                    V.then(dve.scalar_tensor_tensor(m, bv_b[:, at], kcol[:, KD + k:KD + k + 1], m, ALU.mult, ALU.add))
                    V.then(dve.scalar_tensor_tensor(m, m, 1.0 / NODES, blk, ALU.mult, ALU.mult))
                    last = dve.tensor_tensor(m, m, ident, ALU.add)
                last.then_inc(kvm_done, 1)
                with dve.Fori(0, LOOPS) as c:
                    dve.wait_ge(mx_ps, c + 2)
                    a = xres[:, ds(c * (B * D), B * D)]
                    dve.tensor_tensor(a, a, psB, ALU.add).then_inc(mx_add, 1)

            @block.tensor
            def _(pe):
                pe.wait_ge(ld_e1, 16)
                for k in range(KD):
                    last = pe.transpose(bank(7, E0, k * E0), rw_raw[:, k * P:(k + 1) * P], ident[0:E0, 0:E0])
                last.then_inc(rw_ps, 1)
                pe.wait_ge(rw_sb, 1)
                pe.wait_ge(ld_b, 6 * 16)
                with pe.Fori(0, LOOPS) as c:
                    transpose7(pe, c, CALL1)
                    pe.wait_ge(xt_done, c * 2 + (2 * CALL1 + 1))
                    pe.wait_ge(lg_sb, c + 1)
                    for i in range(B):
                        for k in range(KD):
                            last = pe.matmul(bank(4, E0, i * E0), xt7v[:, i, k, :], rw_t[:, k * E0:(k + 1) * E0],
                                             start=(k == 0), stop=(k == KD - 1))
                    last.then_inc(lg_ps, 1)
                    pe.wait_ge(xt_done, c * 2 + (2 * CALL1 + 2))
                pe.wait_ge(ld_e2, 48)
                pe.sem_inc(x2_add, 1)
                with pe.Fori(0, LOOPS) as c:
                    def hidden(j):
                        for f in range(2):
                            for k in range(KD):
                                last = pe.matmul(bank(2 * (j % 2) + f, HALF), w1v[:, k, j * P:(j + 1) * P],
                                                 xnT3[:, k, ds(c * (B * P) + f * HALF, HALF)],
                                                 start=(k == 0), stop=(k == KD - 1))
                        last.then_inc(m1_ps, 1)

                    pe.wait_ge(ib_done, c + 1)
                    for i in range(B):
                        last = pe.transpose(bank(0, P, i * P), xn7[:, i * P:(i + 1) * P], ident)
                    last.then_inc(ib_ps, 1)
                    pe.wait_ge(hot_e, c * 2 + 2)
                    pe.wait_ge(x2_add, c + 1)
                    for i in range(B):
                        pe.matmul(half(4, i), hot32[0:E0, i * P:(i + 1) * P], b2_s[0:E0, :], start=(i % 2 == 0),
                                  stop=False, skip_group_check=True)
                    hidden(0)
                    for j in range(HB):
                        if j + 1 < HB:
                            hidden(j + 1)
                        pe.wait_ge(hm_done, c * HB + (j + 1))
                        for i in range(B):
                            last = pe.matmul(half(4, i), hm_ring[j % 2][:, i * P:(i + 1) * P],
                                             w2_s[:, j * D:(j + 1) * D], start=False, stop=(j == HB - 1),
                                             skip_group_check=True)
                        last.then_inc(m2_ps, 1)
                pe.wait_ge(z_done, 1)
                pe.matmul(psC, zeros, z7[:, 0:KD * (P + 1)], start=True, stop=False, skip_group_check=True)
                pe.sem_inc(gram, 1)
                with pe.Fori(0, LOOPS) as c:
                    transpose7(pe, c, CALL2)
                    pe.wait_ge(xt_done, c * 2 + (2 * CALL2 + 2))
                    for i in range(B):
                        for k in range(KD):
                            last = pe.matmul(bank(i, ROW1), xt7v[:, i, k, :], g1_w[:, k * ROW1:(k + 1) * ROW1],
                                             start=(k == 0), stop=(k == KD - 1))
                    last.then_inc(h_ps, 1)
                    pe.wait_ge(z_done, c + 2)
                    for i in range(B):
                        for k in range(KD):
                            last = pe.matmul(psC[:, k * (P + 1):(k + 1) * (P + 1)], z7v[:, i, k, 0:P], z7v[:, i, k, :],
                                             start=False, stop=False, skip_group_check=True)
                    last.then_inc(gram, 1)
                    pe.wait_ge(h_sb, c + (CALL1 + 1))
                pe.wait_ge(s_done, 1)
                for k in range(KD):
                    last = pe.matmul(bank(0, P, k * P), s_bc[:, k * P:(k + 1) * P], ident, start=True, stop=True)
                last.then_inc(s_ps, 1)
                pe.wait_ge(kvm_done, 1)
                pe.sem_inc(mx_ps, 1)
                pe.sem_inc(mx_add, 1)
                with pe.Fori(0, LOOPS) as c:
                    pe.wait_ge(xs_done, c + 2)
                    pe.wait_ge(mx_add, c + 1)
                    for i in range(B):
                        for k in range(KD):
                            last = pe.matmul(half(4, i)[:, k * P:(k + 1) * P], xt7v[:, i, k, :],
                                             kvm[:, k * P:(k + 1) * P], start=True, stop=True)
                    last.then_inc(mx_ps, 1)

        scratch(XNT, ACC)
        vv = visit_views()
        scratch(XNT, ACC)
        rows = take(R * U * ROW1).rearrange("p (r u w) -> p r u w", r=R, u=U)
        scratch(ACC + BUCKETS * ACC_W)
        hot_b = [take(U * P // 2).bitcast(BF16) for _ in range(2)]
        hot_t = take(U * P // 2).bitcast(BF16)
        ident_b = take(P // 2).bitcast(BF16)
        lc = take(BUCKETS * 2 * GH)
        lc_parts = take(BUCKETS * PARTS * 2 * GH // 2).bitcast(BF16)
        look = take(U * 2 * GH).rearrange("p (u w) -> p u w", u=U)
        r_max, r_rows = take(GH), take(GH * P)
        score = take(U * GH).rearrange("p (u h) -> p u h", u=U)
        assert place["at"] <= FREE
        scratch(FREE)
        hot = take(2 * U * P).rearrange("p (b u n) -> p b u n", b=2, u=U)
        idx_ring = take(R * U).bitcast(I32)
        den7, t7 = take(B * GH), take(B * D)
        lc3 = lc.rearrange("p (t w) -> p t w", w=2 * GH)
        rl3 = rl_all.rearrange("p (t w) -> p t w", w=2 * GH)
        rows_done = gather_done[0][0:R]
        ROWS_BEFORE = GROUP_LOOPS * 16
        SUMS_BEFORE, ADDS_BEFORE = NVIS + 2 * U, NVIS + GNN0_BANKS
        lcp = lc_parts.rearrange("p (t q w) -> p t q w", q=PARTS, w=2 * GH)
        LW = PARTS * 2 * GH
        (rm_done, rm_ps, lc_done, hots_done, hott_ps, hott_done, look_ps, score_done, ex_done, msg_done,
         hot_done32, idx_done) = (
            sem(n) for n in ("rm_done rm_ps lc_done hots_done hott_ps hott_done look_ps score_done ex_done "
                             "msg_done hot_done32 idx_done").split())

        with nc.Block() as block:
            @block.sync
            def _(sp):
                visits_sync(sp, 1, vv)
                sp.sem_inc(tiles_ready, 1)

            @block.gpsimd
            def _(pool):
                visits_pool(pool, 1, vv)
                pool.wait_ge(edges_ready, 2)
                pool.wait_ge(tiles_ready, 2)
                with pool.Fori(0, RINGS_OF_R) as j:
                    for r in range(R):
                        g = j * R + r
                        pool.wait_ge(idx_done, g + 1)
                        for u in range(U):
                            if u % HALF_U == 0:
                                pool.wait_ge(gnn_ps, g * U + (SUMS_BEFORE + u + HALF_U))
                                pool.sem_inc(dma_turn, 1)
                            gather_row(pool, rows[:, r, u, :], ROW1, idx_ring[:, r * U + u:r * U + u + 1], h1_table,
                                       rows_done[r])

            @block.scalar
            def _(act):
                def keep_hot(g):
                    act.wait_ge(hott_ps, g + 1)
                    act.copy(hot_t, bank(0, U * P // 2).bitcast(BF16)).then_inc(hott_done, 1)

                def widen_hot(g, b):
                    act.wait_ge(hots_done, g + 1)
                    act.copy(hot[:, b, :, :].rearrange("p u n -> p (u n)"), hot_b[b]).then_inc(hot_done32, 1)

                def weigh(g, r):
                    act.wait_ge(score_done, g + 1)
                    act.activation(rows[:, r, :, D:D + GH], score, ACT.Exp, scale=-1.0).then_inc(ex_done, 1)

                def step(j, r, last=False):
                    g = j * R + r
                    if not last:
                        weigh(g + 1, (r + 1) % R)
                    keep_hot(g + 2)
                    act.wait_ge(gnn_ps, g * U + (SUMS_BEFORE + (R + 1) * U))
                    widen_hot(g + 2, r % 2)

                for g in range(2):
                    keep_hot(g)
                    widen_hot(g, g)
                weigh(0, 0)
                with act.Fori(0, RINGS_OF_R - 1) as j:
                    for r in range(R):
                        step(j, r)
                for r in range(R):
                    step(RINGS_OF_R - 1, r, last=(r == R - 1))

            @block.vector
            def _(dve):
                V.then(dve.tensor_reduce(r_max, rl3[:, 0:T, 0:GH].rearrange("p t h -> p h t"), AX_X, ALU.max))
                dve.tensor_copy(r_rows.rearrange("p (h n) -> p h n", h=GH),
                                r_max.unsqueeze(2).to_broadcast([P, GH, P])).then_inc(rm_done, 1)
                dve.wait_ge(rm_ps, 1)
                V.then(dve.tensor_reduce(r_max, bank(3, GH * P).rearrange("p (h n) -> p h n", h=GH), AX_X, ALU.max))
                V.then(dve.memset(lc, 0.0))
                V.add(dve.tensor_copy(lc3[:, 0:T, 0:GH], rl3[:, 0:T, GH:]))
                bound = lc3[:, 0:T, GH:]
                V.then(dve.tensor_tensor(bound, rl3[:, 0:T, GH:], r_max.unsqueeze(1).to_broadcast([P, T, GH]), ALU.add))
                V.then(dve.scalar_tensor_tensor(bound, bound, ALPHA, bound, ALU.mult, ALU.max))
                V.then(dve.tensor_scalar(bound, bound, -LIFT - OTHER, None, ALU.add))
                for q in range(PARTS):
                    V.then(dve.tensor_copy(lcp[:, :, q, :], lc3))
                    if q + 1 < PARTS:
                        V.then(dve.tensor_tensor(lc3, lc3, lcp[:, :, q, :], ALU.subtract))
                V.then(dve.tensor_copy(ident_b, ident))
                dve.sem_inc(lc_done, 1)
                visits_dve(dve, 1, vv)
                V.then(dve.memset(acc, 0.0))
                dve.sem_inc(edges_ready, 1)
                dve.sem_inc(gnn_add, GNN1_BANKS)
                dve.wait_ge(tiles_ready, 2)

                def name_rows(g, r):
                    dve.tensor_copy(idx_ring[:, r * U:(r + 1) * U], v_idx[:, ds(g * U, U)]).then_inc(idx_done, 1)

                def one_hot(g, b):
                    wide = [P, U, P]
                    dve.tensor_tensor(hot_b[b].rearrange("p (u n) -> p u n", u=U), iota.unsqueeze(1).to_broadcast(wide),
                                      v_loc[:, ds(g * U, U)].unsqueeze(2).to_broadcast(wide), ALU.is_equal
                                      ).then_inc(hots_done, 1)

                def attend(j, r, stage):
                    g, b = j * R + r, r % 2
                    if stage == 0:
                        dve.wait_ge(rows_done[r], j * (16 * U) + (ROWS_BEFORE + 16 * U))
                        name_rows(g + R, r)
                        dve.wait_ge(look_ps, g + 1)
                        V.add(dve.tensor_reduce(look, bank(2 + b, U * LW).rearrange(
                            "p (u q w) -> p u w q", u=U, q=PARTS), AX_X, ALU.add))
                    elif stage == 1:
                        V.settle()
                        V.add(dve.tensor_tensor(score, look[:, :, 0:GH], rows[:, r, :, D:D + GH], ALU.add))
                    elif stage == 2:
                        V.settle()
                        V.add(dve.scalar_tensor_tensor(score, score, ALPHA, score, ALU.mult, ALU.max))
                    elif stage == 3:
                        V.settle()
                        dve.scalar_tensor_tensor(score, look[:, :, GH:], OTHER, score, ALU.add, ALU.subtract
                                                 ).then_inc(score_done, 1)
                    elif stage == 4:
                        dve.wait_ge(hot_done32, g + 1)
                        one_hot(g + 2, b)
                    else:
                        dve.wait_ge(ex_done, g + 1)
                        q = (stage - 5) * HALF_U
                        msg = rows[:, r, q:q + HALF_U, 0:D].rearrange("p u (h f) -> p u h f", h=GH)
                        ex = rows[:, r, q:q + HALF_U, D:D + GH].unsqueeze(3).to_broadcast([P, HALF_U, GH, GF])
                        dve.tensor_tensor(msg, msg, ex, ALU.mult).then_inc(msg_done, 1)

                STAGES = 7

                def step(j, r, last=False):
                    g = j * R + r
                    tiles = load_tiles(dve, g * U)
                    for u in range(U):
                        add_sums(dve, g * U + u, tiles[u], ACC_W, 4 + u % GNN1_BANKS, SUMS_BEFORE + R * U,
                                 ADDS_BEFORE + GNN1_BANKS)
                        if u >= U - STAGES and not last:
                            attend(j + (r + 1) // R, (r + 1) % R, u - (U - STAGES))

                for r in range(R):
                    name_rows(r, r)
                for g in range(2):
                    one_hot(g, g)
                for stage in range(STAGES):
                    attend(0, 0, stage)
                with V.loop(RINGS_OF_R - 1, R * 3) as j:
                    for r in range(R):
                        step(j, r)
                for r in range(R):
                    step(RINGS_OF_R - 1, r, last=(r == R - 1))
                dve.wait_ge(gnn_add, 2 * NVIS + GNN0_BANKS + GNN1_BANKS)
                with V.loop(LOOPS, 4) as c:
                    got = acc[:, ds(c * (B * ACC_W), B * ACC_W)].rearrange("p (i w) -> p i w", i=B)
                    den = den7.rearrange("p (i h) -> p i h", i=B)
                    V.then(dve.tensor_scalar(den, got[:, :, D:], DEN_MIN, None, ALU.max))
                    V.then(dve.reciprocal(den7, den7))
                    V.then(dve.tensor_tensor(t7.rearrange("p (i h f) -> p i h f", i=B, h=GH),
                                             got[:, :, 0:D].rearrange("p i (h f) -> p i h f", h=GH),
                                             den.unsqueeze(3).to_broadcast([P, B, GH, GF]), ALU.mult))
                    a = xres[:, ds(c * (B * D), B * D)]
                    V.then(dve.tensor_tensor(a, a, t7, ALU.add))

            @block.tensor
            def _(pe):
                pe.wait_ge(rm_done, 1)
                for h in range(GH):
                    last = pe.transpose(bank(3, P, h * P), r_rows[:, h * P:(h + 1) * P], ident)
                last.then_inc(rm_ps, 1)
                pe.wait_ge(lc_done, 1)
                visits_pe(pe, 1, vv)
                pe.sem_inc(gnn_ps, R * U)
                pe.wait_ge(edges_ready, 2)
                pe.wait_ge(tiles_ready, 2)

                def flip_hot(g, b):
                    pe.wait_ge(hots_done, g + 1)
                    for u in range(U):
                        last = pe.transpose(bank(0, P // 2, u * P // 2).bitcast(BF16), hot_b[b][:, u * P:(u + 1) * P],
                                            ident_b)
                    last.then_inc(hott_ps, 1)

                def look_up(g, b):
                    tiles = load_tiles(pe, g * U)
                    pe.wait_ge(hott_done, g + 1)
                    for u in range(U):
                        last = pe.matmul(bank(2 + b, LW, u * LW), hot_t[:, u * P:(u + 1) * P],
                                         lc_parts[:, ds(tiles[u] * LW, LW)], start=True, stop=True)
                    last.then_inc(look_ps, 1)

                flip_hot(0, 0)
                look_up(0, 0)
                flip_hot(1, 1)
                with pe.Fori(0, RINGS_OF_R) as j:
                    for r in range(R):
                        g, b = j * R + r, r % 2
                        look_up(g + 1, 1 - b)
                        pe.wait_ge(hot_done32, g + 1)
                        for u in range(U):
                            if u % HALF_U == 0:
                                pe.wait_ge(msg_done, g * 2 + (u // HALF_U + 1))
                            if u == HALF_U:
                                flip_hot(g + 2, b)
                            pe.wait_ge(gnn_add, g * U + (ADDS_BEFORE + u + 1))
                            pe.matmul(bank(4 + u % GNN1_BANKS, ACC_W), hot[:, b, u, :], rows[:, r, u, 0:ACC_W],
                                      start=True, stop=True).then_inc(gnn_ps, 1)

        W_E = KD * F1
        assert W_E == FB * D
        TILES_LO = (T + 1) // 2
        HALVES = [(k, t0, t1) for k in range(K1) for t0, t1 in ((0, TILES_LO), (TILES_LO, T))]
        SLOT_PAIRS = SLOT_TILES // 2
        assert SLOT_PAIRS * 2 == SLOT_TILES
        W1_AT, W2_AT = arena_words - 2 * E1 * W_E, arena_words - E1 * W_E
        scratch(GRAPH, W1_AT)
        pos_i, back_i = take(K1 * T).bitcast(I32), take(K1 * T).bitcast(I32)
        top_w = take(K1 * T)
        mix_w = take(T * E1)
        slot_e = take(SLOT_TILES + K1).bitcast(I32)
        b1_t = take(E1 * FB)
        RINGS = place["at"]
        x_in, x_t = [take(D) for _ in range(2)], [take(D) for _ in range(2)]
        w1_ring = [take(W_E) for _ in range(2)]
        h_t = [take(F1) for _ in range(2)]
        y_ring = [take(D) for _ in range(2)]
        scratch(RINGS, W1_AT)
        xs7 = take(B * D)
        slot_idx = take(K1 * B).bitcast(I32)
        scratch(W1_AT)
        w1_all, w2_all = take(E1 * W_E), take(E1 * W_E)
        scratch(W2_AT)
        xn7, xt7 = take(B * D), take(B * D)
        gw, gate_b, b1_raw = take(KD * E1), take(E1), take(P)
        gates, picks, rev = take(T * E1), take(K1 * T * E1), take(E1)
        eq, top_v, first = take(T * E1), take(K1 * T), take(T)
        counts, cum, place_f = take(K1 * T * E1), take(K1 * T * E1), take(K1 * T * E1)
        e_n, e_i, e_tiles, e_cum, e_off = (take(E1) for _ in range(5))
        e_start = take(E1)
        dump, not_node, pos_f = take(K1), take(1), take(K1 * T)
        grid = take((SLOT_TILES + K1) * E1)
        xn7v = xn7.rearrange("p (i k n) -> p i k n", i=B, k=KD)
        xt7v = xt7.rearrange("p (i k n) -> p i k n", i=B, k=KD)
        picks4 = picks.rearrange("p (k t e) -> p k t e", k=K1, e=E1)
        (ld_m, ld_m1, ld_m2, b1_ps, tw_in, tw_exp, picks_done, cnt_ps, pos_done, xs_ready, xs_free) = (
            sem(n) for n in ("ld_m ld_m1 ld_m2 b1_ps tw_in tw_exp picks_done cnt_ps pos_done xs_ready xs_free"
                             ).split())
        moved = gather_done[1]
        MOVED = GROUP_LOOPS * 16
        CALL3 = 3 * LOOPS

        with nc.Block() as block:
            @block.sync
            def _(sp):
                sp.dma_start(gw.rearrange("p (k e) -> p k e", k=KD),
                             L1_ffn_gate_w.rearrange("(k p) e -> p k e", p=P)).then_inc(ld_m, 16)
                sp.dma_start(gate_b, L1_ffn_gate_b.partition_broadcast(P)).then_inc(ld_m, 16)
                sp.dma_start(b1_raw[0:E1 * FB, :], L1_ffn_b1.rearrange("e (f p) -> (e f) p", p=P)).then_inc(ld_m, 16)
                with sp.Fori(0, E1) as e:
                    sp.dma_start(w1_all[:, ds(e * W_E, W_E)].rearrange("p (k f) -> p k f", k=KD),
                                 L1_ffn_w1[ds(e, 1), :, :].rearrange("o (k p) f -> p (o k) f", p=P)).then_inc(ld_m1, 16)
                sp.wait_ge(pos_done, 1)
                with sp.Fori(0, E1) as e:
                    sp.dma_start(w2_all[:, ds(e * W_E, W_E)].rearrange("p (f d) -> p f d", f=FB),
                                 L1_ffn_w2[ds(e, 1), :, :].rearrange("o (f p) d -> p (o f) d", p=P)).then_inc(ld_m2, 16)
                sp.wait_ge(ld_m1, E1 * 16)
                sp.wait_ge(ld_m2, E1 * 16)

            @block.gpsimd
            def _(pool):
                pool.sem_inc(xs_free, 1)
                pool.wait_ge(pos_done, 1)
                with G.loop(LOOPS, 1) as c:
                    G.then(pool.tensor_copy(slot_idx.rearrange("p (k i) -> p k i", k=K1),
                                            pos_i.rearrange("p (k t) -> p k t", k=K1)[:, :, ds(c * B, B)]))
                    for i in range(B):
                        pool.wait_ge(xs_ready, c * B + (i + 1))
                        pool.sem_inc(dma_turn, 1)
                        for k in range(K1):
                            pool.indirect_dma_start(slot_rows, bass.IndirectOffsetOnAxis(
                                ap=slot_idx[:, k * B + i:k * B + i + 1], axis=0), xs7[:, i * D:(i + 1) * D], None
                            ).then_inc(moved[i], 16)
                    for i in range(B):
                        pool.wait_ge(moved[i], c * (16 * K1) + (MOVED + 16 * K1))
                    pool.sem_inc(xs_free, 1)

            @block.scalar
            def _(act):
                ln_root(act)
                act.wait_ge(b1_ps, 1)
                act.copy(b1_t, bank(7, E1 * FB))
                with act.Fori(0, LOOPS) as c:
                    act.wait_ge(tp_done, c + (CALL3 + 2))
                    act.copy(xt7, psA).then_inc(xt_done, 1)
                act.wait_ge(tw_in, 1)
                act.activation(top_v[:, T:], top_v[:, T:], ACT.Exp).then_inc(tw_exp, 1)

            @block.vector
            def _(dve):
                ln_stats(dve)
                def keep_gates(c):
                    dve.wait_ge(lg_ps, c + (LOOPS + 1))
                    dve.tensor_copy(gates[:, ds(c * (B * E1), B * E1)], bank(4, B * E1)).then_inc(lg_sb, 1)

                norm7(dve, 0, CALL3)
                with dve.Fori(0, LOOPS - 1) as c:
                    norm7(dve, c + 1, CALL3)
                    keep_gates(c)
                keep_gates(LOOPS - 1)
                dve.wait_ge(lg_sb, 2 * LOOPS + 1)
                wide = [P, T, E1]
                g3, eq3 = (a.rearrange("p (t e) -> p t e", e=E1) for a in (gates, eq))
                dve.wait_ge(ld_m, 48)
                V.add(dve.tensor_tensor(g3, g3, gate_b.unsqueeze(1).to_broadcast(wide), ALU.add))
                V.then(dve.tensor_scalar(rev, iota[:, 0:E1], -1.0, float(E1), ALU.mult, ALU.add))
                for k in range(K1):
                    best = top_v[:, k * T:(k + 1) * T]
                    V.then(dve.tensor_reduce(best, g3, AX_X, ALU.max))
                    V.then(dve.tensor_tensor(eq3, g3, best.unsqueeze(2).to_broadcast(wide), ALU.is_ge))
                    V.then(dve.tensor_tensor(eq3, eq3, rev.unsqueeze(1).to_broadcast(wide), ALU.mult))
                    V.then(dve.tensor_reduce(first, eq3, AX_X, ALU.max))
                    V.then(dve.tensor_tensor(picks4[:, k], rev.unsqueeze(1).to_broadcast(wide),
                                             first.unsqueeze(2).to_broadcast(wide), ALU.is_equal))
                    if k == 0:
                        V.then(dve.scalar_tensor_tensor(g3, picks4[:, k], -3.0e38, g3, ALU.mult, ALU.add))
                for k in range(K1):
                    V.add(dve.tensor_scalar(picks4[:, k, T - 1, :], picks4[:, k, T - 1, :], rowmask, None, ALU.mult))
                V.settle()
                dve.sem_inc(picks_done, 1)
                dve.tensor_tensor(top_v[:, T:], top_v[:, T:], top_v[:, 0:T], ALU.subtract).then_inc(tw_in, 1)
                dve.wait_ge(tw_exp, 1)
                V.then(dve.tensor_scalar(first, top_v[:, T:], 1.0, None, ALU.add))
                V.then(dve.reciprocal(top_w[:, 0:T], first))
                V.then(dve.tensor_tensor(top_w[:, T:], top_v[:, T:], top_w[:, 0:T], ALU.mult))
                mix3 = mix_w.rearrange("p (t e) -> p t e", e=E1)
                V.add(dve.tensor_tensor(mix3, picks4[:, 0], top_w[:, 0:T].unsqueeze(2).to_broadcast(wide), ALU.mult))
                V.then(dve.tensor_tensor(eq3, picks4[:, 1], top_w[:, T:].unsqueeze(2).to_broadcast(wide), ALU.mult))
                V.add(dve.tensor_tensor(mix3, mix3, eq3, ALU.add))
                dve.wait_ge(cnt_ps, 1)
                by_e = [a.rearrange("p (e k t) -> p k t e", e=E1, k=K1) for a in (counts, cum)]
                for n, (k, t0, t1) in enumerate(HALVES):
                    V.add(dve.tensor_copy(by_e[0][:, k, t0:t1, :],
                                          bank(4 + n, (t1 - t0) * E1).rearrange("p (t e) -> p t e", e=E1)))
                V.settle()
                V.then(dve.tensor_tensor_scan(cum, counts, counts, 0.0, ALU.add, ALU.bypass))
                ends = cum.rearrange("p (e m) -> p e m", e=E1)
                V.then(dve.tensor_copy(e_n, ends[:, :, K1 * T - 1]))
                V.then(dve.tensor_tensor(cum, cum, counts, ALU.subtract))
                V.then(dve.tensor_copy(e_start, ends[:, :, 0]))
                V.then(dve.tensor_tensor(e_n, e_n, e_start, ALU.subtract))
                V.then(dve.tensor_scalar(e_n, e_n, float(P - 1), None, ALU.add))
                V.then(dve.tensor_copy(e_i.bitcast(I32), e_n))
                V.then(dve.tensor_scalar(e_off.bitcast(I32), e_i.bitcast(I32), 7, None, ALU.arith_shift_right))
                V.then(dve.tensor_copy(e_tiles, e_off.bitcast(I32)))
                V.then(dve.tensor_tensor_scan(e_cum, e_tiles, e_tiles, 0.0, ALU.add, ALU.bypass))
                V.then(dve.tensor_tensor(e_off, e_cum, e_tiles, ALU.subtract))
                V.then(dve.scalar_tensor_tensor(e_off, e_off, float(P), e_start, ALU.mult, ALU.subtract))
                V.then(dve.tensor_tensor(ends, ends, e_off.unsqueeze(2).to_broadcast([P, E1, K1 * T]), ALU.add))
                place4 = place_f.rearrange("p (k t e) -> p k t e", k=K1, e=E1)
                for n, (k, t0, t1) in enumerate(HALVES):
                    V.add(dve.tensor_tensor(place4[:, k, t0:t1, :], by_e[1][:, k, t0:t1, :],
                                            bank(n, (t1 - t0) * E1).rearrange("p (t e) -> p t e", e=E1), ALU.add))
                V.settle()
                V.then(dve.tensor_tensor(place_f, place_f, picks, ALU.mult))
                V.then(dve.tensor_reduce(pos_f, place_f.rearrange("p (m e) -> p m e", e=E1), AX_X, ALU.add))
                V.add(dve.tensor_scalar(not_node, rowmask, -1.0, 1.0, ALU.mult, ALU.add))
                for k in range(K1):
                    V.add(dve.tensor_scalar(dump[:, k:k + 1], lane, float(SLOTS + k * P), None, ALU.add))
                V.settle()
                for k in range(K1):
                    at = pos_f[:, k * T + T - 1:k * T + T]
                    V.add(dve.scalar_tensor_tensor(at, dump[:, k:k + 1], not_node, at, ALU.mult, ALU.add))
                V.settle()
                V.then(dve.tensor_copy(pos_i, pos_f))
                V.then(dve.tensor_scalar(pos_f, pos_f, float(SLOTS - 1), None, ALU.min))
                V.add(dve.tensor_copy(back_i, pos_f))
                tiles = [P, SLOT_TILES + K1, E1]
                grid3 = grid.rearrange("p (s e) -> p s e", e=E1)
                V.then(dve.tensor_tensor(grid3, iota[:, 0:SLOT_TILES + K1].unsqueeze(2).to_broadcast(tiles),
                                         e_cum.unsqueeze(1).to_broadcast(tiles), ALU.is_ge))
                V.then(dve.tensor_reduce(cum[:, 0:SLOT_TILES + K1], grid3, AX_X, ALU.add))
                V.then(dve.tensor_scalar(cum[:, 0:SLOT_TILES + K1], cum[:, 0:SLOT_TILES + K1], float(E1 - 1), None,
                                         ALU.min))
                V.then(dve.tensor_copy(slot_e, cum[:, 0:SLOT_TILES + K1]))
                dve.sem_inc(pos_done, 1)
                with dve.Fori(0, LOOPS) as c:
                    dve.wait_ge(xs_free, c + 1)
                    for i in range(B):
                        normalise(dve, xs7[:, i * D:(i + 1) * D], c * B + i).then_inc(xs_ready, 1)

            @block.tensor
            def _(pe):
                pe.wait_ge(ld_m, 48)
                pe.transpose(bank(7, E1 * FB), b1_raw[0:E1 * FB, :], ident[0:E1 * FB, 0:E1 * FB]).then_inc(b1_ps, 1)
                with pe.Fori(0, LOOPS) as c:
                    transpose7(pe, c, CALL3)
                    pe.wait_ge(xt_done, c + (2 * CALL3 + 1))
                    pe.wait_ge(lg_sb, c + (LOOPS + 1))
                    for i in range(B):
                        for k in range(KD):
                            last = pe.matmul(bank(4, E1, i * E1), xt7v[:, i, k, :], gw[:, k * E1:(k + 1) * E1],
                                             start=(k == 0), stop=(k == KD - 1))
                    last.then_inc(lg_ps, 1)
                pe.wait_ge(picks_done, 1)
                for at, m in ((0, tri), (4, ones)):
                    for n, (k, t0, t1) in enumerate(HALVES):
                        last = pe.matmul(bank(at + n, (t1 - t0) * E1), m,
                                         picks4[:, k, t0:t1, :].rearrange("p t e -> p (t e)"), start=True, stop=True)
                last.then_inc(cnt_ps, 1)

        (in_ps, in_done, m1h_ps, h_done, w1_done, m2h_ps, y_done, y_free) = (
            sem(n) for n in "in_ps in_done m1h_ps h_done w1_done m2h_ps y_done y_free".split())
        x_ld = [sem(f"x_ld{b}") for b in range(2)]

        def load_experts(engine, first):
            return nc.values_load_multi_w_load_instructions(
                slot_e[0:1, ds(first, 2)], engines=[engine.engine], min_val=0, max_val=E1 - 1,
                skip_runtime_bounds_check_because="a slot's expert is the least of a count and E1 - 1")[1]

        with nc.Block() as block:
            @block.sync
            def _(sp):
                sp.sem_inc(y_free, 32)
                for b in range(2):
                    sp.dma_start(x_in[b], slot_rows[b * P:(b + 1) * P, :]).then_inc(x_ld[b], 16)
                sp.wait_ge(in_ps, 1)
                sp.dma_start(x_in[0], slot_rows[2 * P:3 * P, :]).then_inc(x_ld[0], 16)
                with sp.Fori(0, SLOT_PAIRS) as j:
                    for b in range(2):
                        s = j * 2 + b
                        sp.wait_ge(in_ps, s + 2)
                        sp.dma_start(x_in[1 - b], slot_rows[ds((s + 3) * P, P), :]).then_inc(x_ld[1 - b], 16)
                        sp.wait_ge(y_done, s + 3)
                        sp.dma_start(slot_out[ds(s * P, P), :], y_ring[b]).then_inc(y_free, 16)
                sp.wait_ge(y_free, SLOT_TILES * 16 + 32)
                sp.wait_ge(x_ld[0], SLOT_PAIRS * 16 + 32)
                sp.wait_ge(x_ld[1], SLOT_PAIRS * 16 + 16)

            @block.scalar
            def _(act):
                with act.Fori(0, SLOT_PAIRS) as j:
                    experts = load_experts(act, j * 2)
                    for b in range(2):
                        s = j * 2 + b
                        for f in range(FB):
                            act.wait_ge(m1h_ps, s * 2 + (f // 2 + 1))
                            act.activation(h_t[b][:, f * P:(f + 1) * P], bank(2 + 2 * b + f // 2, P, f % 2 * P), ACT.Relu,
                                           bias=b1_t[:, ds(experts[b] * FB + f, 1)]).then_inc(h_done, 1)

            @block.vector
            def _(dve):
                def take_in(s, b):
                    dve.wait_ge(in_ps, s + 1)
                    dve.tensor_copy(x_t[b], bank(b, D)).then_inc(in_done, 1)

                def take_w1(expert, b):
                    dve.tensor_copy(w1_ring[b], w1_all[:, ds(expert * W_E, W_E)]).then_inc(w1_done, 1)

                dve.sem_inc(y_done, 2)
                experts = load_experts(dve, 0)
                for b in range(2):
                    take_w1(experts[b], b)
                    take_in(b, b)
                with dve.Fori(0, SLOT_PAIRS) as j:
                    experts = load_experts(dve, j * 2 + 2)
                    for b in range(2):
                        s = j * 2 + b
                        dve.wait_ge(m1h_ps, s * 2 + 2)
                        take_w1(experts[b], b)
                        take_in(s + 2, b)
                        dve.wait_ge(m2h_ps, s + 1)
                        dve.wait_ge(y_free, s * 16 + 16)
                        dve.tensor_copy(y_ring[b], bank(6 + b, D)).then_inc(y_done, 1)

            @block.tensor
            def _(pe):
                def flip(b, nth):
                    pe.wait_ge(x_ld[b], nth * 16 + 16)
                    for k in range(KD):
                        last = pe.transpose(bank(b, P, k * P), x_in[b][:, k * P:(k + 1) * P], ident)
                    last.then_inc(in_ps, 1)

                def hidden(s, b):
                    pe.wait_ge(in_done, s + 1)
                    pe.wait_ge(w1_done, s + 1)
                    for f in range(FB):
                        for k in range(KD):
                            last = pe.matmul(bank(2 + 2 * b + f // 2, P, f % 2 * P),
                                             w1_ring[b][:, k * F1 + f * P:k * F1 + (f + 1) * P],
                                             x_t[b][:, k * P:(k + 1) * P], start=(k == 0), stop=(k == KD - 1))
                        if f % 2:
                            last.then_inc(m1h_ps, 1)

                flip(0, 0)
                flip(1, 0)
                hidden(0, 0)
                with pe.Fori(0, SLOT_PAIRS) as j:
                    experts = load_experts(pe, j * 2)
                    for b in range(2):
                        s = j * 2 + b
                        hidden(s + 1, 1 - b)
                        flip(b, j + 1)
                        pe.wait_ge(y_done, s + 1)
                        for f in range(FB):
                            pe.wait_ge(h_done, s * FB + (f + 1))
                            last = pe.matmul(bank(6 + b, D), h_t[b][:, f * P:(f + 1) * P],
                                             w2_all[:, ds(experts[b] * W_E + f * D, D)], start=(f == 0),
                                             stop=(f == FB - 1))
                        last.then_inc(m2h_ps, 1)

        scratch(RINGS)
        got_k = [[take(D) for _ in range(B)] for _ in range(K1)]
        back_idx = take(K1 * B).bitcast(I32)
        y7, t7 = take(B * D), take(B * D)
        mix7, mix_t = take(B * E1), take(B * P)
        b2_s, gamma_b, beta_b = take(D), take(D), take(D)
        mean7, rstd7 = take(B), take(B)
        (ld_o, back_free, mix_in, mixt_ps, mixt_done, b2_ps, y_sum, out_done, out_st) = (
            sem(n) for n in "ld_o back_free mix_in mixt_ps mixt_done b2_ps y_sum out_done out_st".split())
        NORMS = calls["ln_dve"]

        with nc.Block() as block:
            @block.sync
            def _(sp):
                sp.dma_start(b2_s[0:E1, :], L1_ffn_b2).then_inc(ld_o, 16)
                sp.dma_start(gamma_b, L1_ffn_gamma.partition_broadcast(P)).then_inc(ld_o, 16)
                sp.dma_start(beta_b, L1_ffn_beta.partition_broadcast(P)).then_inc(ld_o, 16)

                def store(c, tiles):
                    sp.dma_start(out[ds(c * (B * P), tiles * P), :].rearrange("(i p) d -> p i d", p=P),
                                 xres[:, ds(c * (B * D), tiles * D)].rearrange("p (i d) -> p i d", d=D)
                                 ).then_inc(out_st, 16)

                with sp.Fori(0, LOOPS - 1) as c:
                    sp.wait_ge(out_done, c + 2)
                    store(c, B)
                sp.wait_ge(out_done, LOOPS + 1)
                store(LOOPS - 1, B - 1)
                sp.dma_start(out[(T - 1) * P:, :], xres[0:TAIL, (T - 1) * D:]).then_inc(out_st, 16)
                sp.wait_ge(out_st, (LOOPS + 1) * 16)

            @block.gpsimd
            def _(pool):
                with G.loop(LOOPS, 1) as c:
                    pool.wait_ge(back_free, c + 1)
                    G.then(pool.tensor_copy(back_idx.rearrange("p (k i) -> p k i", k=K1),
                                            back_i.rearrange("p (k t) -> p k t", k=K1)[:, :, ds(c * B, B)]))
                    pool.sem_inc(dma_turn, 1)
                    for i in range(B):
                        for k in range(K1):
                            pool.indirect_dma_start(got_k[k][i], None, slot_out, bass.IndirectOffsetOnAxis(
                                ap=back_idx[:, k * B + i:k * B + i + 1], axis=0)).then_inc(moved[i], 16)

            @block.scalar
            def _(act):
                with act.Fori(0, LOOPS) as c:
                    act.copy(mix7, mix_w[:, ds(c * (B * E1), B * E1)]).then_inc(mix_in, 1)
                    act.wait_ge(mixt_ps, c + 1)
                    act.copy(mix_t[0:E1, :], ps[0:E1, 0:B * P]).then_inc(mixt_done, 1)
                    root(act, B, c + (NORMS + 1))

            @block.vector
            def _(dve):
                dve.sem_inc(back_free, 1)
                dve.sem_inc(out_done, 1)
                dve.wait_ge(ld_o, 48)
                with V.loop(LOOPS, 14 + 3 * B) as c:
                    dve.wait_ge(out_done, c + 1)
                    for i in range(B):
                        V.add(normalise(dve, y7[:, i * D:(i + 1) * D], c * B + i))
                    V.settle()
                    dve.wait_ge(b2_ps, c + 1)
                    V.then(dve.tensor_tensor(y7, y7, psB, ALU.add))
                    for i in range(B):
                        y = y7[:, i * D:(i + 1) * D]
                        dve.wait_ge(moved[i], c * (16 * K1) + (MOVED + (LOOPS + 1) * 16 * K1))
                        dve.scalar_tensor_tensor(y, got_k[0][i], top_w[:, ds(c * B + i, 1)], y, ALU.mult, ALU.add
                                                 ).then_inc(y_sum, 1)
                    for i in range(B):
                        y = y7[:, i * D:(i + 1) * D]
                        dve.wait_ge(y_sum, c * (2 * B) + B)
                        dve.scalar_tensor_tensor(y, got_k[1][i], top_w[:, ds(c * B + (T + i), 1)], y, ALU.mult, ALU.add
                                                 ).then_inc(y_sum, 1)
                    dve.wait_ge(y_sum, c * (2 * B) + 2 * B)
                    dve.sem_inc(back_free, 1)
                    for i in range(B):
                        V.add(dve.bn_stats(stats[:, i * 6:i * 6 + 6], y7[:, i * D:(i + 1) * D]))
                    V.settle()
                    ln_roots(dve, B, mean7, rstd7, c + (NORMS + 1))
                    for i in range(B):
                        V.add(dve.tensor_scalar(t7[:, i * D:(i + 1) * D], y7[:, i * D:(i + 1) * D], mean7[:, i:i + 1],
                                                rstd7[:, i:i + 1], ALU.subtract, ALU.mult))
                    V.settle()
                    t = t7.rearrange("p (i d) -> p i d", i=B)
                    V.then(dve.tensor_tensor(t, t, gamma_b.unsqueeze(1).to_broadcast([P, B, D]), ALU.mult))
                    V.then(dve.tensor_tensor(t, t, beta_b.unsqueeze(1).to_broadcast([P, B, D]), ALU.add))
                    a = xres[:, ds(c * (B * D), B * D)]
                    dve.tensor_tensor(a, a, t7, ALU.add).then_inc(out_done, 1)

            @block.tensor
            def _(pe):
                pe.wait_ge(ld_o, 48)
                with pe.Fori(0, LOOPS) as c:
                    pe.wait_ge(mix_in, c + 1)
                    for i in range(B):
                        last = pe.transpose(ps[0:E1, i * P:(i + 1) * P], mix7[:, i * E1:(i + 1) * E1], ident)
                    last.then_inc(mixt_ps, 1)
                    pe.wait_ge(mixt_done, c + 1)
                    for i in range(B):
                        last = pe.matmul(half(4, i), mix_t[0:E1, i * P:(i + 1) * P], b2_s[0:E1, :],
                                         start=True, stop=True)
                    last.then_inc(b2_ps, 1)


_INS = ['x', 'src', 'dst', 'edge_weight', 'L0_gnn_W', 'L0_gnn_b', 'L0_mix_Wq', 'L0_mix_Wkv', 'L0_mix_Wproj',
        'L0_mix_bproj', 'L0_ffn_router_w', 'L0_ffn_router_b', 'L0_ffn_W1', 'L0_ffn_b1', 'L0_ffn_W2', 'L0_ffn_b2',
        'L1_gnn_W', 'L1_gnn_a_l', 'L1_gnn_a_r', 'L1_mix_kln_weight', 'L1_mix_kln_bias', 'L1_mix_vln_weight',
        'L1_mix_vln_bias', 'L1_ffn_gate_w', 'L1_ffn_gate_b', 'L1_ffn_w1', 'L1_ffn_b1', 'L1_ffn_w2', 'L1_ffn_b2',
        'L1_ffn_gamma', 'L1_ffn_beta']


def kernel(**inputs):
    import numpy as _np
    import concourse.bacc as _bacc
    from concourse import mybir as _mybir
    from concourse.bass_utils import run_bass_kernel_spmd as _run

    nc = _bacc.Bacc("TRN2", target_bir_lowering=False, num_devices=1)
    arrays, args = {}, []
    for name in _INS:
        a = _np.ascontiguousarray(inputs[name])
        arrays[f"in_{name}"] = a
        args.append(nc.dram_tensor(f"in_{name}", a.shape, _mybir.dt.from_np(a.dtype), kind="ExternalInput").ap())
    out = nc.dram_tensor("out_x", (NODES, D), F32, kind="ExternalOutput").ap()
    gps_two_layers(nc, *args, out)
    r = _run(nc, [arrays], core_ids=[0])
    return r.results[0]["out_x"]
```

```python
from contextlib import ExitStack, contextmanager

import concourse.bass as bass
from concourse import mybir

F32 = mybir.dt.float32
I32 = mybir.dt.int32
U32 = mybir.dt.uint32
BF16 = mybir.dt.bfloat16
ALU = mybir.AluOpType
ACT = mybir.ActivationFunctionType
AX_X = mybir.AxisListType.X
RMAX = bass.bass_isa.ReduceOp.max
ds = bass.ds

P = 128
NODES, D, EDGES = 6250, 256, 100000
T = -(-NODES // P)
NP = T * P
TAIL = NODES - (T - 1) * P
B = 7
LOOPS = T // B
assert LOOPS * B == T
KD = D // P
C = -(-EDGES // P)
EP = C * P
BUCKETS = T + 1
SCAT = 17
SCAT_LOOPS = C // (2 * SCAT)
assert SCAT_LOOPS * 2 * SCAT == C
SCAT_CUTS = (6, 7, 12, 15)
U = 8
HALF_U = U // 2
GROUP_LOOPS = -(-(C + T - 1) // (2 * U))
R = 4
RINGS_OF_R = GROUP_LOOPS * 2 // R
assert RINGS_OF_R * R == GROUP_LOOPS * 2
VT = -(-(GROUP_LOOPS * 2 * U) // P)
NV = VT * P
HC = 32
GH, GF = 4, 64
ROW1 = D + 2 * GH
ACC_W = D + GH
E0, H0 = 32, 64
HB = E0 * H0 // P
HALF = B * P // 2
E1, F1, K1 = 16, 512, 2
FB = F1 // P
SLOT_TILES = K1 * T + E1
SLOTS = SLOT_TILES * P
SPARE = K1 + 1
Q0 = 4
BATCHES0 = 2 * -(-(T + E0) // (2 * Q0))
LN_EPS, KV_EPS, D_MIN = 1e-5, 1e-5, 1e-6
ALPHA = 0.2
LIFT = 60.0
OTHER = 4096.0
DEN_MIN = 1e-30
PARTS = 3


class Steps:

    def __init__(self, engine, sem):
        self.engine, self.sem, self.n, self.i, self.per = engine, sem, 0, None, 0

    def add(self, ins):
        ins.then_inc(self.sem, 1)
        self.n += 1

    def settle(self):
        self.engine.wait_ge(self.sem, self.n if self.i is None else self.n + self.i * self.per)

    def then(self, ins):
        self.add(ins)
        self.settle()

    @contextmanager
    def loop(self, count, per):
        first = self.n
        with self.engine.Fori(0, count) as i:
            self.i, self.per = i, per
            yield i
            assert self.n - first == per, (self.n - first, per)
        self.i, self.n = None, first + per * count


def gps_two_layers(nc, x, src, dst, edge_weight, L0_gnn_W, L0_gnn_b, L0_mix_Wq, L0_mix_Wkv, L0_mix_Wproj,
                   L0_mix_bproj, L0_ffn_router_w, L0_ffn_router_b, L0_ffn_W1, L0_ffn_b1, L0_ffn_W2, L0_ffn_b2,
                   L1_gnn_W, L1_gnn_a_l, L1_gnn_a_r, L1_mix_kln_weight, L1_mix_kln_bias, L1_mix_vln_weight,
                   L1_mix_vln_bias, L1_ffn_gate_w, L1_ffn_gate_b, L1_ffn_w1, L1_ffn_b1, L1_ffn_w2, L1_ffn_b2,
                   L1_ffn_gamma, L1_ffn_beta, out):
    with ExitStack() as ctx:
        def sem(name):
            return ctx.enter_context(nc.semaphore(name))

        def dram(name, shape, dt=F32):
            return nc.dram_tensor(name, shape, dt, kind="Internal").ap()

        h0_table = dram("h0_table", (NP, D))
        h1_table = dram("h1_table", (NP, ROW1))
        edges_by = [dram("edges_by_dst", (EP, 4)), dram("edges_by_src", (EP, 4))]
        visit_tiles = dram("visit_tiles", (2, NV), I32)
        slot_rows = dram("slot_rows", (SLOTS + SPARE * P, D))
        slot_out = dram("slot_out", (SLOTS, D))

        arena_words = 53200
        arena = ctx.enter_context(nc.sbuf_tensor("arena", [P, arena_words], F32))
        place = {"at": 0}

        def take(words):
            at = place["at"]
            place["at"] = at + words
            assert place["at"] <= place.get("end", arena_words), place
            return arena[:, at:at + words]

        def scratch(at, end=arena_words):
            place["at"], place["end"] = at, end

        xres = take(T * D)
        ident, tri, ones, iota = take(P), take(P), take(P), take(P)
        zeros = take(P)
        blk = take(P)
        lane, rowmask = take(1), take(1)
        stats, mean, rstd, lnt = take(6 * T), take(T), take(T), take(4 * T)
        tot = [take(BUCKETS), take(BUCKETS)]
        base = take(BUCKETS)
        unsorted_f, unsorted = take(2), take(1).bitcast(I32)
        cnt = [take(2 * BUCKETS), take(2 * BUCKETS)]
        GRAPH = place["at"]
        rl_all = take(BUCKETS * 2 * GH)
        v_loc, v_w = take(NV), take(NV)
        v_idx = take(NV).bitcast(I32)
        tile_row = take(NV).bitcast(I32)
        XNT = place["at"]
        xnT = take(KD * NP)
        ACC = place["at"]
        acc = take(BUCKETS * ACC_W)
        src_f, dst_f, pos_src = take(C), take(C), take(C)
        w_f, pos_dst = take(C), take(C)
        FREE = place["at"]
        xnT3 = xnT.rearrange("p (k n) -> p k n", k=KD)
        acc3 = acc.rearrange("p (t w) -> p t w", w=ACC_W)

        ps = ctx.enter_context(nc.psum_tensor("ps", [P, 8 * 512], F32))

        def bank(b, width=512, at=0):
            return ps[:, b * 512 + at:b * 512 + at + width]

        def half(b, i, width=D):
            return ps[:, b * 512 + i * 256:b * 512 + i * 256 + width]

        V, G = Steps(nc.vector, sem("dve_step")), Steps(nc.gpsimd, sem("pool_step"))
        V_SORT, G_SORT = Steps(nc.vector, sem("dve_sort_step")), Steps(nc.gpsimd, sem("pool_sort_step"))

        var_ready, std_ready = sem("var_ready"), sem("std_ready")
        calls = {"ln_dve": 0, "ln_act": 0}

        def ln_stats(dve):
            with V.loop(LOOPS, B) as c:
                for i in range(B):
                    V.add(dve.bn_stats(stats[:, ds((c * B + i) * 6, 6)], xres[:, ds((c * B + i) * D, D)]))
            V.settle()
            ln_roots(dve, T, mean, rstd, calls["ln_dve"] + 1)
            calls["ln_dve"] += 1

        def ln_roots(dve, tiles, mean, rstd, nth):
            s = stats[:, 0:6 * tiles].rearrange("p (t s) -> p t s", s=6)
            a, b, c, d = (lnt[:, i * T:i * T + tiles] for i in range(4))
            V.add(dve.tensor_tensor(a, s[:, :, 1], s[:, :, 4], ALU.add))
            V.add(dve.tensor_tensor(b, s[:, :, 1], s[:, :, 4], ALU.subtract))
            V.then(dve.tensor_tensor(c, s[:, :, 2], s[:, :, 5], ALU.add))
            V.add(dve.tensor_scalar(mean, a, 0.5, None, ALU.mult))
            V.then(dve.tensor_tensor(d, b, b, ALU.mult))
            V.then(dve.scalar_tensor_tensor(b, d, D / 4, c, ALU.mult, ALU.add))
            dve.tensor_scalar(a, b, 1.0 / D, LN_EPS, ALU.mult, ALU.add).then_inc(var_ready, 1)
            dve.wait_ge(std_ready, nth)
            V.then(dve.reciprocal(c, b))
            V.then(dve.tensor_tensor(d, c, c, ALU.mult))
            V.then(dve.tensor_tensor(b, d, a, ALU.mult))
            V.then(dve.tensor_scalar(d, b, -0.5, 1.5, ALU.mult, ALU.add))
            V.then(dve.tensor_tensor(rstd, d, c, ALU.mult))

        def ln_root(act):
            calls["ln_act"] += 1
            root(act, T, calls["ln_act"])

        def root(act, tiles, nth):
            act.wait_ge(var_ready, nth)
            act.activation(lnt[:, T:T + tiles], lnt[:, 0:tiles], ACT.Sqrt).then_inc(std_ready, 1)

        def normalise(dve, to, t):
            return dve.tensor_scalar(to, xres[:, ds(t * D, D)], mean[:, ds(t, 1)], rstd[:, ds(t, 1)],
                                     ALU.subtract, ALU.mult)

        tot_ready, base_ps = sem("tot_ready"), sem("base_ps")

        def rank_keys(dve, keys, temps):
            key_t, eq = temps[0:2]
            V.then(dve.tensor_copy(key_t.bitcast(I32), keys))
            V.then(dve.tensor_scalar(eq.bitcast(I32), key_t.bitcast(I32), 7, None, ALU.arith_shift_right))
            V.then(dve.tensor_copy(key_t, eq.bitcast(I32)))

        def rank_counts(dve, steps, key_t, eqs, counts):
            n = len(eqs)
            assert BUCKETS % n == 0
            with steps.loop(BUCKETS // n, 2 * n) as b:
                for i, eq in enumerate(eqs):
                    steps.add(dve.tensor_scalar(eq, key_t, iota[:, ds(b * n + i, 1)], None, ALU.is_equal))
                steps.settle()
                for i, eq in enumerate(eqs):
                    steps.add(dve.tensor_reduce(counts[:, ds(b * n + i, 1)], eq, AX_X, ALU.add))
                steps.settle()

        def rank_bases(dve, nth, order):
            dve.sem_inc(tot_ready, 1)
            dve.wait_ge(base_ps, nth)
            count, cum = cnt[order][:, 0:BUCKETS], cnt[order][:, BUCKETS:]
            V.then(dve.tensor_copy(count, bank(7, BUCKETS, 64)))
            V.then(dve.tensor_tensor_scan(cum, count, count, 0.0, ALU.add, ALU.bypass))
            V.then(dve.tensor_tensor(base, cum, count, ALU.subtract))
            V.then(dve.scalar_tensor_tensor(base, base, -1.0, bank(7, BUCKETS), ALU.add, ALU.add))

        def rank_step(dve, b, step, pos, temps):
            key_t, eq, scan, part = temps
            if step == 0:
                V_SORT.then(dve.tensor_scalar(eq, key_t, iota[:, ds(b, 1)], None, ALU.is_equal))
            elif step == 1:
                V_SORT.then(dve.tensor_tensor_scan(scan, eq, eq, 0.0, ALU.add, ALU.bypass))
            elif step == 2:
                V_SORT.then(dve.scalar_tensor_tensor(part, scan, base[:, ds(b, 1)], eq, ALU.add, ALU.mult))
            else:
                V_SORT.then(dve.tensor_tensor(pos, pos, part, ALU.add))

        def rank_sums(pe, nth, order):
            pe.wait_ge(tot_ready, nth)
            pe.matmul(bank(7, BUCKETS), tri, tot[order], start=True, stop=True)
            pe.matmul(bank(7, BUCKETS, 64), ones, tot[order], start=True, stop=True).then_inc(base_ps, 1)

        scat_done = [[sem(f"scat{c}_done{b}") for b in range(2)] for c in range(2)]
        dma_turn = sem("dma_turn")

        class Scatter:

            def __init__(self, pool, steps, call, pos, fields, ring, begun=False):
                self.pool, self.steps, self.call, self.pos, self.fields = pool, steps, call, pos, fields
                self.offs = ring[:, 0:2 * SCAT].bitcast(I32).rearrange("p (b s) -> p b s", b=2)
                self.load = ring[:, 2 * SCAT:10 * SCAT].rearrange("p (b s f) -> p b s f", b=2, s=SCAT)
                steps.then(pool.memset(ring[:, 2 * SCAT:10 * SCAT], 0.0))
                if not begun:
                    for b in range(2):
                        self.send(b, b * SCAT)

            def send(self, b, first):
                pool, steps = self.pool, self.steps
                steps.add(pool.tensor_copy(self.offs[:, b, :], self.pos[:, ds(first, SCAT)]))
                for f, field in enumerate(self.fields):
                    steps.add(pool.tensor_copy(self.load[:, b, :, f], field[:, ds(first, SCAT)]))
                steps.settle()
                pool.sem_inc(dma_turn, 1)
                for s in range(SCAT):
                    pool.indirect_dma_start(edges_by[self.call],
                                            bass.IndirectOffsetOnAxis(ap=self.offs[:, b, s:s + 1], axis=0),
                                            self.load[:, b, s, :], None).then_inc(scat_done[self.call][b], 16)

            def go_on(self, first, count):
                with self.steps.loop(count, 2 * (1 + len(self.fields))) as i:
                    for b in range(2):
                        self.pool.wait_ge(scat_done[self.call][b], i * (16 * SCAT) + (first + 1) * (16 * SCAT))
                        self.send(b, i * (2 * SCAT) + ((first + 1) * (2 * SCAT) + b * SCAT))

            def end(self, loops=SCAT_LOOPS):
                for b in range(2):
                    self.pool.wait_ge(scat_done[self.call][b], loops * 16 * SCAT)

        gather_done = [sem(f"gather{n}_done") for n in range(U)]
        moved = gather_done[0:B]
        TURNS = -(-LOOPS // 2), LOOPS // 2

        def moved_before(layer, i):
            return GROUP_LOOPS * 2 * 16 + (layer and fetched0(i) + (RINGS_OF_R * U * 16 if i < R else 0))

        def fetched0(i):
            return TURNS[i % 2] * 16 * B if i < 4 else 0

        picks_done, cnt_ps, pos_done, xs_ready, xs_free = (
            sem(n) for n in "picks_done cnt_ps pos_done xs_ready xs_free".split())

        def choice_parts(K, E):
            per = 4 // K
            cuts = [T * n // per for n in range(per + 1)]
            return [(k, a, b) for k in range(K) for a, b in zip(cuts, cuts[1:])]

        def choice_sums(pe, nth, K, E, picks):
            pe.wait_ge(picks_done, nth)
            for at, m in ((0, tri), (4, ones)):
                for n, (k, t0, t1) in enumerate(choice_parts(K, E)):
                    last = pe.matmul(bank(at + n, (t1 - t0) * E), m,
                                     picks[:, (k * T + t0) * E:(k * T + t1) * E], start=True, stop=True)
            last.then_inc(cnt_ps, 1)

        def choice_memory(K, E):
            return ({n: take(K * T * E) for n in ("counts", "cum", "place")}
                    | {n: take(E) for n in ("n", "i", "tiles", "cum_tiles", "off", "start")}
                    | {n: take(w) for n, w in (("dump", K), ("not_node", 1), ("pos", K * T))})

        def place_choices(dve, nth, K, E, picks, m, slot_tiles, pos_i, back_i, slot_e):
            dve.wait_ge(cnt_ps, nth)
            parts = choice_parts(K, E)
            counts, cum, place = m["counts"], m["cum"], m["place"]
            by_e = [a.rearrange("p (e k t) -> p k t e", e=E, k=K) for a in (counts, cum)]
            for n, (k, t0, t1) in enumerate(parts):
                V.add(dve.tensor_copy(by_e[0][:, k, t0:t1, :],
                                      bank(4 + n, (t1 - t0) * E).rearrange("p (t e) -> p t e", e=E)))
            V.settle()
            V.then(dve.tensor_tensor_scan(cum, counts, counts, 0.0, ALU.add, ALU.bypass))
            ends = cum.rearrange("p (e m) -> p e m", e=E)
            V.then(dve.tensor_copy(m["n"], ends[:, :, K * T - 1]))
            V.then(dve.tensor_tensor(cum, cum, counts, ALU.subtract))
            V.then(dve.tensor_copy(m["start"], ends[:, :, 0]))
            V.then(dve.tensor_tensor(m["n"], m["n"], m["start"], ALU.subtract))
            V.then(dve.tensor_scalar(m["n"], m["n"], float(P - 1), None, ALU.add))
            V.then(dve.tensor_copy(m["i"].bitcast(I32), m["n"]))
            V.then(dve.tensor_scalar(m["off"].bitcast(I32), m["i"].bitcast(I32), 7, None, ALU.arith_shift_right))
            V.then(dve.tensor_copy(m["tiles"], m["off"].bitcast(I32)))
            V.then(dve.tensor_tensor_scan(m["cum_tiles"], m["tiles"], m["tiles"], 0.0, ALU.add, ALU.bypass))
            V.then(dve.tensor_tensor(m["off"], m["cum_tiles"], m["tiles"], ALU.subtract))
            V.then(dve.scalar_tensor_tensor(m["off"], m["off"], float(P), m["start"], ALU.mult, ALU.subtract))
            V.then(dve.tensor_tensor(ends, ends, m["off"].unsqueeze(2).to_broadcast([P, E, K * T]), ALU.add))
            place4 = place.rearrange("p (k t e) -> p k t e", k=K, e=E)
            for n, (k, t0, t1) in enumerate(parts):
                V.add(dve.tensor_tensor(place4[:, k, t0:t1, :], by_e[1][:, k, t0:t1, :],
                                        bank(n, (t1 - t0) * E).rearrange("p (t e) -> p t e", e=E), ALU.add))
            V.settle()
            V.then(dve.tensor_tensor(place, place, picks, ALU.mult))
            V.then(dve.tensor_reduce(m["pos"], place.rearrange("p (m e) -> p m e", e=E), AX_X, ALU.add))
            V.add(dve.tensor_scalar(m["not_node"], rowmask, -1.0, 1.0, ALU.mult, ALU.add))
            for k in range(K):
                V.add(dve.tensor_scalar(m["dump"][:, k:k + 1], lane, float(SLOTS + k * P), None, ALU.add))
            V.settle()
            for k in range(K):
                at = m["pos"][:, k * T + T - 1:k * T + T]
                V.add(dve.scalar_tensor_tensor(at, m["dump"][:, k:k + 1], m["not_node"], at, ALU.mult, ALU.add))
            V.settle()
            V.then(dve.tensor_copy(pos_i, m["pos"]))
            V.then(dve.tensor_scalar(m["pos"], m["pos"], float(slot_tiles * P - 1), None, ALU.min))
            V.add(dve.tensor_copy(back_i, m["pos"]))
            n = slot_e.shape[1]
            tiles, of = [P, min(n, P), E], place[:, 0:n]
            for s0 in range(0, n, T):
                s1 = min(s0 + T, n)
                grid = counts[:, 0:(s1 - s0) * E].rearrange("p (s e) -> p s e", e=E)
                V.then(dve.tensor_tensor(grid, iota[:, s0:s1].unsqueeze(2).to_broadcast([P, s1 - s0, E]),
                                         m["cum_tiles"].unsqueeze(1).to_broadcast([P, s1 - s0, E]), ALU.is_ge))
                V.then(dve.tensor_reduce(of[:, s0:s1], grid, AX_X, ALU.add))
            V.then(dve.tensor_scalar(of, of, float(E - 1), None, ALU.min))
            V.then(dve.tensor_copy(slot_e, of))
            dve.sem_inc(pos_done, 1)

        assert LOOPS % 2 == 1

        def scatter_rows(pool, layer, K, pos_i, idx, rows):
            def group(j, b):
                c = j * 2 + b
                G.then(pool.tensor_copy(idx[b].rearrange("p (k i) -> p k i", k=K),
                                        pos_i.rearrange("p (k t) -> p k t", k=K)[:, :, ds(c * B, B)]))
                for i in range(B):
                    pool.wait_ge(xs_ready, c * B + (layer * T + i + 1))
                    pool.sem_inc(dma_turn, 1)
                    for k in range(K):
                        pool.indirect_dma_start(slot_rows, bass.IndirectOffsetOnAxis(
                            ap=idx[b][:, k * B + i:k * B + i + 1], axis=0), rows[b][:, i * D:(i + 1) * D], None
                        ).then_inc(moved[b], 16)
                pool.wait_ge(moved[1 - b], (j + b) * (16 * K * B) + moved_before(layer, 1 - b))
                pool.sem_inc(xs_free, 1)

            pool.wait_ge(pos_done, layer + 1)
            with G.loop(LOOPS // 2, 2) as j:
                for b in range(2):
                    group(j, b)
            group(LOOPS // 2, 0)
            pool.wait_ge(moved[0], TURNS[0] * 16 * K * B + moved_before(layer, 0))

        def rows_to_scatter(dve, layer, rows):
            def group(c, b):
                dve.wait_ge(xs_free, c + (layer * LOOPS + 1))
                for i in range(B):
                    normalise(dve, rows[b][:, i * D:(i + 1) * D], c * B + i).then_inc(xs_ready, 1)

            with dve.Fori(0, LOOPS // 2) as j:
                for b in range(2):
                    group(j * 2 + b, b)
            group(LOOPS - 1, 0)

        def fetch_rows(pool, tiles, K, back_i, idx, got, free, done):
            def group(c, b):
                pool.wait_ge(free, c + 1)
                G.then(pool.tensor_copy(idx[b].rearrange("p (k i) -> p k i", k=K),
                                        back_i.rearrange("p (k t) -> p k t", k=K)[:, :, ds(c * B, B)]))
                pool.sem_inc(dma_turn, 1)
                for i in range(B):
                    for k in range(K):
                        pool.indirect_dma_start(got[b][k][i], None, slot_out[0:tiles * P, :],
                                                bass.IndirectOffsetOnAxis(
                                                    ap=idx[b][:, k * B + i:k * B + i + 1], axis=0)
                                                ).then_inc(done[b][i], 16)

            with G.loop(LOOPS // 2, 2) as j:
                for b in range(2):
                    group(j * 2 + b, b)
            group(LOOPS - 1, 0)

        vis_done, vis_rows, vis_cols, vis_ps, vis_tile, vis_out, vis_back = (sem(n) for n in (
            "vis_done", "vis_rows", "vis_cols", "vis_ps", "vis_tile", "vis_out", "vis_back"))

        def visit_views():
            v = {n: take(w) for n, w in (("grid", VT * T), ("tmp", 8 * T), ("vid", VT), ("tile", VT),
                                         ("chunk", VT), ("rows", VT * 4 * P), ("cols", VT * 3 * P))}
            v.update({n: take(VT).bitcast(I32) for n in ("chunk_i", "tile_i", "vid_i")})
            return v

        def visits_dve(dve, call, v):
            count, cum = cnt[call][:, 0:T], cnt[call][:, BUCKETS:BUCKETS + T]
            t = [v["tmp"][:, i * T:(i + 1) * T] for i in range(8)]
            ti = [a.bitcast(I32) for a in t]
            V.add(dve.tensor_tensor(t[0], cum, count, ALU.subtract))
            V.then(dve.tensor_scalar(t[1], cum, float(P - 1), None, ALU.add))
            V.add(dve.tensor_copy(ti[2], t[0]))
            V.then(dve.tensor_copy(ti[3], t[1]))
            V.add(dve.tensor_scalar(ti[4], ti[2], 7, None, ALU.arith_shift_right))
            V.then(dve.tensor_scalar(ti[5], ti[3], 7, None, ALU.arith_shift_right))
            V.add(dve.tensor_copy(t[0], ti[4]))
            V.then(dve.tensor_copy(t[1], ti[5]))
            V.add(dve.tensor_scalar(t[2], count, 0.0, None, ALU.is_gt))
            V.then(dve.tensor_tensor(t[3], t[1], t[0], ALU.subtract))
            V.then(dve.tensor_tensor(t[3], t[3], t[2], ALU.mult))
            V.then(dve.tensor_tensor_scan(t[4], t[3], t[3], 0.0, ALU.add, ALU.bypass))
            V.then(dve.tensor_tensor(t[5], t[4], t[3], ALU.subtract))
            V.add(dve.memset(t[7], 0.0))
            V.then(dve.tensor_tensor(t[6], t[0], t[5], ALU.subtract))
            V.add(dve.tensor_tensor(t[7][:, 0:T - 1], t[6][:, 1:T], t[6][:, 0:T - 1], ALU.subtract))
            dve.wait_ge(vis_back, call + 1)
            V.then(dve.tensor_copy(v["vid"], v["vid_i"]))
            grid = v["grid"].rearrange("p (v t) -> p v t", t=T)
            V.then(dve.tensor_tensor(grid, v["vid"].unsqueeze(2).to_broadcast([P, VT, T]),
                                     t[4].unsqueeze(1).to_broadcast([P, VT, T]), ALU.is_ge))
            V.then(dve.tensor_reduce(v["tile"], grid, AX_X, ALU.add))
            V.then(dve.tensor_tensor(grid, grid, t[7].unsqueeze(1).to_broadcast([P, VT, T]), ALU.mult))
            V.then(dve.tensor_reduce(v["chunk"], grid, AX_X, ALU.add))
            V.then(dve.tensor_tensor(v["chunk"], v["chunk"], v["vid"], ALU.add))
            V.then(dve.tensor_scalar(v["chunk"], v["chunk"], t[6][:, 0:1], float(C - 1), ALU.add, ALU.min))
            dve.tensor_copy(v["tile_i"], v["tile"]).then_inc(vis_tile, 1)
            dve.tensor_copy(v["chunk_i"], v["chunk"]).then_inc(vis_done, 1)
            V.then(dve.tensor_scalar(v["tile"], v["tile"], float(P), None, ALU.mult))
            dve.wait_ge(vis_rows, (call + 1) * VT * 16)
            cols = v["cols"].rearrange("p (v f e) -> p v f e", v=VT, f=3)
            got = v["rows"].rearrange("p (v e f) -> p v f e", v=VT, f=4)
            for j in range(VT):
                dve.tensor_copy(cols[:, j, 0:3:2, :], got[:, j, 0:3:2, :]).then_inc(vis_cols, 1)
                dve.tensor_scalar(cols[:, j, 1, :], got[:, j, 1, :], v["tile"][:, j:j + 1], None,
                                  ALU.subtract).then_inc(vis_cols, 1)
            for j in range(VT):
                dve.wait_ge(vis_ps, call * VT + j + 1)
                got = bank(j, 3 * P)
                V.add(dve.tensor_scalar(v_idx[:, j * P:(j + 1) * P], got[:, 0:P], float(NP - 1), None, ALU.min))
                V.add(dve.tensor_copy(v_loc[:, j * P:(j + 1) * P], got[:, P:2 * P]))
                V.add(dve.tensor_copy(v_w[:, j * P:(j + 1) * P], got[:, 2 * P:]))

        def visits_pool(pool, call, v):
            pool.iota(v["vid_i"], [[P, VT]], base=0, channel_multiplier=1).then_inc(vis_back, 1)
            pool.wait_ge(vis_done, call + 1)
            table = edges_by[call].rearrange("(c e) f -> c (e f)", e=P)
            for j in range(VT):
                pool.indirect_dma_start(v["rows"][:, j * 4 * P:(j + 1) * 4 * P], None, table,
                                        bass.IndirectOffsetOnAxis(ap=v["chunk_i"][:, j:j + 1], axis=0)
                                        ).then_inc(vis_rows, 16)

        def visits_pe(pe, call, v):
            cols = v["cols"].rearrange("p (v f e) -> p v f e", v=VT, f=3)
            for j in range(VT):
                pe.wait_ge(vis_cols, (call * VT + j + 1) * 2)
                for f in range(3):
                    last = pe.transpose(bank(j, P, f * P), cols[:, j, f, :], ident)
                last.then_inc(vis_ps, 1)

        def visits_sync(sp, call, v):
            sp.wait_ge(vis_tile, call + 1)
            sp.dma_start(visit_tiles[call].rearrange("(v p) -> p v", p=P), v["tile_i"],
                         allow_slow_non_contiguous=True).then_inc(vis_out, 16)
            sp.wait_ge(vis_out, 16 * (2 * call + 1))
            sp.dma_start(tile_row[0:1, :], visit_tiles[call].rearrange("(o v) -> o v", o=1)).then_inc(vis_out, 16)
            sp.wait_ge(vis_out, 16 * (2 * call + 2))

        z_x, z_e, ld_x, ld_e, kc, zero_done, z_slots = (sem(n) for n in "z_x z_e ld_x ld_e kc zero_done z_slots".split())
        scratch(FREE)
        temps = [take(C) for _ in range(4)]
        iota_i, lane_i, shift_i, shift_f = (take(n) for n in (P, 1, P + 1, P + 1))
        scratch(ACC, FREE)
        inter = take(4 * C)
        src_temps = [take(C) for _ in range(6)]
        inter_done, edges_out, sort_in, sort_ps, unsorted_done = (
            sem(n) for n in "inter_done edges_out sort_in sort_ps unsorted_done".split())
        iota_i, lane_i, shift_i = (a.bitcast(I32) for a in (iota_i, lane_i, shift_i))

        def load_edges(sp, to, a):
            full, at = EDGES // C, 0
            for n in (full // 16 * 16, full % 16):
                sp.dma_start(to[at:at + n, :], a[at * C:(at + n) * C].rearrange("(p c) -> p c", c=C)).then_inc(ld_e, 16)
                at += n
            sp.dma_start(to[full:full + 1, 0:EDGES - full * C],
                         a[full * C:EDGES].rearrange("(o c) -> o c", o=1)).then_inc(ld_e, 16)

        with nc.Block() as block:
            @block.sync
            def _(sp):
                sp.wait_ge(z_e, 3)
                load_edges(sp, dst_f.bitcast(I32), dst)
                load_edges(sp, src_f.bitcast(I32), src)
                load_edges(sp, w_f, edge_weight)
                sp.wait_ge(z_x, 1)
                sp.dma_start(xres[:, 0:(T - 1) * D].rearrange("p (t d) -> p t d", d=D),
                             x[0:(T - 1) * P, :].rearrange("(t p) d -> p t d", p=P)).then_inc(ld_x, 16)
                sp.dma_start(xres[0:TAIL, (T - 1) * D:], x[(T - 1) * P:, :]).then_inc(ld_x, 16)
                sp.wait_ge(inter_done, 1)
                sp.dma_start(edges_by[0].rearrange("(p c) f -> p (c f)", p=P), inter).then_inc(edges_out, 16)
                sp.wait_ge(zero_done, 1)
                tiles = SLOT_TILES + SPARE
                sp.dma_start(slot_rows.rearrange("(p t) (k d) -> p (t k) d", p=P, k=KD),
                             zeros.unsqueeze(1).to_broadcast([P, tiles * KD, P])).then_inc(z_slots, 16)
                sp.wait_ge(ld_x, 32)
                sp.wait_ge(z_slots, 16)
                sp.wait_ge(edges_out, 16)

            @block.gpsimd
            def _(pool):
                G.add(pool.memset(ident, 0.0))
                G.add(pool.memset(tri, 1.0))
                pool.iota(iota_i, [[1, P]], base=0, channel_multiplier=0).then_inc(kc, 1)
                pool.iota(lane_i, [[0, 1]], base=0, channel_multiplier=1).then_inc(kc, 1)
                G.settle()
                pool.affine_select(out=ident, in_=ident, compare_op=ALU.not_equal, fill=1.0, base=0,
                                   pattern=[[-1, P]], channel_multiplier=1).then_inc(kc, 1)
                pool.affine_select(out=tri, in_=tri, compare_op=ALU.is_gt, fill=0.0, base=0,
                                   pattern=[[1, P]], channel_multiplier=-1).then_inc(kc, 1)

            @block.vector
            def _(dve):
                dve.memset(dst_f.bitcast(I32), NP).then_inc(z_e, 1)
                dve.memset(src_f.bitcast(I32), NP).then_inc(z_e, 1)
                dve.memset(w_f, 0.0).then_inc(z_e, 1)
                dve.memset(xres[:, (T - 1) * D:], 0.0).then_inc(z_x, 1)
                V.add(dve.memset(ones, 1.0))
                dve.memset(zeros, 0.0).then_inc(zero_done, 1)
                dve.wait_ge(kc, 4)
                V.add(dve.tensor_copy(iota, iota_i))
                V.add(dve.tensor_copy(lane, lane_i))
                V.add(dve.tensor_scalar(shift_i[:, 0:P], iota_i, 5, None, ALU.arith_shift_right))
                V.then(dve.tensor_scalar(shift_i[:, P:], lane_i, 5, None, ALU.arith_shift_right))
                V.add(dve.tensor_scalar(rowmask, lane, float(TAIL), None, ALU.is_lt))
                V.then(dve.tensor_copy(shift_f, shift_i))
                V.then(dve.tensor_scalar(blk, shift_f[:, 0:P], shift_f[:, P:], None, ALU.is_equal))
                dve.wait_ge(ld_e, 9 * 16)
                for a in (dst_f, src_f):
                    V.then(dve.tensor_copy(temps[0], a.bitcast(I32)))
                    V.then(dve.tensor_copy(a, temps[0]))
                rows4 = inter.rearrange("p (c f) -> p c f", f=4)
                for f, a in enumerate((src_f, dst_f, w_f)):
                    V.add(dve.tensor_copy(rows4[:, :, f], a))
                V.then(dve.memset(rows4[:, :, 3], 0.0))
                dve.sem_inc(inter_done, 1)
                rank_keys(dve, dst_f, temps)
                key_t, eq = temps[0], temps[1]
                dve.memset(unsorted_f, 0.0).then_inc(sort_in, 1)
                V.then(dve.tensor_tensor(eq[:, 1:], key_t[:, 1:], key_t[:, 0:C - 1], ALU.is_lt))
                dve.wait_ge(sort_ps, 1)
                V.add(dve.tensor_reduce(unsorted_f[:, 0:1], eq[:, 1:], AX_X, ALU.max))
                V.add(dve.tensor_tensor(unsorted_f[0:P - 1, 1:2], ps[0:P - 1, 0:1], key_t[0:P - 1, C - 1:], ALU.is_lt))
                V.settle()
                dve.sem_inc(sort_in, 1)
                dve.wait_ge(sort_ps, 2)
                V.then(dve.tensor_reduce(unsorted_f[:, 0:1], bank(1, 2), AX_X, ALU.add))
                V.then(dve.tensor_copy(unsorted, unsorted_f[:, 0:1]))
                dve.sem_inc(unsorted_done, 1)
                V.add(dve.memset(tot[0], 0.0))
                V.add(dve.memset(pos_dst, 0.0))
                V.then(dve.memset(pos_src, 0.0))
                with dve.If(dve.value_load(unsorted[0:1, 0:1], min_val=0, max_val=2 * P) > 0):
                    rank_counts(dve, V_SORT, temps[0], src_temps[1:], tot[0])
                rank_bases(dve, 1, 0)
                with dve.If(dve.value_load(unsorted[0:1, 0:1], min_val=0, max_val=2 * P) > 0):
                    with V_SORT.loop(BUCKETS, 4) as b:
                        for step in range(4):
                            rank_step(dve, b, step, pos_dst, temps)
                rank_keys(dve, src_f, src_temps)
                rank_counts(dve, V, src_temps[0], src_temps[1:], tot[1])
                rank_bases(dve, 2, 1)

            @block.tensor
            def _(pe):
                pe.wait_ge(kc, 4)
                pe.wait_ge(sort_in, 1)
                pe.matmul(ps[0:P - 1, 0:1], ident[:, 1:], temps[0][:, 0:1], start=True, stop=True).then_inc(sort_ps, 1)
                pe.wait_ge(sort_in, 2)
                pe.matmul(bank(1, 2), ones, unsorted_f, start=True, stop=True).then_inc(sort_ps, 1)
                rank_sums(pe, 1, 0)
                rank_sums(pe, 2, 1)

        scratch(ACC, ACC + BUCKETS * ACC_W)
        w0 = take(KD * D)
        RAW = place["at"]
        wq_r, wkv_r, wp_r = (take(n * D) for n in (KD, 2 * KD, KD))
        wqT, wkvT, wpT = (take(n * D) for n in (KD, 2 * KD, KD))
        xn7 = take(B * D)
        xt7 = take(B * D)
        ring_a, ring_b = take(B * D), take(B * D)
        key_t = take(C)
        scratch(FREE)
        h7 = take(B * D)
        v7 = take(B * KD * (P + 1))
        scat_ring = take(10 * SCAT)
        ctx_m, ctx_t, ksum, ksum_b, kv_out = take(KD * P), take(KD * P), take(KD), take(KD * P), take(KD * D)
        scratch(GRAPH, XNT)
        rank_scan = [take(C) for _ in range(2)]
        dst_t, dst_eq = take(C), [take(C) for _ in range(2)]
        scratch(RAW, RAW + 4 * KD * D)
        rank_eq = [take(C) for _ in range(2)]
        xn7v = xn7.rearrange("p (i k n) -> p i k n", i=B, k=KD)
        xt7v = xt7.rearrange("p (i k n) -> p i k n", i=B, k=KD)
        v7v = v7.rearrange("p (i k n) -> p i k n", i=B, k=KD)
        psA, psB = bank(0, B * D), bank(4, B * D)
        psV = half(0, B, B * D)
        LATE = [*range(1, B), 0]
        psC = bank(7, KD * (P + 1))
        (ld_w, w_ps, w_sb, xn_done, tp_done, xt_done, h_ps, h_sb, h_st, h_free, k_ps, v_ps, k_min, k_exp, k_done, v_done,
         c_done, c_sb, c_ps, c_back, q_ps, q_min, q_exp, q_done, den_ps, qn_done, mix_ps, mix_add) = (
            sem(n) for n in ("ld_w w_ps w_sb xn_done tp_done xt_done h_ps h_sb h_st h_free k_ps v_ps k_min k_exp k_done "
                             "v_done c_done c_sb c_ps c_back q_ps q_min q_exp q_done den_ps qn_done mix_ps mix_add"
                             ).split())

        rank_ready, rank_used = sem("rank_ready"), sem("rank_used")

        def rank_tile(dve, b, i):
            eq, scan = rank_eq[i % 2], rank_scan[i % 2]
            if i == 0:
                V.settle()
            V.add(dve.tensor_scalar(eq, key_t, iota[:, ds(b, 1)], None, ALU.is_equal))
            V.add(dve.tensor_scalar(dst_eq[i % 2], dst_t, iota[:, ds(b, 1)], None, ALU.is_equal))
            V.settle()
            dve.tensor_tensor_scan(scan, eq, eq, base[:, ds(b, 1)], ALU.add, ALU.bypass).then_inc(rank_ready, 1)
            V.add(dve.tensor_reduce(tot[0][:, ds(b, 1)], dst_eq[i % 2], AX_X, ALU.add))

        def rank_add(pool, n, i):
            eq, scan = rank_eq[i % 2], rank_scan[i % 2]
            pool.wait_ge(rank_ready, n + 1)
            G.then(pool.tensor_tensor(scan, scan, eq, ALU.mult))
            G.then(pool.tensor_tensor(pos_src, pos_src, scan, ALU.add))
            pool.sem_inc(rank_used, 1)

        def norm7(dve, c, base):
            dve.wait_ge(tp_done, c + (base + 1))
            for i in range(B):
                last = normalise(dve, xn7[:, i * D:(i + 1) * D], c * B + i)
            last.then_inc(xn_done, 1)

        def transpose7(pe, c, base):
            pe.wait_ge(xn_done, c + (base + 1))
            for i in range(B):
                for k in range(KD):
                    last = pe.transpose(half(0, i)[:, k * P:(k + 1) * P], xn7v[:, i, k, :], ident)
            last.then_inc(tp_done, 1)

        def keep7(act, c, base):
            act.wait_ge(tp_done, c + (base + 2))
            act.copy(xt7, psA).then_inc(xt_done, 1)
            act.copy(xnT3[:, :, ds(c * (B * P), B * P)].rearrange("p k (i n) -> p i k n", i=B),
                     psA.rearrange("p (i k n) -> p i k n", i=B, k=KD)).then_inc(xt_done, 1)

        def store7(sp, c, base, ring, table, width):
            sp.wait_ge(h_sb, c + (base + 1))
            sp.dma_start(table[ds(c * (B * P), B * P), :].rearrange("(i p) d -> p i d", p=P),
                         ring.rearrange("p (i d) -> p i d", i=B)[:, :, 0:width]).then_inc(h_st, 16)
            sp.wait_ge(h_st, c * 16 + (base + 1) * 16)
            sp.sem_inc(h_free, 1)

        with nc.Block() as block:
            @block.sync
            def _(sp):
                for to, w in ((w0, L0_gnn_W), (wq_r, L0_mix_Wq), (wkv_r, L0_mix_Wkv), (wp_r, L0_mix_Wproj)):
                    sp.dma_start(to.rearrange("p (k c) -> p k c", c=D),
                                 w.rearrange("(k p) c -> p k c", p=P)).then_inc(ld_w, 16)
                sp.sem_inc(h_free, 1)
                with sp.Fori(0, LOOPS) as c:
                    store7(sp, c, 0, h7, h0_table, D)

            @block.gpsimd
            def _(pool):
                with pool.If(pool.value_load(unsorted[0:1, 0:1], min_val=0, max_val=2 * P) > 0):
                    edges = Scatter(pool, G_SORT, 0, pos_dst, (src_f, dst_f, w_f), scat_ring)
                    edges.go_on(0, SCAT_LOOPS - 1)
                    edges.end()
                rank_add(pool, 0, 0)
                with G.loop(LOOPS, 2 * B) as c:
                    for i in range(B):
                        rank_add(pool, c * B + (i + 1), i)
                edges = Scatter(pool, G, 1, pos_src, (dst_f, src_f), scat_ring)
                edges.go_on(0, SCAT_CUTS[0])
                edges.end(SCAT_CUTS[0] + 1)

            @block.scalar
            def _(act):
                ln_root(act)
                for n, (to, b, width) in enumerate(((wqT, 0, 512), (wkvT, 1, 1024), (wpT, 3, 512))):
                    act.wait_ge(w_ps, n + 1)
                    act.copy(to, bank(b, width)).then_inc(w_sb, 1)
                act.wait_ge(v_done, 1)
                with act.Fori(0, LOOPS) as c:
                    keep7(act, c, 0)
                    act.wait_ge(h_ps, c + 1)
                    act.wait_ge(h_free, c + 1)
                    act.copy(h7, psV).then_inc(h_sb, 1)
                    act.wait_ge(k_min, c + 1)
                    act.activation(ring_a, ring_a, ACT.Exp).then_inc(k_exp, 1)
                    act.wait_ge(c_done, c + 1)
                    act.wait_ge(v_ps, c + 1)
                    act.copy(v7v[:, :, :, 0:P], psV.rearrange("p (i k n) -> p i k n", i=B, k=KD)).then_inc(v_done, 1)
                act.wait_ge(c_ps, 1)
                act.copy(ctx_t, bank(0, KD * P)).then_inc(c_back, 1)
                act.wait_ge(c_ps, 2)
                act.copy(kv_out, bank(1, KD * D)).then_inc(c_back, 1)
                with act.Fori(0, LOOPS) as c:
                    act.wait_ge(q_min, c + 1)
                    act.activation(ring_a, ring_a, ACT.Exp).then_inc(q_exp, 1)

            @block.vector
            def _(dve):
                ln_stats(dve)
                dve.memset(v7, 1.0).then_inc(v_done, 1)
                dve.wait_ge(w_ps, 3)
                rank_keys(dve, src_f, (key_t, rank_eq[0]))
                rank_keys(dve, dst_f, (dst_t, dst_eq[0]))
                rank_tile(dve, BUCKETS - 1, 0)
                with V.loop(LOOPS, 3 * B) as c:
                    norm7(dve, c, 0)
                    for i in range(B):
                        dve.wait_ge(rank_used, c * B + max(i, 1))
                        rank_tile(dve, c * B + i, i)
                    dve.wait_ge(k_ps, c + 1)
                    dve.tensor_scalar(ring_a, psA, 0.0, None, ALU.min).then_inc(k_min, 1)
                    dve.wait_ge(k_exp, c + 1)
                    dve.wait_ge(c_done, c + 1)
                    dve.scalar_tensor_tensor(ring_b, psA, 0.0, ring_a, ALU.max, ALU.add).then_inc(k_done, 1)
                dve.wait_ge(c_done, LOOPS + 1)
                for j in range(KD):
                    V.add(dve.tensor_tensor(ctx_m[:, j * P:(j + 1) * P], psC[:, j * (P + 1):j * (P + 1) + P], blk,
                                            ALU.mult))
                last = dve.tensor_scalar(ksum, psC[:, P::P + 1], float(NODES - NP), None, ALU.add)
                V.then(last)
                for j in range(KD):
                    last = dve.tensor_scalar(ksum_b[:, j * P:(j + 1) * P], blk, ksum[:, j:j + 1], None, ALU.mult)
                last.then_inc(c_sb, 1)

                def queries(c):
                    dve.wait_ge(q_ps, c + 1)
                    dve.tensor_scalar(ring_a, psA, 0.0, None, ALU.min).then_inc(q_min, 1)
                    dve.wait_ge(q_exp, c + 1)
                    dve.scalar_tensor_tensor(ring_b, psA, 0.0, ring_a, ALU.max, ALU.add).then_inc(q_done, 1)

                def attend(c, last=False):
                    dve.wait_ge(den_ps, c + 1)
                    V.then(dve.tensor_scalar(xn7, psB, D_MIN, None, ALU.max))
                    V.then(dve.reciprocal(xn7, xn7))
                    dve.tensor_tensor(xn7, ring_b, xn7, ALU.mult).then_inc(qn_done, 1)
                    if not last:
                        dve.wait_ge(qn_done, c + 1)
                        queries(c + 1)
                    dve.wait_ge(mix_ps, c + 1)
                    a = xres[:, ds(c * (B * D), B * D)]
                    dve.tensor_tensor(a, a, psB, ALU.add).then_inc(mix_add, 1)

                queries(0)
                with V.loop(LOOPS - 1, 2) as c:
                    attend(c)
                attend(LOOPS - 1, last=True)
                rank_bases(dve, 3, 0)

            @block.tensor
            def _(pe):
                pe.sem_inc(tp_done, 1)
                pe.wait_ge(ld_w, 64)
                for n, (raw, b, blocks) in enumerate(((wq_r, 0, KD), (wkv_r, 1, 2 * KD), (wp_r, 3, KD))):
                    for k in range(KD):
                        for o in range(blocks):
                            last = pe.transpose(bank(b, P, (k * blocks + o) * P),
                                                raw[:, o * D + k * P:o * D + (k + 1) * P], ident)
                    last.then_inc(w_ps, 1)
                pe.wait_ge(w_sb, 3)
                pe.wait_ge(v_done, 1)
                pe.matmul(psC, zeros, v7[:, 0:KD * (P + 1)], start=True, stop=False, skip_group_check=True)
                pe.sem_inc(c_done, 1)
                with pe.Fori(0, LOOPS) as c:
                    transpose7(pe, c, 0)
                    pe.wait_ge(xt_done, c * 2 + 1)
                    for i in LATE:
                        if i == LATE[-1]:
                            pe.wait_ge(xt_done, c * 2 + 2)
                        for k in range(KD):
                            last = pe.matmul(half(0, B + i), xt7v[:, i, k, :], w0[:, k * D:(k + 1) * D],
                                             start=(k == 0), stop=(k == KD - 1))
                    last.then_inc(h_ps, 1)
                    for i in range(B):
                        if i == B - 1:
                            pe.wait_ge(h_sb, c + 1)
                        for k in range(KD):
                            last = pe.matmul(half(0, i), xt7v[:, i, k, :], wkvT[:, k * 2 * D:k * 2 * D + D],
                                             start=(k == 0), stop=(k == KD - 1))
                    last.then_inc(k_ps, 1)
                    for i in LATE:
                        if i == LATE[-1]:
                            pe.wait_ge(k_done, c + 1)
                        for k in range(KD):
                            last = pe.matmul(half(0, B + i), xt7v[:, i, k, :], wkvT[:, k * 2 * D + D:(k + 1) * 2 * D],
                                             start=(k == 0), stop=(k == KD - 1))
                    last.then_inc(v_ps, 1)
                    pe.wait_ge(v_done, c + 2)
                    for i in range(B):
                        for k in range(KD):
                            last = pe.matmul(psC[:, k * (P + 1):(k + 1) * (P + 1)],
                                             ring_b[:, i * D + k * P:i * D + (k + 1) * P], v7v[:, i, k, :],
                                             start=False, stop=False, skip_group_check=True)
                    last.then_inc(c_done, 1)
                pe.wait_ge(c_sb, 1)
                for j in range(KD):
                    last = pe.transpose(bank(0, P, j * P), ctx_m[:, j * P:(j + 1) * P], ident)
                last.then_inc(c_ps, 1)
                pe.wait_ge(c_back, 1)
                for j in range(KD):
                    last = pe.matmul(bank(1, D, j * D), ctx_t[:, j * P:(j + 1) * P], wpT[:, j * D:(j + 1) * D],
                                     start=True, stop=True)
                last.then_inc(c_ps, 1)
                pe.wait_ge(c_back, 2)
                pe.sem_inc(mix_add, 1)

                def queries(c):
                    for i in range(B):
                        for o in range(KD):
                            for k in range(KD):
                                last = pe.matmul(half(0, i)[:, o * P:(o + 1) * P],
                                                 wqT[:, k * D + o * P:k * D + (o + 1) * P],
                                                 xnT3[:, k, ds((c * B + i) * P, P)], start=(k == 0), stop=(k == KD - 1))
                    last.then_inc(q_ps, 1)

                def attend(c, last=False):
                    pe.wait_ge(q_done, c + 1)
                    pe.wait_ge(mix_add, c + 1)
                    for i in range(B):
                        for k in range(KD):
                            q = ring_b[:, i * D + k * P:i * D + (k + 1) * P]
                            ins = pe.matmul(half(4, i)[:, k * P:(k + 1) * P], ksum_b[:, k * P:(k + 1) * P], q,
                                            start=True, stop=True)
                    ins.then_inc(den_ps, 1)
                    if not last:
                        queries(c + 1)
                    pe.wait_ge(qn_done, c + 1)
                    for i in range(B):
                        for k in range(KD):
                            ins = pe.matmul(half(4, i), xn7[:, i * D + k * P:i * D + (k + 1) * P],
                                            kv_out[:, k * D:(k + 1) * D], start=(k == 0), stop=(k == KD - 1))
                    ins.then_inc(mix_ps, 1)

                queries(0)
                with pe.Fori(0, LOOPS - 1) as c:
                    attend(c)
                attend(LOOPS - 1, last=True)
                pe.wait_ge(mix_add, LOOPS + 1)
                rank_sums(pe, 3, 0)

        edges_ready, tiles_ready, hot_done, gnn_ps, gnn_add = (sem(n) for n in (
            "edges_ready", "tiles_ready", "hot_done", "gnn_ps", "gnn_add"))
        scratch(XNT, ACC)
        vv = visit_views()
        rows = take(2 * U * ROW1).rearrange("p (b u w) -> p b u w", b=2, u=U)
        scratch(FREE)
        hot = take(2 * U * P).rearrange("p (b u n) -> p b u n", b=2, u=U)
        idx_ring = take(2 * U).bitcast(I32)
        scat_ring = take(10 * SCAT)
        NVIS = GROUP_LOOPS * 2 * U
        GNN0_BANKS, GNN1_BANKS = 8, 4

        def gather_row(pool, slot, width, idx, table, done):
            pool.indirect_dma_start(slot[:, 0:width], None, table, bass.IndirectOffsetOnAxis(ap=idx, axis=0)
                                    ).then_inc(done, 16)

        def load_tiles(engine, first):
            return nc.values_load_multi_w_load_instructions(
                tile_row[0:1, ds(first, U)], engines=[engine.engine], min_val=0, max_val=T,
                skip_runtime_bounds_check_because="a visit's tile is a count of at most T tiles")[1]

        def add_sums(dve, n, tile, width, b, sums_before, adds_before):
            dve.wait_ge(gnn_ps, n + (sums_before + 1))
            dve.wait_ge(gnn_add, n + adds_before)
            to = acc[:, ds(tile * ACC_W, width)]
            dve.tensor_tensor(to, to, bank(b, width), ALU.add).then_inc(gnn_add, 1)

        with nc.Block() as block:
            @block.sync
            def _(sp):
                visits_sync(sp, 0, vv)
                sp.sem_inc(tiles_ready, 1)

            @block.gpsimd
            def _(pool):
                visits_pool(pool, 0, vv)
                edges = Scatter(pool, G, 1, pos_src, (dst_f, src_f), scat_ring, begun=True)
                edges.go_on(SCAT_CUTS[0], SCAT_CUTS[1] - SCAT_CUTS[0])
                edges.end(SCAT_CUTS[1] + 1)
                pool.wait_ge(edges_ready, 1)
                with G.loop(GROUP_LOOPS, 2) as j:
                    for b in range(2):
                        pool.wait_ge(gnn_ps, j * (2 * U) + (b + 1) * U)
                        G.then(pool.tensor_copy(idx_ring[:, b * U:(b + 1) * U], v_idx[:, ds(j * (2 * U) + b * U, U)]))
                        pool.sem_inc(dma_turn, 1)
                        for u in range(U):
                            gather_row(pool, rows[:, b, u, :], D, idx_ring[:, b * U + u:b * U + u + 1], h0_table,
                                       gather_done[(b * U + u) // 2])

            @block.vector
            def _(dve):
                visits_dve(dve, 0, vv)
                V.then(dve.memset(acc, 0.0))
                dve.sem_inc(edges_ready, 1)
                dve.sem_inc(gnn_add, GNN0_BANKS)
                dve.wait_ge(tiles_ready, 1)
                def weighted_hot(n, b, u):
                    dve.tensor_scalar(hot[:, b, u, :], iota, v_loc[:, ds(n, 1)], v_w[:, ds(n, 1)],
                                      ALU.is_equal, ALU.mult).then_inc(hot_done, 1)

                for u in range(U):
                    weighted_hot(u, 0, u)
                with nc.vector.Fori(0, GROUP_LOOPS) as j:
                    for b in range(2):
                        tiles = load_tiles(dve, j * (2 * U) + b * U)
                        for u in range(U):
                            weighted_hot(j * (2 * U) + (b + 1) * U + u, 1 - b, u)
                            add_sums(dve, j * (2 * U) + b * U + u, tiles[u], D, u, 2 * U, GNN0_BANKS)

            @block.tensor
            def _(pe):
                visits_pe(pe, 0, vv)
                pe.sem_inc(gnn_ps, 2 * U)
                pe.wait_ge(edges_ready, 1)
                with pe.Fori(0, GROUP_LOOPS) as j:
                    for b in range(2):
                        for u in range(U):
                            n = j * (2 * U) + b * U + u
                            pe.wait_ge(hot_done, n + 1)
                            if u % 2 == 0:
                                pe.wait_ge(gather_done[(b * U + u) // 2], j * 32 + 32)
                            pe.wait_ge(gnn_add, n + 1)
                            pe.matmul(bank(u, D), hot[:, b, u, :], rows[:, b, u, 0:D], start=True, stop=True
                                      ).then_inc(gnn_ps, 1)

        scratch(FREE)
        scat_ring = take(10 * SCAT)
        xn7, xt7 = take(B * D), take(B * D)
        bias_b, bproj_b = take(D), take(D)
        rw_t, router_b, b1_t, b2_s = take(KD * E0), take(E0), take(E0), take(D)
        pos_i, back_i = take(T).bitcast(I32), take(T).bitcast(I32)
        slot_e = take((BATCHES0 + 2) * Q0).bitcast(I32)
        node_idx = [take(B).bitcast(I32) for _ in range(2)]
        scratch(place["at"])
        mean56, std56 = take(B * D // HC), take(B * D // HC)
        scratch(ACC, ACC + BUCKETS * ACC_W)
        w1_all = take(E0 * KD * H0)
        w2_all = take(E0 * D)
        w_f_at = ACC + BUCKETS * ACC_W + 3 * C
        scratch(w_f_at, FREE)
        g1_w = take(KD * ROW1)
        scratch(XNT, ACC)
        picks = take(T * E0)
        RINGS0 = place["at"]
        logits, is_top, rev, rw_raw = take(T * E0), take(T * E0), take(E0), take(D)[0:E0, :]
        memory = choice_memory(1, E0)
        scratch(RINGS0, ACC)
        x_in = [take(Q0 * D) for _ in range(2)]
        x_t = [take(Q0 * D) for _ in range(2)]
        w1_ring = [take(Q0 * KD * H0) for _ in range(2)]
        h_t = [take(Q0 * P)[0:H0, :] for _ in range(2)]
        y_ring = [take(Q0 * D) for _ in range(2)]
        scratch(RINGS0, ACC)
        got7 = [take(B * D) for _ in range(2)]
        got0 = [[[g[:, i * D:(i + 1) * D] for i in range(B)]] for g in got7]
        mix7, mix_t = take(B * E0), take(B * P)
        scratch(ACC, ACC + BUCKETS * ACC_W)
        z7 = take(B * KD * (P + 1))
        xc7, sq7, h7 = take(B * D), take(B * D), take(B * ROW1)
        al_b, ar_b, wa_tmp = take(D), take(D), take(D)
        wk_c, bk_c, wv_b, bv_b, kcol = take(KD), take(KD), take(D), take(D), take(2 * KD)
        s_bc, kvm, kv_t = take(KD * P), take(KD * P), take(KD * P)
        xn7v = xn7.rearrange("p (i k n) -> p i k n", i=B, k=KD)
        xt7v = xt7.rearrange("p (i k n) -> p i k n", i=B, k=KD)
        z7v = z7.rearrange("p (i k n) -> p i k n", i=B, k=KD)
        (ld_b, ld_e1, ld_e2, ld_g, x1_done, rw_ps, rw_sb, lg_ps, lg_sb, in0_ps, in0_done, w0_done, m1_ps, he_done,
         m2_ps, y0_done, y0_free, pick_in, pick_ps, pick_done, b20_ps, got_free, x2_done, sq_in, sq_done, ss_done,
         sd_done, z_done, gram, s_done, s_ps, kvm_done, xs_done, mx_ps, mx_add) = (sem(n) for n in (
             "ld_b ld_e1 ld_e2 ld_g x1_done rw_ps rw_sb lg_ps lg_sb in0_ps in0_done w0_done m1_ps he_done m2_ps "
             "y0_done y0_free pick_in pick_ps pick_done b20_ps got_free x2_done sq_in sq_done ss_done sd_done z_done "
             "gram s_done s_ps kvm_done xs_done mx_ps mx_add").split())
        slots_in, slots_out, b20_free = sem("slots_in"), sem("slots_out"), sem("b20_free")
        x0_ld = [sem(f"x0_ld{b}") for b in range(2)]
        batch_rows = slot_rows[0:(BATCHES0 + 3) * Q0 * P, :].rearrange("(q p) d -> p q d", p=P)
        batch_out = slot_out[0:BATCHES0 * Q0 * P, :].rearrange("(q p) d -> p q d", p=P)
        assert (BATCHES0 + 3) * Q0 <= SLOT_TILES + SPARE

        def load_experts0(engine, first):
            return nc.values_load_multi_w_load_instructions(
                slot_e[0:1, ds(first, Q0)], engines=[engine.engine], min_val=0, max_val=E0 - 1,
                skip_runtime_bounds_check_because="a slot's expert is the least of a count and E0 - 1")[1]

        CALL1, CALL2 = LOOPS, 2 * LOOPS

        def mask_padding(dve):
            last = xres[:, (T - 1) * D:]
            V.then(dve.tensor_scalar(last, last, rowmask, None, ALU.mult))

        with nc.Block() as block:
            @block.sync
            def _(sp):
                for to, a in ((bias_b, L0_gnn_b), (bproj_b, L0_mix_bproj), (router_b, L0_ffn_router_b)):
                    sp.dma_start(to, a.partition_broadcast(P)).then_inc(ld_b, 16)
                sp.dma_start(b1_t[0:H0, :], L0_ffn_b1.rearrange("e h -> h e"), allow_slow_non_contiguous=True
                             ).then_inc(ld_b, 16)
                sp.dma_start(b2_s[0:E0, :], L0_ffn_b2).then_inc(ld_b, 16)
                sp.dma_start(g1_w.rearrange("p (k w) -> p k w", k=KD)[:, :, 0:D],
                             L1_gnn_W.rearrange("(k p) w -> p k w", p=P)).then_inc(ld_b, 16)
                sp.wait_ge(x1_done, 1)
                sp.dma_start(rw_raw, L0_ffn_router_w).then_inc(ld_e1, 16)
                for k in range(KD):
                    sp.dma_start(w1_all.rearrange("p (e k h) -> p e k h", k=KD, h=H0)[:, :, k, :],
                                 L0_ffn_W1[:, k * P:(k + 1) * P, :].rearrange("e p h -> p e h")).then_inc(ld_e2, 16)
                sp.dma_start(w2_all[0:H0, :].rearrange("h (e d) -> h e d", d=D), L0_ffn_W2.rearrange("e h d -> h e d")
                             ).then_inc(ld_e2, 16)
                sp.wait_ge(ld_e2, 48)
                sp.sem_inc(y0_free, 32)
                sp.wait_ge(slots_in, 1)
                for b in range(2):
                    sp.dma_start(x_in[b].rearrange("p (q d) -> p q d", d=D), batch_rows[:, b * Q0:(b + 1) * Q0, :]
                                 ).then_inc(x0_ld[b], 16)
                sp.wait_ge(in0_ps, 1)
                sp.dma_start(x_in[0].rearrange("p (q d) -> p q d", d=D), batch_rows[:, 2 * Q0:3 * Q0, :]
                             ).then_inc(x0_ld[0], 16)
                with sp.Fori(0, BATCHES0 // 2) as j:
                    for b in range(2):
                        s = j * 2 + b
                        sp.wait_ge(in0_ps, s + 2)
                        sp.dma_start(x_in[1 - b].rearrange("p (q d) -> p q d", d=D),
                                     batch_rows[:, ds((s + 3) * Q0, Q0), :]).then_inc(x0_ld[1 - b], 16)
                        sp.wait_ge(y0_done, s + 3)
                        sp.dma_start(batch_out[:, ds(s * Q0, Q0), :], y_ring[b].rearrange("p (q d) -> p q d", d=D)
                                     ).then_inc(y0_free, 16)
                sp.wait_ge(y0_free, BATCHES0 * 16 + 32)
                sp.wait_ge(x0_ld[0], BATCHES0 * 8 + 32)
                sp.wait_ge(x0_ld[1], BATCHES0 * 8 + 16)
                sp.sem_inc(slots_out, 1)
                sp.wait_ge(x2_done, 1)
                sp.dma_start(al_b, L1_gnn_a_l.rearrange("o h f -> (o h f)").partition_broadcast(P)).then_inc(ld_g, 16)
                sp.dma_start(ar_b, L1_gnn_a_r.rearrange("o h f -> (o h f)").partition_broadcast(P)).then_inc(ld_g, 16)
                for to, a in ((wk_c, L1_mix_kln_weight), (bk_c, L1_mix_kln_bias)):
                    sp.dma_start(to, a.rearrange("h o c -> (h o c)").rearrange("(k p) -> p k", p=P),
                                 allow_slow_non_contiguous=True).then_inc(ld_g, 16)
                for to, a in ((wv_b, L1_mix_vln_weight), (bv_b, L1_mix_vln_bias)):
                    sp.dma_start(to, a.rearrange("h o c -> (h o c)").partition_broadcast(P)).then_inc(ld_g, 16)
                with sp.Fori(0, LOOPS) as c:
                    store7(sp, c, CALL1, h7, h1_table, ROW1)

            @block.gpsimd
            def _(pool):
                edges = Scatter(pool, G, 1, pos_src, (dst_f, src_f), scat_ring, begun=True)
                edges.go_on(SCAT_CUTS[1], SCAT_CUTS[2] - SCAT_CUTS[1])
                pool.sem_inc(xs_free, 1)
                scatter_rows(pool, 0, 1, pos_i, node_idx, (xn7, xt7))
                pool.sem_inc(slots_in, 1)
                edges.go_on(SCAT_CUTS[2], SCAT_CUTS[3] - SCAT_CUTS[2])
                pool.wait_ge(slots_out, 1)
                fetch_rows(pool, BATCHES0 * Q0, 1, back_i, node_idx, got0, got_free, [[moved[2 + b]] * B for b in range(2)])
                edges.go_on(SCAT_CUTS[3], SCAT_LOOPS - 1 - SCAT_CUTS[3])
                edges.end()

            @block.scalar
            def _(act):
                ln_root(act)
                act.wait_ge(rw_ps, 1)
                act.copy(rw_t, bank(7, KD * E0)).then_inc(rw_sb, 1)
                with act.Fori(0, LOOPS) as c:
                    act.wait_ge(tp_done, c + (CALL1 + 2))
                    act.copy(xt7, psA).then_inc(xt_done, 1)
                act.wait_ge(pos_done, 1)
                with act.Fori(0, BATCHES0 // 2) as j:
                    for b in range(2):
                        s = j * 2 + b
                        experts = load_experts0(act, s * Q0)
                        act.wait_ge(m1_ps, s + 1)
                        for q in range(Q0):
                            act.activation(h_t[b][:, q * P:(q + 1) * P], ps[0:H0, (2 + b) * 512 + q * P:(2 + b) * 512 + (q + 1) * P],
                                           ACT.Relu, bias=b1_t[0:H0, ds(experts[q], 1)]).then_inc(he_done, 1)
                with act.Fori(0, LOOPS) as c:
                    act.wait_ge(pick_ps, c + 1)
                    act.copy(mix_t[0:E0, :], ps[0:E0, 0:B * P]).then_inc(pick_done, 1)
                ln_root(act)
                with act.Fori(0, LOOPS) as c:
                    keep7(act, c, CALL2)
                    act.wait_ge(sq_in, c + 1)
                    act.activation(sq7, xc7, ACT.Square).then_inc(sq_done, 1)
                    act.wait_ge(ss_done, c + 1)
                    act.activation(std56, std56, ACT.Sqrt, scale=1.0 / (HC - 1)).then_inc(sd_done, 1)
                    act.wait_ge(h_ps, c + (LOOPS + 1))
                    act.wait_ge(h_free, c + (LOOPS + 1))
                    got = bank(0, B * 512).rearrange("p (i w) -> p i w", w=512)
                    act.copy(rl_all[:, ds(c * (B * 2 * GH), B * 2 * GH)].rearrange("p (i w) -> p i w", i=B),
                             got[:, :, D:ROW1])
                    act.copy(h7.rearrange("p (i w) -> p i w", i=B), got[:, :, 0:ROW1]).then_inc(h_sb, 1)
                act.sem_inc(xs_done, 1)
                with act.Fori(0, LOOPS) as c:
                    act.wait_ge(mx_ps, c + 1)
                    act.copy(xt7v.rearrange("p i k n -> p k i n"),
                             xnT3[:, :, ds(c * (B * P), B * P)].rearrange("p k (i n) -> p k i n", i=B)
                             ).then_inc(xs_done, 1)

            @block.vector
            def _(dve):
                dve.wait_ge(ld_b, 6 * 16)
                with V.loop(LOOPS, 3) as c:
                    a = xres[:, ds(c * (B * D), B * D)].rearrange("p (i d) -> p i d", i=B)
                    t = xn7.rearrange("p (i d) -> p i d", i=B)
                    got = acc[:, ds(c * (B * ACC_W), B * ACC_W)].rearrange("p (i w) -> p i w", i=B)[:, :, 0:D]
                    wide = [w.unsqueeze(1).to_broadcast([P, B, D]) for w in (bias_b, bproj_b)]
                    V.then(dve.tensor_tensor(t, got, wide[0], ALU.add))
                    V.then(dve.scalar_tensor_tensor(t, t, 0.0, wide[1], ALU.max, ALU.add))
                    V.then(dve.tensor_tensor(a, a, t, ALU.add))
                dve.sem_inc(x1_done, 1)
                mask_padding(dve)
                ln_stats(dve)
                def keep_logits(c):
                    dve.wait_ge(lg_ps, c + 1)
                    dve.tensor_copy(logits[:, ds(c * (B * E0), B * E0)], bank(4, B * E0)).then_inc(lg_sb, 1)

                dve.sem_inc(lg_sb, 1)
                norm7(dve, 0, CALL1)
                with dve.Fori(0, LOOPS - 1) as c:
                    norm7(dve, c + 1, CALL1)
                    keep_logits(c)
                keep_logits(LOOPS - 1)
                dve.wait_ge(lg_sb, LOOPS + 1)
                wide = [P, T, E0]
                lg3, eq3 = (a.rearrange("p (t e) -> p t e", e=E0) for a in (logits, is_top))
                V.add(dve.tensor_tensor(lg3, lg3, router_b.unsqueeze(1).to_broadcast(wide), ALU.add))
                V.add(dve.tensor_scalar(rev, iota[:, 0:E0], -1.0, float(E0), ALU.mult, ALU.add))
                V.settle()
                best = memory["pos"]
                V.then(dve.tensor_reduce(best, lg3, AX_X, ALU.max))
                V.then(dve.tensor_tensor(eq3, lg3, best.unsqueeze(2).to_broadcast(wide), ALU.is_ge))
                V.then(dve.tensor_tensor(eq3, eq3, rev.unsqueeze(1).to_broadcast(wide), ALU.mult))
                V.then(dve.tensor_reduce(best, eq3, AX_X, ALU.max))
                V.then(dve.tensor_tensor(picks.rearrange("p (t e) -> p t e", e=E0), rev.unsqueeze(1).to_broadcast(wide),
                                         best.unsqueeze(2).to_broadcast(wide), ALU.is_equal))
                V.then(dve.tensor_scalar(picks[:, (T - 1) * E0:], picks[:, (T - 1) * E0:], rowmask, None, ALU.mult))
                dve.sem_inc(picks_done, 1)
                place_choices(dve, 1, 1, E0, picks, memory, BATCHES0 * Q0, pos_i, back_i, slot_e)
                rows_to_scatter(dve, 0, (xn7, xt7))

                def take_in(s, b):
                    dve.wait_ge(in0_ps, s + 1)
                    dve.tensor_copy(x_t[b], bank(0, Q0 * D)).then_inc(in0_done, 1)

                def take_w1(experts, b):
                    for q in range(Q0):
                        last = dve.tensor_copy(w1_ring[b][:, q * KD * H0:(q + 1) * KD * H0],
                                               w1_all[:, ds(experts[q] * (KD * H0), KD * H0)])
                    last.then_inc(w0_done, 1)

                dve.wait_ge(ld_e2, 48)
                dve.sem_inc(y0_done, 2)
                for b in range(2):
                    take_w1(load_experts0(dve, b * Q0), b)
                    take_in(b, b)
                with dve.Fori(0, BATCHES0 // 2) as j:
                    for b in range(2):
                        s = j * 2 + b
                        experts = load_experts0(dve, (s + 2) * Q0)
                        dve.wait_ge(m1_ps, s + 1)
                        take_w1(experts, b)
                        take_in(s + 2, b)
                        dve.wait_ge(m2_ps, s + 1)
                        dve.wait_ge(y0_free, s * 16 + 16)
                        dve.tensor_copy(y_ring[b], bank(4 + 2 * b, Q0 * D)).then_inc(y0_done, 1)
                dve.wait_ge(y0_free, BATCHES0 * 16 + 32)
                def pick(c):
                    dve.tensor_copy(mix7, picks[:, ds(c * (B * E0), B * E0)]).then_inc(pick_in, 1)

                def add_rows(j, b, last=False):
                    c = j * 2 + b
                    dve.wait_ge(b20_ps, c + 1)
                    if not last:
                        pick(c + 1)
                    dve.wait_ge(moved[2 + b], j * (16 * B) + (moved_before(0, 2 + b) + 16 * B))
                    dve.tensor_tensor(got7[b], got7[b], psB, ALU.add).then_inc(b20_free, 1)
                    dve.wait_ge(b20_free, c + 2)
                    a = xres[:, ds(c * (B * D), B * D)]
                    dve.scalar_tensor_tensor(a, got7[b], 0.0, a, ALU.max, ALU.add).then_inc(got_free, 1)

                dve.sem_inc(got_free, 2)
                dve.sem_inc(b20_free, 1)
                pick(0)
                with dve.Fori(0, LOOPS // 2) as j:
                    for b in range(2):
                        add_rows(j, b)
                add_rows(LOOPS // 2, 0, last=True)
                dve.wait_ge(got_free, LOOPS + 2)
                dve.sem_inc(x2_done, 1)
                mask_padding(dve)
                ln_stats(dve)
                dve.wait_ge(ld_g, 6 * 16)
                for k in range(KD):
                    for f, a in ((0, ar_b), (1, al_b)):
                        V.then(dve.tensor_tensor(wa_tmp, g1_w[:, k * ROW1:k * ROW1 + D], a, ALU.mult))
                        at = k * ROW1 + D + f * GH
                        V.then(dve.tensor_reduce(g1_w[:, at:at + GH], wa_tmp.rearrange("p (h f) -> p h f", h=GH),
                                                 AX_X, ALU.add))
                dve.memset(z7, 1.0).then_inc(z_done, 1)
                with V.loop(LOOPS, 5) as c:
                    norm7(dve, c, CALL2)
                    dve.wait_ge(xn_done, c + (CALL2 + 1))
                    heads = xn7.rearrange("p (m e) -> p m e", e=HC)
                    cents = xc7.rearrange("p (m e) -> p m e", e=HC)
                    V.then(dve.tensor_reduce(mean56, heads, AX_X, ALU.add))
                    V.then(dve.tensor_scalar(mean56, mean56, 1.0 / HC, None, ALU.mult))
                    dve.tensor_tensor(cents, heads, mean56.unsqueeze(2).to_broadcast([P, B * D // HC, HC]),
                                      ALU.subtract).then_inc(sq_in, 1)
                    dve.wait_ge(sq_done, c + 1)
                    dve.tensor_reduce(std56, sq7.rearrange("p (m e) -> p m e", e=HC), AX_X, ALU.add
                                      ).then_inc(ss_done, 1)
                    dve.wait_ge(sd_done, c + 1)
                    V.then(dve.tensor_scalar(std56, std56, KV_EPS, None, ALU.add))
                    V.then(dve.reciprocal(std56, std56))
                    dve.wait_ge(gram, c + 1)
                    V.add(dve.tensor_tensor(
                        z7.rearrange("p (m w) -> p m w", w=P + 1)[:, :, 0:P].rearrange("p m (h e) -> p m h e", e=HC),
                        xc7.rearrange("p (m h e) -> p m h e", m=B * KD, e=HC),
                        std56.rearrange("p (m h) -> p m h", m=B * KD).unsqueeze(3).to_broadcast(
                            [P, B * KD, P // HC, HC]), ALU.mult))
                    V.settle()
                    dve.sem_inc(z_done, 1)
                dve.wait_ge(gram, LOOPS + 1)
                V.add(dve.tensor_tensor(kcol[:, 0:KD], wk_c, psC[:, P::P + 1], ALU.mult))
                V.add(dve.tensor_scalar(kcol[:, KD:], bk_c, float(NODES), None, ALU.mult))
                for k in range(KD):
                    last = dve.tensor_copy(s_bc[:, k * P:(k + 1) * P],
                                           psC[:, k * (P + 1) + P:(k + 1) * (P + 1)].to_broadcast([P, P]))
                last.then_inc(s_done, 1)
                V.settle()
                dve.wait_ge(s_ps, 1)
                for k in range(KD):
                    m, at = kvm[:, k * P:(k + 1) * P], slice(k * P, (k + 1) * P)
                    t = kv_t[:, at]
                    V.add(dve.scalar_tensor_tensor(m, psC[:, k * (P + 1):k * (P + 1) + P], wk_c[:, k:k + 1],
                                                   wv_b[:, at], ALU.mult, ALU.mult))
                    V.then(dve.tensor_tensor(t, bank(0, P, k * P), wv_b[:, at], ALU.mult))
                    V.then(dve.scalar_tensor_tensor(m, bv_b[:, at], kcol[:, k:k + 1], m, ALU.mult, ALU.add))
                    V.then(dve.scalar_tensor_tensor(m, t, bk_c[:, k:k + 1], m, ALU.mult, ALU.add))
                    V.then(dve.scalar_tensor_tensor(m, bv_b[:, at], kcol[:, KD + k:KD + k + 1], m, ALU.mult, ALU.add))
                    V.then(dve.scalar_tensor_tensor(m, m, 1.0 / NODES, blk, ALU.mult, ALU.mult))
                    last = dve.tensor_tensor(m, m, ident, ALU.add)
                last.then_inc(kvm_done, 1)
                with dve.Fori(0, LOOPS) as c:
                    dve.wait_ge(mx_ps, c + 2)
                    a = xres[:, ds(c * (B * D), B * D)]
                    dve.tensor_tensor(a, a, psB, ALU.add).then_inc(mx_add, 1)

            @block.tensor
            def _(pe):
                pe.wait_ge(ld_e1, 16)
                for k in range(KD):
                    last = pe.transpose(bank(7, E0, k * E0), rw_raw[:, k * P:(k + 1) * P], ident[0:E0, 0:E0])
                last.then_inc(rw_ps, 1)
                pe.wait_ge(rw_sb, 1)
                pe.wait_ge(ld_b, 6 * 16)
                with pe.Fori(0, LOOPS) as c:
                    transpose7(pe, c, CALL1)
                    pe.wait_ge(xt_done, c + (2 * LOOPS + 1))
                    pe.wait_ge(lg_sb, c + 1)
                    for i in range(B):
                        for k in range(KD):
                            last = pe.matmul(bank(4, E0, i * E0), xt7v[:, i, k, :], rw_t[:, k * E0:(k + 1) * E0],
                                             start=(k == 0), stop=(k == KD - 1))
                    last.then_inc(lg_ps, 1)
                choice_sums(pe, 1, 1, E0, picks)
                pe.wait_ge(ld_e2, 48)
                pe.wait_ge(pos_done, 1)

                def flip(b, nth):
                    pe.wait_ge(x0_ld[b], nth * 16 + 16)
                    for q in range(Q0):
                        for k in range(KD):
                            last = pe.transpose(bank(0, P, (q * KD + k) * P), x_in[b][:, (q * KD + k) * P:(q * KD + k + 1) * P],
                                                ident)
                    last.then_inc(in0_ps, 1)

                def hidden(s, b):
                    pe.wait_ge(in0_done, s + 1)
                    pe.wait_ge(w0_done, s + 1)
                    for q in range(Q0):
                        for k in range(KD):
                            last = pe.matmul(ps[0:H0, (2 + b) * 512 + q * P:(2 + b) * 512 + (q + 1) * P],
                                             w1_ring[b][:, (q * KD + k) * H0:(q * KD + k + 1) * H0],
                                             x_t[b][:, (q * KD + k) * P:(q * KD + k + 1) * P],
                                             start=(k == 0), stop=(k == KD - 1))
                    last.then_inc(m1_ps, 1)

                flip(0, 0)
                pe.wait_ge(in0_done, 1)
                flip(1, 0)
                hidden(0, 0)
                with pe.Fori(0, BATCHES0 // 2) as j:
                    for b in range(2):
                        s = j * 2 + b
                        experts = load_experts0(pe, s * Q0)
                        hidden(s + 1, 1 - b)
                        flip(b, j + 1)
                        pe.wait_ge(y0_done, s + 1)
                        pe.wait_ge(he_done, s * Q0 + Q0)
                        for q in range(Q0):
                            last = pe.matmul(bank(4 + 2 * b, D, q * D), h_t[b][:, q * P:(q + 1) * P],
                                             w2_all[0:H0, ds(experts[q] * D, D)], start=True, stop=True)
                        last.then_inc(m2_ps, 1)
                pe.wait_ge(y0_done, BATCHES0 + 2)
                with pe.Fori(0, LOOPS) as c:
                    pe.wait_ge(pick_in, c + 1)
                    for i in range(B):
                        last = pe.transpose(ps[0:E0, i * P:(i + 1) * P], mix7[:, i * E0:(i + 1) * E0], ident)
                    last.then_inc(pick_ps, 1)
                    pe.wait_ge(pick_done, c + 1)
                    pe.wait_ge(b20_free, c + 1)
                    for i in range(B):
                        last = pe.matmul(half(4, i), mix_t[0:E0, i * P:(i + 1) * P], b2_s[0:E0, :], start=True, stop=True)
                    last.then_inc(b20_ps, 1)
                pe.wait_ge(z_done, 1)
                pe.matmul(psC, zeros, z7[:, 0:KD * (P + 1)], start=True, stop=False, skip_group_check=True)
                pe.sem_inc(gram, 1)
                with pe.Fori(0, LOOPS) as c:
                    transpose7(pe, c, CALL2)
                    pe.wait_ge(xt_done, c * 2 + (3 * LOOPS + 2))
                    for i in range(B):
                        for k in range(KD):
                            last = pe.matmul(bank(i, ROW1), xt7v[:, i, k, :], g1_w[:, k * ROW1:(k + 1) * ROW1],
                                             start=(k == 0), stop=(k == KD - 1))
                    last.then_inc(h_ps, 1)
                    pe.wait_ge(z_done, c + 2)
                    for i in range(B):
                        for k in range(KD):
                            last = pe.matmul(psC[:, k * (P + 1):(k + 1) * (P + 1)], z7v[:, i, k, 0:P], z7v[:, i, k, :],
                                             start=False, stop=False, skip_group_check=True)
                    last.then_inc(gram, 1)
                    pe.wait_ge(h_sb, c + (CALL1 + 1))
                pe.wait_ge(s_done, 1)
                for k in range(KD):
                    last = pe.matmul(bank(0, P, k * P), s_bc[:, k * P:(k + 1) * P], ident, start=True, stop=True)
                last.then_inc(s_ps, 1)
                pe.wait_ge(kvm_done, 1)
                pe.sem_inc(mx_ps, 1)
                pe.sem_inc(mx_add, 1)
                with pe.Fori(0, LOOPS) as c:
                    pe.wait_ge(xs_done, c + 2)
                    pe.wait_ge(mx_add, c + 1)
                    for i in range(B):
                        for k in range(KD):
                            last = pe.matmul(half(4, i)[:, k * P:(k + 1) * P], xt7v[:, i, k, :],
                                             kvm[:, k * P:(k + 1) * P], start=True, stop=True)
                    last.then_inc(mx_ps, 1)

        scratch(XNT, ACC)
        vv = visit_views()
        scratch(XNT, ACC)
        rows = take(R * U * ROW1).rearrange("p (r u w) -> p r u w", r=R, u=U)
        scratch(ACC + BUCKETS * ACC_W)
        hot_b = [take(U * P // 2).bitcast(BF16) for _ in range(2)]
        hot_t = take(U * P // 2).bitcast(BF16)
        ident_b = take(P // 2).bitcast(BF16)
        lc = take(BUCKETS * 2 * GH)
        lc_parts = take(BUCKETS * PARTS * 2 * GH // 2).bitcast(BF16)
        look = take(U * 2 * GH).rearrange("p (u w) -> p u w", u=U)
        r_max, r_rows = take(GH), take(GH * P)
        score = take(U * GH).rearrange("p (u h) -> p u h", u=U)
        assert place["at"] <= FREE
        scratch(FREE)
        hot = take(2 * U * P).rearrange("p (b u n) -> p b u n", b=2, u=U)
        idx_ring = take(R * U).bitcast(I32)
        den7, t7 = take(B * GH), take(B * D)
        lc3 = lc.rearrange("p (t w) -> p t w", w=2 * GH)
        rl3 = rl_all.rearrange("p (t w) -> p t w", w=2 * GH)
        rows_done = gather_done[0:R]
        ROWS_BEFORE = [moved_before(0, r) + fetched0(r) for r in range(R)]
        SUMS_BEFORE, ADDS_BEFORE = NVIS + 2 * U, NVIS + GNN0_BANKS
        lcp = lc_parts.rearrange("p (t q w) -> p t q w", q=PARTS, w=2 * GH)
        LW = PARTS * 2 * GH
        (rm_done, rm_ps, lc_done, hots_done, hott_ps, hott_done, look_ps, score_done, ex_done, msg_done,
         hot_done32, idx_done) = (
            sem(n) for n in ("rm_done rm_ps lc_done hots_done hott_ps hott_done look_ps score_done ex_done "
                             "msg_done hot_done32 idx_done").split())

        with nc.Block() as block:
            @block.sync
            def _(sp):
                visits_sync(sp, 1, vv)
                sp.sem_inc(tiles_ready, 1)

            @block.gpsimd
            def _(pool):
                visits_pool(pool, 1, vv)
                pool.wait_ge(edges_ready, 2)
                pool.wait_ge(tiles_ready, 2)
                with pool.Fori(0, RINGS_OF_R) as j:
                    for r in range(R):
                        g = j * R + r
                        pool.wait_ge(idx_done, g + 1)
                        for u in range(U):
                            if u % HALF_U == 0:
                                pool.wait_ge(gnn_ps, g * U + (SUMS_BEFORE + u + HALF_U))
                                pool.sem_inc(dma_turn, 1)
                            gather_row(pool, rows[:, r, u, :], ROW1, idx_ring[:, r * U + u:r * U + u + 1], h1_table,
                                       rows_done[r])

            @block.scalar
            def _(act):
                def keep_hot(g):
                    act.wait_ge(hott_ps, g + 1)
                    act.copy(hot_t, bank(0, U * P // 2).bitcast(BF16)).then_inc(hott_done, 1)

                def widen_hot(g, b):
                    act.wait_ge(hots_done, g + 1)
                    act.copy(hot[:, b, :, :].rearrange("p u n -> p (u n)"), hot_b[b]).then_inc(hot_done32, 1)

                def weigh(g, r):
                    act.wait_ge(score_done, g + 1)
                    act.activation(rows[:, r, :, D:D + GH], score, ACT.Exp, scale=-1.0).then_inc(ex_done, 1)

                def step(j, r, last=False):
                    g = j * R + r
                    if not last:
                        weigh(g + 1, (r + 1) % R)
                    keep_hot(g + 2)
                    act.wait_ge(gnn_ps, g * U + (SUMS_BEFORE + (R + 1) * U))
                    widen_hot(g + 2, r % 2)

                for g in range(2):
                    keep_hot(g)
                    widen_hot(g, g)
                weigh(0, 0)
                with act.Fori(0, RINGS_OF_R - 1) as j:
                    for r in range(R):
                        step(j, r)
                for r in range(R):
                    step(RINGS_OF_R - 1, r, last=(r == R - 1))

            @block.vector
            def _(dve):
                V.then(dve.tensor_reduce(r_max, rl3[:, 0:T, 0:GH].rearrange("p t h -> p h t"), AX_X, ALU.max))
                dve.tensor_copy(r_rows.rearrange("p (h n) -> p h n", h=GH),
                                r_max.unsqueeze(2).to_broadcast([P, GH, P])).then_inc(rm_done, 1)
                dve.wait_ge(rm_ps, 1)
                V.then(dve.tensor_reduce(r_max, bank(3, GH * P).rearrange("p (h n) -> p h n", h=GH), AX_X, ALU.max))
                V.then(dve.memset(lc, 0.0))
                V.add(dve.tensor_copy(lc3[:, 0:T, 0:GH], rl3[:, 0:T, GH:]))
                bound = lc3[:, 0:T, GH:]
                V.then(dve.tensor_tensor(bound, rl3[:, 0:T, GH:], r_max.unsqueeze(1).to_broadcast([P, T, GH]), ALU.add))
                V.then(dve.scalar_tensor_tensor(bound, bound, ALPHA, bound, ALU.mult, ALU.max))
                V.then(dve.tensor_scalar(bound, bound, -LIFT - OTHER, None, ALU.add))
                for q in range(PARTS):
                    V.then(dve.tensor_copy(lcp[:, :, q, :], lc3))
                    if q + 1 < PARTS:
                        V.then(dve.tensor_tensor(lc3, lc3, lcp[:, :, q, :], ALU.subtract))
                V.then(dve.tensor_copy(ident_b, ident))
                dve.sem_inc(lc_done, 1)
                visits_dve(dve, 1, vv)
                V.then(dve.memset(acc, 0.0))
                dve.sem_inc(edges_ready, 1)
                dve.sem_inc(gnn_add, GNN1_BANKS)
                dve.wait_ge(tiles_ready, 2)

                def name_rows(g, r):
                    dve.tensor_copy(idx_ring[:, r * U:(r + 1) * U], v_idx[:, ds(g * U, U)]).then_inc(idx_done, 1)

                def one_hot(g, b):
                    wide = [P, U, P]
                    dve.tensor_tensor(hot_b[b].rearrange("p (u n) -> p u n", u=U), iota.unsqueeze(1).to_broadcast(wide),
                                      v_loc[:, ds(g * U, U)].unsqueeze(2).to_broadcast(wide), ALU.is_equal
                                      ).then_inc(hots_done, 1)

                def attend(j, r, stage):
                    g, b = j * R + r, r % 2
                    if stage == 0:
                        dve.wait_ge(rows_done[r], j * (16 * U) + (ROWS_BEFORE[r] + 16 * U))
                        name_rows(g + R, r)
                        dve.wait_ge(look_ps, g + 1)
                        V.add(dve.tensor_reduce(look, bank(2 + b, U * LW).rearrange(
                            "p (u q w) -> p u w q", u=U, q=PARTS), AX_X, ALU.add))
                    elif stage == 1:
                        V.settle()
                        V.add(dve.tensor_tensor(score, look[:, :, 0:GH], rows[:, r, :, D:D + GH], ALU.add))
                    elif stage == 2:
                        V.settle()
                        V.add(dve.scalar_tensor_tensor(score, score, ALPHA, score, ALU.mult, ALU.max))
                    elif stage == 3:
                        V.settle()
                        dve.scalar_tensor_tensor(score, look[:, :, GH:], OTHER, score, ALU.add, ALU.subtract
                                                 ).then_inc(score_done, 1)
                    elif stage == 4:
                        dve.wait_ge(hot_done32, g + 1)
                        one_hot(g + 2, b)
                    else:
                        dve.wait_ge(ex_done, g + 1)
                        q = (stage - 5) * HALF_U
                        msg = rows[:, r, q:q + HALF_U, 0:D].rearrange("p u (h f) -> p u h f", h=GH)
                        ex = rows[:, r, q:q + HALF_U, D:D + GH].unsqueeze(3).to_broadcast([P, HALF_U, GH, GF])
                        dve.tensor_tensor(msg, msg, ex, ALU.mult).then_inc(msg_done, 1)

                STAGES = 7

                def step(j, r, last=False):
                    g = j * R + r
                    tiles = load_tiles(dve, g * U)
                    for u in range(U):
                        add_sums(dve, g * U + u, tiles[u], ACC_W, 4 + u % GNN1_BANKS, SUMS_BEFORE + R * U,
                                 ADDS_BEFORE + GNN1_BANKS)
                        if u >= U - STAGES and not last:
                            attend(j + (r + 1) // R, (r + 1) % R, u - (U - STAGES))

                for r in range(R):
                    name_rows(r, r)
                for g in range(2):
                    one_hot(g, g)
                for stage in range(STAGES):
                    attend(0, 0, stage)
                with V.loop(RINGS_OF_R - 1, R * 3) as j:
                    for r in range(R):
                        step(j, r)
                for r in range(R):
                    step(RINGS_OF_R - 1, r, last=(r == R - 1))
                dve.wait_ge(gnn_add, 2 * NVIS + GNN0_BANKS + GNN1_BANKS)
                with V.loop(LOOPS, 4) as c:
                    got = acc[:, ds(c * (B * ACC_W), B * ACC_W)].rearrange("p (i w) -> p i w", i=B)
                    den = den7.rearrange("p (i h) -> p i h", i=B)
                    V.then(dve.tensor_scalar(den, got[:, :, D:], DEN_MIN, None, ALU.max))
                    V.then(dve.reciprocal(den7, den7))
                    V.then(dve.tensor_tensor(t7.rearrange("p (i h f) -> p i h f", i=B, h=GH),
                                             got[:, :, 0:D].rearrange("p i (h f) -> p i h f", h=GH),
                                             den.unsqueeze(3).to_broadcast([P, B, GH, GF]), ALU.mult))
                    a = xres[:, ds(c * (B * D), B * D)]
                    V.then(dve.tensor_tensor(a, a, t7, ALU.add))

            @block.tensor
            def _(pe):
                pe.wait_ge(rm_done, 1)
                for h in range(GH):
                    last = pe.transpose(bank(3, P, h * P), r_rows[:, h * P:(h + 1) * P], ident)
                last.then_inc(rm_ps, 1)
                pe.wait_ge(lc_done, 1)
                visits_pe(pe, 1, vv)
                pe.sem_inc(gnn_ps, R * U)
                pe.wait_ge(edges_ready, 2)
                pe.wait_ge(tiles_ready, 2)

                def flip_hot(g, b):
                    pe.wait_ge(hots_done, g + 1)
                    for u in range(U):
                        last = pe.transpose(bank(0, P // 2, u * P // 2).bitcast(BF16), hot_b[b][:, u * P:(u + 1) * P],
                                            ident_b)
                    last.then_inc(hott_ps, 1)

                def look_up(g, b):
                    tiles = load_tiles(pe, g * U)
                    pe.wait_ge(hott_done, g + 1)
                    for u in range(U):
                        last = pe.matmul(bank(2 + b, LW, u * LW), hot_t[:, u * P:(u + 1) * P],
                                         lc_parts[:, ds(tiles[u] * LW, LW)], start=True, stop=True)
                    last.then_inc(look_ps, 1)

                flip_hot(0, 0)
                look_up(0, 0)
                flip_hot(1, 1)
                with pe.Fori(0, RINGS_OF_R) as j:
                    for r in range(R):
                        g, b = j * R + r, r % 2
                        look_up(g + 1, 1 - b)
                        pe.wait_ge(hot_done32, g + 1)
                        for u in range(U):
                            if u % HALF_U == 0:
                                pe.wait_ge(msg_done, g * 2 + (u // HALF_U + 1))
                            if u == HALF_U:
                                flip_hot(g + 2, b)
                            pe.wait_ge(gnn_add, g * U + (ADDS_BEFORE + u + 1))
                            pe.matmul(bank(4 + u % GNN1_BANKS, ACC_W), hot[:, b, u, :], rows[:, r, u, 0:ACC_W],
                                      start=True, stop=True).then_inc(gnn_ps, 1)

        W_E = KD * F1
        assert W_E == FB * D
        SLOT_PAIRS = SLOT_TILES // 2
        assert SLOT_PAIRS * 2 == SLOT_TILES
        W1_AT, W2_AT = arena_words - 2 * E1 * W_E, arena_words - E1 * W_E
        scratch(GRAPH, W1_AT)
        pos_i, back_i = take(K1 * T).bitcast(I32), take(K1 * T).bitcast(I32)
        top_w = take(K1 * T)
        mix_w = take(T * E1)
        slot_e = take(SLOT_TILES + K1).bitcast(I32)
        b1_t = take(E1 * FB)
        RINGS = place["at"]
        x_in, x_t = [take(D) for _ in range(2)], [take(D) for _ in range(2)]
        w1_ring = [take(W_E) for _ in range(2)]
        h_t = [take(F1) for _ in range(2)]
        y_ring = [take(D) for _ in range(2)]
        scratch(RINGS, W1_AT)
        xs7 = [take(B * D) for _ in range(2)]
        slot_idx = [take(K1 * B).bitcast(I32) for _ in range(2)]
        scratch(W1_AT)
        w1_all, w2_all = take(E1 * W_E), take(E1 * W_E)
        scratch(W2_AT)
        xn7, xt7 = take(B * D), take(B * D)
        gw, gate_b, b1_raw = take(KD * E1), take(E1), take(P)
        gates, picks, rev = take(T * E1), take(K1 * T * E1), take(E1)
        eq, top_v, first = take(T * E1), take(K1 * T), take(T)
        memory = choice_memory(K1, E1)
        xn7v = xn7.rearrange("p (i k n) -> p i k n", i=B, k=KD)
        xt7v = xt7.rearrange("p (i k n) -> p i k n", i=B, k=KD)
        picks4 = picks.rearrange("p (k t e) -> p k t e", k=K1, e=E1)
        ld_m, ld_m1, ld_m2, b1_ps, tw_in, tw_exp = (sem(n) for n in "ld_m ld_m1 ld_m2 b1_ps tw_in tw_exp".split())
        CALL3 = 3 * LOOPS

        with nc.Block() as block:
            @block.sync
            def _(sp):
                sp.dma_start(gw.rearrange("p (k e) -> p k e", k=KD),
                             L1_ffn_gate_w.rearrange("(k p) e -> p k e", p=P)).then_inc(ld_m, 16)
                sp.dma_start(gate_b, L1_ffn_gate_b.partition_broadcast(P)).then_inc(ld_m, 16)
                sp.dma_start(b1_raw[0:E1 * FB, :], L1_ffn_b1.rearrange("e (f p) -> (e f) p", p=P)).then_inc(ld_m, 16)
                with sp.Fori(0, E1) as e:
                    sp.dma_start(w1_all[:, ds(e * W_E, W_E)].rearrange("p (k f) -> p k f", k=KD),
                                 L1_ffn_w1[ds(e, 1), :, :].rearrange("o (k p) f -> p (o k) f", p=P)).then_inc(ld_m1, 16)
                sp.wait_ge(pos_done, 2)
                with sp.Fori(0, E1) as e:
                    sp.dma_start(w2_all[:, ds(e * W_E, W_E)].rearrange("p (f d) -> p f d", f=FB),
                                 L1_ffn_w2[ds(e, 1), :, :].rearrange("o (f p) d -> p (o f) d", p=P)).then_inc(ld_m2, 16)
                sp.wait_ge(ld_m1, E1 * 16)
                sp.wait_ge(ld_m2, E1 * 16)

            @block.gpsimd
            def _(pool):
                scatter_rows(pool, 1, K1, pos_i, slot_idx, xs7)

            @block.scalar
            def _(act):
                ln_root(act)
                act.wait_ge(b1_ps, 1)
                act.copy(b1_t, bank(7, E1 * FB))
                with act.Fori(0, LOOPS) as c:
                    act.wait_ge(tp_done, c + (CALL3 + 2))
                    act.copy(xt7, psA).then_inc(xt_done, 1)
                act.wait_ge(tw_in, 1)
                act.activation(top_v[:, T:], top_v[:, T:], ACT.Exp).then_inc(tw_exp, 1)

            @block.vector
            def _(dve):
                ln_stats(dve)
                def keep_gates(c):
                    dve.wait_ge(lg_ps, c + (LOOPS + 1))
                    dve.tensor_copy(gates[:, ds(c * (B * E1), B * E1)], bank(4, B * E1)).then_inc(lg_sb, 1)

                norm7(dve, 0, CALL3)
                with dve.Fori(0, LOOPS - 1) as c:
                    norm7(dve, c + 1, CALL3)
                    keep_gates(c)
                keep_gates(LOOPS - 1)
                dve.wait_ge(lg_sb, 2 * LOOPS + 1)
                wide = [P, T, E1]
                g3, eq3 = (a.rearrange("p (t e) -> p t e", e=E1) for a in (gates, eq))
                dve.wait_ge(ld_m, 48)
                V.add(dve.tensor_tensor(g3, g3, gate_b.unsqueeze(1).to_broadcast(wide), ALU.add))
                V.then(dve.tensor_scalar(rev, iota[:, 0:E1], -1.0, float(E1), ALU.mult, ALU.add))
                for k in range(K1):
                    best = top_v[:, k * T:(k + 1) * T]
                    V.then(dve.tensor_reduce(best, g3, AX_X, ALU.max))
                    V.then(dve.tensor_tensor(eq3, g3, best.unsqueeze(2).to_broadcast(wide), ALU.is_ge))
                    V.then(dve.tensor_tensor(eq3, eq3, rev.unsqueeze(1).to_broadcast(wide), ALU.mult))
                    V.then(dve.tensor_reduce(first, eq3, AX_X, ALU.max))
                    V.then(dve.tensor_tensor(picks4[:, k], rev.unsqueeze(1).to_broadcast(wide),
                                             first.unsqueeze(2).to_broadcast(wide), ALU.is_equal))
                    if k == 0:
                        V.then(dve.scalar_tensor_tensor(g3, picks4[:, k], -3.0e38, g3, ALU.mult, ALU.add))
                for k in range(K1):
                    V.add(dve.tensor_scalar(picks4[:, k, T - 1, :], picks4[:, k, T - 1, :], rowmask, None, ALU.mult))
                V.settle()
                dve.sem_inc(picks_done, 1)
                dve.tensor_tensor(top_v[:, T:], top_v[:, T:], top_v[:, 0:T], ALU.subtract).then_inc(tw_in, 1)
                dve.wait_ge(tw_exp, 1)
                V.then(dve.tensor_scalar(first, top_v[:, T:], 1.0, None, ALU.add))
                V.then(dve.reciprocal(top_w[:, 0:T], first))
                V.then(dve.tensor_tensor(top_w[:, T:], top_v[:, T:], top_w[:, 0:T], ALU.mult))
                mix3 = mix_w.rearrange("p (t e) -> p t e", e=E1)
                V.add(dve.tensor_tensor(mix3, picks4[:, 0], top_w[:, 0:T].unsqueeze(2).to_broadcast(wide), ALU.mult))
                V.then(dve.tensor_tensor(eq3, picks4[:, 1], top_w[:, T:].unsqueeze(2).to_broadcast(wide), ALU.mult))
                V.add(dve.tensor_tensor(mix3, mix3, eq3, ALU.add))
                V.settle()
                place_choices(dve, 2, K1, E1, picks, memory, SLOT_TILES, pos_i, back_i, slot_e)
                rows_to_scatter(dve, 1, xs7)

            @block.tensor
            def _(pe):
                pe.wait_ge(ld_m, 48)
                pe.transpose(bank(7, E1 * FB), b1_raw[0:E1 * FB, :], ident[0:E1 * FB, 0:E1 * FB]).then_inc(b1_ps, 1)
                with pe.Fori(0, LOOPS) as c:
                    transpose7(pe, c, CALL3)
                    pe.wait_ge(xt_done, c + (5 * LOOPS + 1))
                    pe.wait_ge(lg_sb, c + (LOOPS + 1))
                    for i in range(B):
                        for k in range(KD):
                            last = pe.matmul(bank(4, E1, i * E1), xt7v[:, i, k, :], gw[:, k * E1:(k + 1) * E1],
                                             start=(k == 0), stop=(k == KD - 1))
                    last.then_inc(lg_ps, 1)
                choice_sums(pe, 2, K1, E1, picks)

        (in_ps, in_done, m1h_ps, h_done, w1_done, m2h_ps, y_done, y_free) = (
            sem(n) for n in "in_ps in_done m1h_ps h_done w1_done m2h_ps y_done y_free".split())
        x_ld = [sem(f"x_ld{b}") for b in range(2)]

        def load_experts(engine, first):
            return nc.values_load_multi_w_load_instructions(
                slot_e[0:1, ds(first, 2)], engines=[engine.engine], min_val=0, max_val=E1 - 1,
                skip_runtime_bounds_check_because="a slot's expert is the least of a count and E1 - 1")[1]

        with nc.Block() as block:
            @block.sync
            def _(sp):
                sp.sem_inc(y_free, 32)
                for b in range(2):
                    sp.dma_start(x_in[b], slot_rows[b * P:(b + 1) * P, :]).then_inc(x_ld[b], 16)
                sp.wait_ge(in_ps, 1)
                sp.dma_start(x_in[0], slot_rows[2 * P:3 * P, :]).then_inc(x_ld[0], 16)
                with sp.Fori(0, SLOT_PAIRS) as j:
                    for b in range(2):
                        s = j * 2 + b
                        sp.wait_ge(in_ps, s + 2)
                        sp.dma_start(x_in[1 - b], slot_rows[ds((s + 3) * P, P), :]).then_inc(x_ld[1 - b], 16)
                        sp.wait_ge(y_done, s + 3)
                        sp.dma_start(slot_out[ds(s * P, P), :], y_ring[b]).then_inc(y_free, 16)
                sp.wait_ge(y_free, SLOT_TILES * 16 + 32)
                sp.wait_ge(x_ld[0], SLOT_PAIRS * 16 + 32)
                sp.wait_ge(x_ld[1], SLOT_PAIRS * 16 + 16)

            @block.scalar
            def _(act):
                with act.Fori(0, SLOT_PAIRS) as j:
                    experts = load_experts(act, j * 2)
                    for b in range(2):
                        s = j * 2 + b
                        for f in range(FB):
                            act.wait_ge(m1h_ps, s * 2 + (f // 2 + 1))
                            act.activation(h_t[b][:, f * P:(f + 1) * P], bank(2 + 2 * b + f // 2, P, f % 2 * P), ACT.Relu,
                                           bias=b1_t[:, ds(experts[b] * FB + f, 1)]).then_inc(h_done, 1)

            @block.vector
            def _(dve):
                def take_in(s, b):
                    dve.wait_ge(in_ps, s + 1)
                    dve.tensor_copy(x_t[b], bank(b, D)).then_inc(in_done, 1)

                def take_w1(expert, b):
                    dve.tensor_copy(w1_ring[b], w1_all[:, ds(expert * W_E, W_E)]).then_inc(w1_done, 1)

                dve.sem_inc(y_done, 2)
                experts = load_experts(dve, 0)
                for b in range(2):
                    take_w1(experts[b], b)
                    take_in(b, b)
                with dve.Fori(0, SLOT_PAIRS) as j:
                    experts = load_experts(dve, j * 2 + 2)
                    for b in range(2):
                        s = j * 2 + b
                        dve.wait_ge(m1h_ps, s * 2 + 2)
                        take_w1(experts[b], b)
                        take_in(s + 2, b)
                        dve.wait_ge(m2h_ps, s + 1)
                        dve.wait_ge(y_free, s * 16 + 16)
                        dve.tensor_copy(y_ring[b], bank(6 + b, D)).then_inc(y_done, 1)

            @block.tensor
            def _(pe):
                def flip(b, nth):
                    pe.wait_ge(x_ld[b], nth * 16 + 16)
                    for k in range(KD):
                        last = pe.transpose(bank(b, P, k * P), x_in[b][:, k * P:(k + 1) * P], ident)
                    last.then_inc(in_ps, 1)

                def hidden(s, b):
                    pe.wait_ge(in_done, s + 1)
                    pe.wait_ge(w1_done, s + 1)
                    for f in range(FB):
                        for k in range(KD):
                            last = pe.matmul(bank(2 + 2 * b + f // 2, P, f % 2 * P),
                                             w1_ring[b][:, k * F1 + f * P:k * F1 + (f + 1) * P],
                                             x_t[b][:, k * P:(k + 1) * P], start=(k == 0), stop=(k == KD - 1))
                        if f % 2:
                            last.then_inc(m1h_ps, 1)

                flip(0, 0)
                flip(1, 0)
                hidden(0, 0)
                with pe.Fori(0, SLOT_PAIRS) as j:
                    experts = load_experts(pe, j * 2)
                    for b in range(2):
                        s = j * 2 + b
                        hidden(s + 1, 1 - b)
                        flip(b, j + 1)
                        pe.wait_ge(y_done, s + 1)
                        for f in range(FB):
                            pe.wait_ge(h_done, s * FB + (f + 1))
                            last = pe.matmul(bank(6 + b, D), h_t[b][:, f * P:(f + 1) * P],
                                             w2_all[:, ds(experts[b] * W_E + f * D, D)], start=(f == 0),
                                             stop=(f == FB - 1))
                        last.then_inc(m2h_ps, 1)

        scratch(RINGS)
        got_k = [[take(D) for _ in range(B)] for _ in range(K1)]
        back_idx = take(K1 * B).bitcast(I32)
        y7, t7 = take(B * D), take(B * D)
        mix7, mix_t = take(B * E1), take(B * P)
        b2_s, gamma_b, beta_b = take(D), take(D), take(D)
        mean7, rstd7 = take(B), take(B)
        (ld_o, back_free, mix_in, mixt_ps, mixt_done, b2_ps, y_sum, out_done, out_st) = (
            sem(n) for n in "ld_o back_free mix_in mixt_ps mixt_done b2_ps y_sum out_done out_st".split())
        NORMS = calls["ln_dve"]

        def scattered1(i):
            return TURNS[i] * 16 * K1 * B if i < 2 else 0

        with nc.Block() as block:
            @block.sync
            def _(sp):
                sp.dma_start(b2_s[0:E1, :], L1_ffn_b2).then_inc(ld_o, 16)
                sp.dma_start(gamma_b, L1_ffn_gamma.partition_broadcast(P)).then_inc(ld_o, 16)
                sp.dma_start(beta_b, L1_ffn_beta.partition_broadcast(P)).then_inc(ld_o, 16)

                def store(c, tiles):
                    sp.dma_start(out[ds(c * (B * P), tiles * P), :].rearrange("(i p) d -> p i d", p=P),
                                 xres[:, ds(c * (B * D), tiles * D)].rearrange("p (i d) -> p i d", d=D)
                                 ).then_inc(out_st, 16)

                with sp.Fori(0, LOOPS - 1) as c:
                    sp.wait_ge(out_done, c + 2)
                    store(c, B)
                sp.wait_ge(out_done, LOOPS + 1)
                store(LOOPS - 1, B - 1)
                sp.dma_start(out[(T - 1) * P:, :], xres[0:TAIL, (T - 1) * D:]).then_inc(out_st, 16)
                sp.wait_ge(out_st, (LOOPS + 1) * 16)

            @block.gpsimd
            def _(pool):
                fetch_rows(pool, SLOT_TILES, K1, back_i, (back_idx, back_idx), (got_k, got_k), back_free, (moved, moved))

            @block.scalar
            def _(act):
                with act.Fori(0, LOOPS) as c:
                    act.copy(mix7, mix_w[:, ds(c * (B * E1), B * E1)]).then_inc(mix_in, 1)
                    act.wait_ge(mixt_ps, c + 1)
                    act.copy(mix_t[0:E1, :], ps[0:E1, 0:B * P]).then_inc(mixt_done, 1)
                    root(act, B, c + (NORMS + 1))

            @block.vector
            def _(dve):
                dve.sem_inc(back_free, 1)
                dve.sem_inc(out_done, 1)
                dve.wait_ge(ld_o, 48)
                with V.loop(LOOPS, 14 + 3 * B) as c:
                    dve.wait_ge(out_done, c + 1)
                    for i in range(B):
                        V.add(normalise(dve, y7[:, i * D:(i + 1) * D], c * B + i))
                    V.settle()
                    dve.wait_ge(b2_ps, c + 1)
                    V.then(dve.tensor_tensor(y7, y7, psB, ALU.add))
                    for i in range(B):
                        y = y7[:, i * D:(i + 1) * D]
                        dve.wait_ge(moved[i], c * (16 * K1) + (moved_before(1, i) + scattered1(i) + 16 * K1))
                        dve.scalar_tensor_tensor(y, got_k[0][i], top_w[:, ds(c * B + i, 1)], y, ALU.mult, ALU.add
                                                 ).then_inc(y_sum, 1)
                    for i in range(B):
                        y = y7[:, i * D:(i + 1) * D]
                        dve.wait_ge(y_sum, c * (2 * B) + B)
                        dve.scalar_tensor_tensor(y, got_k[1][i], top_w[:, ds(c * B + (T + i), 1)], y, ALU.mult, ALU.add
                                                 ).then_inc(y_sum, 1)
                    dve.wait_ge(y_sum, c * (2 * B) + 2 * B)
                    dve.sem_inc(back_free, 1)
                    for i in range(B):
                        V.add(dve.bn_stats(stats[:, i * 6:i * 6 + 6], y7[:, i * D:(i + 1) * D]))
                    V.settle()
                    ln_roots(dve, B, mean7, rstd7, c + (NORMS + 1))
                    for i in range(B):
                        V.add(dve.tensor_scalar(t7[:, i * D:(i + 1) * D], y7[:, i * D:(i + 1) * D], mean7[:, i:i + 1],
                                                rstd7[:, i:i + 1], ALU.subtract, ALU.mult))
                    V.settle()
                    t = t7.rearrange("p (i d) -> p i d", i=B)
                    V.then(dve.tensor_tensor(t, t, gamma_b.unsqueeze(1).to_broadcast([P, B, D]), ALU.mult))
                    V.then(dve.tensor_tensor(t, t, beta_b.unsqueeze(1).to_broadcast([P, B, D]), ALU.add))
                    a = xres[:, ds(c * (B * D), B * D)]
                    dve.tensor_tensor(a, a, t7, ALU.add).then_inc(out_done, 1)

            @block.tensor
            def _(pe):
                pe.wait_ge(ld_o, 48)
                with pe.Fori(0, LOOPS) as c:
                    pe.wait_ge(mix_in, c + 1)
                    for i in range(B):
                        last = pe.transpose(ps[0:E1, i * P:(i + 1) * P], mix7[:, i * E1:(i + 1) * E1], ident)
                    last.then_inc(mixt_ps, 1)
                    pe.wait_ge(mixt_done, c + 1)
                    for i in range(B):
                        last = pe.matmul(half(4, i), mix_t[0:E1, i * P:(i + 1) * P], b2_s[0:E1, :],
                                         start=True, stop=True)
                    last.then_inc(b2_ps, 1)


_INS = ['x', 'src', 'dst', 'edge_weight', 'L0_gnn_W', 'L0_gnn_b', 'L0_mix_Wq', 'L0_mix_Wkv', 'L0_mix_Wproj',
        'L0_mix_bproj', 'L0_ffn_router_w', 'L0_ffn_router_b', 'L0_ffn_W1', 'L0_ffn_b1', 'L0_ffn_W2', 'L0_ffn_b2',
        'L1_gnn_W', 'L1_gnn_a_l', 'L1_gnn_a_r', 'L1_mix_kln_weight', 'L1_mix_kln_bias', 'L1_mix_vln_weight',
        'L1_mix_vln_bias', 'L1_ffn_gate_w', 'L1_ffn_gate_b', 'L1_ffn_w1', 'L1_ffn_b1', 'L1_ffn_w2', 'L1_ffn_b2',
        'L1_ffn_gamma', 'L1_ffn_beta']


def kernel(**inputs):
    import numpy as _np
    import concourse.bacc as _bacc
    from concourse import mybir as _mybir
    from concourse.bass_utils import run_bass_kernel_spmd as _run

    nc = _bacc.Bacc("TRN2", target_bir_lowering=False, num_devices=1)
    arrays, args = {}, []
    for name in _INS:
        a = _np.ascontiguousarray(inputs[name])
        arrays[f"in_{name}"] = a
        args.append(nc.dram_tensor(f"in_{name}", a.shape, _mybir.dt.from_np(a.dtype), kind="ExternalInput").ap())
    out = nc.dram_tensor("out_x", (NODES, D), F32, kind="ExternalOutput").ap()
    gps_two_layers(nc, *args, out)
    r = _run(nc, [arrays], core_ids=[0])
    return r.results[0]["out_x"]
```
